# Optimizing a Trainium2 kernel written in Bass

```python
import numpy as np
import jax
import jax.numpy as jnp

def _softmax(x, axis=-1):
    return jax.nn.softmax(x, axis=axis)

def _gelu(x):
    return jax.nn.gelu(x, approximate=True)

def _silu(x):
    return jax.nn.silu(x)

def _sigmoid(x):
    return jax.nn.sigmoid(x)

def _layernorm(x, axis=-1, eps=1e-05):
    m = jnp.mean(x, axis=axis, keepdims=True)
    v = jnp.var(x, axis=axis, keepdims=True)
    return (x - m) / jnp.sqrt(v + eps)

def _scatter_add(tgt, idx, src, axis=0):
    return tgt.at[idx].add(src)

def _segment_sum(src, seg, n):
    return jax.ops.segment_sum(src, seg, n)
kernel_name = 'mk_decoder_postln_d2_seqx_r4_3348e7'

def setup_inputs(seed: int=0):
    np.random.seed(seed)
    _w = jnp.asarray

    def _rec_inputs():
        import jax
        import jax.numpy as jnp
        _rk = jax.random.key(seed)
        x = -0.0002928 + 1 * jax.random.normal(jax.random.fold_in(_rk, 1), (1, 2048, 256), jnp.float32)
        _lenS = 2048 - jax.random.randint(jax.random.fold_in(_rk, 7), (1,), 0, max(1, 2048 // 4) + 1, jnp.int32)
        _lenS2 = 1601 - jax.random.randint(jax.random.fold_in(_rk, 8), (1,), 0, max(1, 1601 // 4) + 1, jnp.int32)
        _ctx_1024P = jax.random.normal(jax.random.fold_in(_rk, 11), (1, 16, 256), jnp.float32)
        _ctx_1024c = jax.random.dirichlet(jax.random.fold_in(_rk, 511), 0.3 * jnp.ones((16,), jnp.float32), (1, 1601))
        _ctx_1024t = jnp.einsum('bsk,bkd->bsd', _ctx_1024c, _ctx_1024P)
        _ctx_1024t = _ctx_1024t * jax.lax.rsqrt(jnp.mean(jnp.square(_ctx_1024t)) + 1e-12) * 0.953939
        ctx_1024 = -1.39393e-06 + 0.999914 * (_ctx_1024t + 0.3 * jax.random.normal(jax.random.fold_in(_rk, 611), (1, 1601, 256), jnp.float32))
        _validS = jnp.arange(2048)[None, :] < _lenS[:, None]
        _validS2 = jnp.arange(1601)[None, :] < _lenS2[:, None]
        _causal = jnp.tril(jnp.ones((2048, 2048), dtype=bool))
        mask_BxS2_bf1 = jnp.ones((1, 1601), dtype=bool)
        return (x, ctx_1024, mask_BxS2_bf1)
    x, ctx_1024, mask_BxS2_bf1 = _rec_inputs()

    def _L0_attn_setup():
        import math
        import jax, jax.numpy as jnp
        import numpy as np
        D_MODEL = 256
        N_HEADS = 16
        D_K = D_MODEL // N_HEADS
        THETA = 10000.0

        def _rope(t, cos, sin):
            B, H, S, d = t.shape
            tp = t.reshape(B, H, S, d // 2, 2)
            even, odd = (tp[..., 0], tp[..., 1])
            r_even = even * cos - odd * sin
            r_odd = even * sin + odd * cos
            return jnp.stack([r_even, r_odd], axis=-1).reshape(B, H, S, d)
        key = jax.random.key(seed)
        k1, k2, k3 = jax.random.split(key, 3)
        B, S = (2, 512)
        x = jax.random.normal(k1, (B, S, D_MODEL), dtype=jnp.float32)
        std_qkv = math.sqrt(2.0 / (D_MODEL + 3 * D_MODEL))
        std_out = math.sqrt(2.0 / (D_MODEL + D_MODEL))
        w_qkv = jnp.clip(jax.random.normal(k2, (3 * D_MODEL, D_MODEL), dtype=jnp.float32) * std_qkv, -3 * std_qkv, 3 * std_qkv)
        b_qkv = jnp.zeros((3 * D_MODEL,), dtype=jnp.float32)
        w_out = jnp.clip(jax.random.normal(k3, (D_MODEL, D_MODEL), dtype=jnp.float32) * std_out, -3 * std_out, 3 * std_out)
        b_out = jnp.zeros((D_MODEL,), dtype=jnp.float32)
        return {'x': x, 'w_qkv': w_qkv, 'b_qkv': b_qkv, 'w_out': w_out, 'b_out': b_out}
    _L0_attn_all = _L0_attn_setup()
    _L0_attn_in = {k: v for k, v in _L0_attn_all.items() if k in ('w_qkv', 'b_qkv', 'w_out', 'b_out')}
    del _L0_attn_all

    def _L0_xattn_setup():
        import jax, jax.numpy as jnp
        import numpy as np
        B, N, HID, HEADS, TOPK = (2, 512, 256, 16, 64)
        DHEAD = HID // HEADS

        def _split_heads(x):
            b, n, _ = x.shape
            return x.reshape(b, n, HEADS, DHEAD).transpose(0, 2, 1, 3)
        key = jax.random.key(seed)
        ks = jax.random.split(key, 12)
        s = 1.0 / np.sqrt(HID)
        inp = {'q': jax.random.normal(ks[0], (B, N, HID), jnp.float32), 'k': jax.random.normal(ks[1], (B, N, HID), jnp.float32), 'v': jax.random.normal(ks[2], (B, N, HID), jnp.float32), 'mask': jnp.ones((B, N), jnp.bool_), 'topk': TOPK, 'wq_w': jax.random.normal(ks[3], (HID, HID), jnp.float32) * s, 'wq_b': jnp.zeros((HID,), jnp.float32), 'wk_w': jax.random.normal(ks[4], (HID, HID), jnp.float32) * s, 'wk_b': jnp.zeros((HID,), jnp.float32), 'wv_w': jax.random.normal(ks[5], (HID, HID), jnp.float32) * s, 'wv_b': jnp.zeros((HID,), jnp.float32), 'wo_w': jax.random.normal(ks[6], (HID, HID), jnp.float32) * s, 'wo_b': jnp.zeros((HID,), jnp.float32)}
        return inp
    _L0_xattn_all = _L0_xattn_setup()
    _L0_xattn_in = {k: v for k, v in _L0_xattn_all.items() if k in ('wq_w', 'wq_b', 'wk_w', 'wk_b', 'wv_w', 'wv_b', 'wo_w', 'wo_b')}
    del _L0_xattn_all

    def _L0_ffn_setup():
        import jax, jax.numpy as jnp
        import numpy as np
        B, S, D = (1, 512, 256)
        I = 512
        E = 8
        K = 2
        LIMIT = 7.0
        ALPHA = 1.702
        EPS = 1e-05

        def _swiglu(h):
            x_glu = jnp.minimum(h[..., ::2], LIMIT)
            x_lin = jnp.clip(h[..., 1::2], -LIMIT, LIMIT)
            return x_glu * jax.nn.sigmoid(ALPHA * x_glu) * (x_lin + 1.0)

        def _moe(t, gate_w, gate_b, mlp1_w, mlp1_b, mlp2_w, mlp2_b):
            T = t.shape[0]
            logits = t @ gate_w + gate_b
            top_v, top_i = jax.lax.top_k(logits, K)
            probs = jax.nn.softmax(top_v, axis=-1)
            w = jnp.zeros((T, E), t.dtype).at[jnp.arange(T)[:, None], top_i].set(probs)

            def body(acc, ew):
                w1, b1, w2, b2, we = ew
                h = _swiglu(t @ w1 + b1)
                y = h @ w2 + b2
                return (acc + we[:, None] * y, None)
            acc0 = jnp.zeros((T, t.shape[1]), t.dtype)
            acc, _ = jax.lax.scan(body, acc0, (mlp1_w, mlp1_b, mlp2_w, mlp2_b, w.T))
            return acc
        key = jax.random.key(seed)
        ks = jax.random.split(key, 4)
        s = 0.02
        return {'x': jax.random.normal(ks[0], (B, S, D), jnp.float32), 'norm_scale': jnp.ones((D,), jnp.float32), 'gate_w': jax.random.normal(ks[1], (D, E), jnp.float32) * s, 'gate_b': jnp.zeros((E,), jnp.float32), 'mlp1_w': jax.random.normal(ks[2], (E, D, 2 * I), jnp.float32) * s, 'mlp1_b': jnp.zeros((E, 2 * I), jnp.float32), 'mlp2_w': jax.random.normal(ks[3], (E, I, D), jnp.float32) * s, 'mlp2_b': jnp.zeros((E, D), jnp.float32)}
    _L0_ffn_all = _L0_ffn_setup()
    _L0_ffn_in = {k: v for k, v in _L0_ffn_all.items() if k in ('norm_scale', 'gate_w', 'gate_b', 'mlp1_w', 'mlp1_b', 'mlp2_w', 'mlp2_b')}
    del _L0_ffn_all

    def _L1_attn_setup():
        import jax, jax.numpy as jnp
        import numpy as np
        NUM_HEADS = 16
        TOP_K = 64
        key = jax.random.key(seed)
        ks = jax.random.split(key, 9)
        B, S, E = (2, 256, 256)
        x = jax.random.normal(ks[0], (B, S, E), jnp.float32)
        init = lambda k: jax.random.normal(k, (E, E), jnp.float32) * 0.02
        return {'x': x, 'Wq': init(ks[1]), 'bq': jnp.zeros((E,), jnp.float32), 'Wk': init(ks[2]), 'bk': jnp.zeros((E,), jnp.float32), 'Wv': init(ks[3]), 'bv': jnp.zeros((E,), jnp.float32), 'Wo': init(ks[4]), 'bo': jnp.zeros((E,), jnp.float32)}
    _L1_attn_all = _L1_attn_setup()
    _L1_attn_in = {k: v for k, v in _L1_attn_all.items() if k in ('Wq', 'bq', 'Wk', 'bk', 'Wv', 'bv', 'Wo', 'bo')}
    del _L1_attn_all

    def _L1_xattn_setup():
        import jax, jax.numpy as jnp
        import numpy as np
        DIM = 256
        NUM_HEADS = 16
        DIM_HEAD = 64
        INNER = NUM_HEADS * DIM_HEAD
        SCALE = DIM_HEAD ** (-0.5)

        def _layernorm(x, gamma, beta, eps=1e-05):
            mu = jnp.mean(x, axis=-1, keepdims=True)
            var = jnp.mean(jnp.square(x - mu), axis=-1, keepdims=True)
            return (x - mu) * jax.lax.rsqrt(var + eps) * gamma + beta
        key = jax.random.key(seed)
        ks = jax.random.split(key, 8)
        B, SQ, SK = (2, 512, 1024)
        x = jax.random.normal(ks[0], (B, SQ, DIM), dtype=jnp.float32)
        context = jax.random.normal(ks[1], (B, SK, DIM), dtype=jnp.float32)
        ln_gamma = jnp.ones((DIM,), jnp.float32)
        ln_beta = jnp.zeros((DIM,), jnp.float32)
        w_q = jax.random.normal(ks[2], (DIM, INNER), dtype=jnp.float32) / np.sqrt(DIM)
        w_kv = jax.random.normal(ks[3], (DIM, 2 * INNER), dtype=jnp.float32) / np.sqrt(DIM)
        w_out = jax.random.normal(ks[4], (INNER, DIM), dtype=jnp.float32) / np.sqrt(INNER)
        b_out = jnp.zeros((DIM,), jnp.float32)
        gate = jnp.array([0.5], jnp.float32)
        return {'x': x, 'context': context, 'ln_gamma': ln_gamma, 'ln_beta': ln_beta, 'w_q': w_q, 'w_kv': w_kv, 'w_out': w_out, 'b_out': b_out, 'gate': gate}
    _L1_xattn_all = _L1_xattn_setup()
    _L1_xattn_in = {k: v for k, v in _L1_xattn_all.items() if k in ('ln_gamma', 'ln_beta', 'w_q', 'w_kv', 'w_out', 'b_out', 'gate')}
    del _L1_xattn_all

    def _L1_ffn_setup():
        import jax, jax.numpy as jnp
        import numpy as np
        FP8_MAX = 448.0
        FP8 = jnp.float8_e4m3fn
        key = jax.random.key(seed)
        kx, kw, kb = jax.random.split(key, 3)
        B, S, D_in, D_out = (4, 2048, 256, 256)
        x = jax.random.normal(kx, (B, S, D_in), dtype=jnp.float32)
        w = jax.random.normal(kw, (D_out, D_in), dtype=jnp.float32) * 0.02
        weight_scale = jnp.maximum(jnp.max(jnp.abs(w)), 1e-12) / FP8_MAX
        weight = (w / weight_scale).astype(FP8)
        bias = jax.random.normal(kb, (D_out,), dtype=jnp.float32) * 0.01
        return {'x': x, 'weight': weight, 'weight_scale': weight_scale, 'bias': bias}
    _L1_ffn_all = _L1_ffn_setup()
    _L1_ffn_in = {k: v for k, v in _L1_ffn_all.items() if k in ('weight', 'weight_scale', 'bias')}
    del _L1_ffn_all
    return {'x': x, 'ctx_1024': ctx_1024, 'mask_BxS2_bf1': mask_BxS2_bf1, 'L0_attn_w_qkv': _L0_attn_in['w_qkv'], 'L0_attn_b_qkv': _L0_attn_in['b_qkv'], 'L0_attn_w_out': _L0_attn_in['w_out'], 'L0_attn_b_out': _L0_attn_in['b_out'], 'L0_xattn_wq_w': _L0_xattn_in['wq_w'], 'L0_xattn_wq_b': _L0_xattn_in['wq_b'], 'L0_xattn_wk_w': _L0_xattn_in['wk_w'], 'L0_xattn_wk_b': _L0_xattn_in['wk_b'], 'L0_xattn_wv_w': _L0_xattn_in['wv_w'], 'L0_xattn_wv_b': _L0_xattn_in['wv_b'], 'L0_xattn_wo_w': _L0_xattn_in['wo_w'], 'L0_xattn_wo_b': _L0_xattn_in['wo_b'], 'L0_ffn_norm_scale': _L0_ffn_in['norm_scale'], 'L0_ffn_gate_w': _L0_ffn_in['gate_w'], 'L0_ffn_gate_b': _L0_ffn_in['gate_b'], 'L0_ffn_mlp1_w': _L0_ffn_in['mlp1_w'], 'L0_ffn_mlp1_b': _L0_ffn_in['mlp1_b'], 'L0_ffn_mlp2_w': _L0_ffn_in['mlp2_w'], 'L0_ffn_mlp2_b': _L0_ffn_in['mlp2_b'], 'L1_attn_Wq': _L1_attn_in['Wq'], 'L1_attn_bq': _L1_attn_in['bq'], 'L1_attn_Wk': _L1_attn_in['Wk'], 'L1_attn_bk': _L1_attn_in['bk'], 'L1_attn_Wv': _L1_attn_in['Wv'], 'L1_attn_bv': _L1_attn_in['bv'], 'L1_attn_Wo': _L1_attn_in['Wo'], 'L1_attn_bo': _L1_attn_in['bo'], 'L1_xattn_ln_gamma': _L1_xattn_in['ln_gamma'], 'L1_xattn_ln_beta': _L1_xattn_in['ln_beta'], 'L1_xattn_w_q': _L1_xattn_in['w_q'], 'L1_xattn_w_kv': _L1_xattn_in['w_kv'], 'L1_xattn_w_out': _L1_xattn_in['w_out'], 'L1_xattn_b_out': _L1_xattn_in['b_out'], 'L1_xattn_gate': _L1_xattn_in['gate'], 'L1_ffn_weight': _L1_ffn_in['weight'], 'L1_ffn_weight_scale': _L1_ffn_in['weight_scale'], 'L1_ffn_bias': _L1_ffn_in['bias']}

def reference(x, ctx_1024, mask_BxS2_bf1, L0_attn_w_qkv, L0_attn_b_qkv, L0_attn_w_out, L0_attn_b_out, L0_xattn_wq_w, L0_xattn_wq_b, L0_xattn_wk_w, L0_xattn_wk_b, L0_xattn_wv_w, L0_xattn_wv_b, L0_xattn_wo_w, L0_xattn_wo_b, L0_ffn_norm_scale, L0_ffn_gate_w, L0_ffn_gate_b, L0_ffn_mlp1_w, L0_ffn_mlp1_b, L0_ffn_mlp2_w, L0_ffn_mlp2_b, L1_attn_Wq, L1_attn_bq, L1_attn_Wk, L1_attn_bk, L1_attn_Wv, L1_attn_bv, L1_attn_Wo, L1_attn_bo, L1_xattn_ln_gamma, L1_xattn_ln_beta, L1_xattn_w_q, L1_xattn_w_kv, L1_xattn_w_out, L1_xattn_b_out, L1_xattn_gate, L1_ffn_weight, L1_ffn_weight_scale, L1_ffn_bias):
    import jax
    import jax.numpy as jnp

    def _L0_attn_ref(x, w_qkv, b_qkv, w_out, b_out):
        import math
        import jax, jax.numpy as jnp
        import numpy as np
        D_MODEL = 256
        N_HEADS = 16
        D_K = D_MODEL // N_HEADS
        THETA = 10000.0

        def _rope(t, cos, sin):
            B, H, S, d = t.shape
            tp = t.reshape(B, H, S, d // 2, 2)
            even, odd = (tp[..., 0], tp[..., 1])
            r_even = even * cos - odd * sin
            r_odd = even * sin + odd * cos
            return jnp.stack([r_even, r_odd], axis=-1).reshape(B, H, S, d)
        B, S, _ = x.shape
        qkv = jnp.einsum('bsi,oi->bso', x, w_qkv) + b_qkv
        qkv = qkv.reshape(B, S, 3, N_HEADS, D_K).transpose(2, 0, 3, 1, 4)
        q, k, v = (qkv[0], qkv[1], qkv[2])
        inv_freq = THETA ** (-jnp.arange(0, D_K, 2, dtype=jnp.float32) / D_K)
        ang = jnp.arange(S, dtype=jnp.float32)[:, None] * inv_freq[None, :]
        cos, sin = (jnp.cos(ang), jnp.sin(ang))
        q = _rope(q, cos, sin)
        k = _rope(k, cos, sin)
        scale = 1.0 / math.sqrt(D_K)
        scores = jnp.einsum('bhqd,bhkd->bhqk', q.astype(jnp.float32), k.astype(jnp.float32)) * scale
        causal = jnp.tril(jnp.ones((S, S), dtype=bool))
        scores = jnp.where(causal, scores, jnp.finfo(jnp.float32).min)
        ex = jnp.exp(scores - jnp.max(scores, axis=-1, keepdims=True))
        attn = ex / (jnp.sum(ex, axis=-1, keepdims=True) + 1e-08)
        attn = attn.astype(v.dtype)
        o = jnp.einsum('bhqk,bhkd->bhqd', attn, v)
        o = o.transpose(0, 2, 1, 3).reshape(B, S, D_MODEL)
        out = jnp.einsum('bsi,oi->bso', o, w_out) + b_out
        return out

    def _L0_xattn_ref(q, k, v, mask, topk, wq_w, wq_b, wk_w, wk_b, wv_w, wv_b, wo_w, wo_b):
        import jax, jax.numpy as jnp
        import numpy as np
        B, N, HID, HEADS, TOPK = (2, 512, 256, 16, 64)
        DHEAD = HID // HEADS

        def _split_heads(x):
            b, n, _ = x.shape
            return x.reshape(b, n, HEADS, DHEAD).transpose(0, 2, 1, 3)
        qh = _split_heads(q @ wq_w.T + wq_b)
        kh = _split_heads(k @ wk_w.T + wk_b)
        vh = _split_heads(v @ wv_w.T + wv_b)
        scores = jnp.einsum('bhqd,bhkd->bhqk', qh, kh) / np.sqrt(DHEAD)
        neg = jnp.finfo(scores.dtype).min
        scores = jnp.where(mask[:, None, None, :], scores, neg)
        if topk and 0 < topk < scores.shape[-1]:
            vals, idx = jax.lax.top_k(scores, topk)
            b, h, nq, _ = scores.shape
            bI = jnp.arange(b)[:, None, None, None]
            hI = jnp.arange(h)[None, :, None, None]
            qI = jnp.arange(nq)[None, None, :, None]
            scores = jnp.full_like(scores, neg).at[bI, hI, qI, idx].set(vals)
        probs = jax.nn.softmax(scores, axis=-1)
        ctx = jnp.einsum('bhqk,bhkd->bhqd', probs, vh)
        ctx = ctx.transpose(0, 2, 1, 3).reshape(q.shape[0], q.shape[1], HID)
        return ctx @ wo_w.T + wo_b

    def _L0_ffn_ref(x, norm_scale, gate_w, gate_b, mlp1_w, mlp1_b, mlp2_w, mlp2_b):
        import jax, jax.numpy as jnp
        import numpy as np
        B, S, D = (1, 512, 256)
        I = 512
        E = 8
        K = 2
        LIMIT = 7.0
        ALPHA = 1.702
        EPS = 1e-05

        def _swiglu(h):
            x_glu = jnp.minimum(h[..., ::2], LIMIT)
            x_lin = jnp.clip(h[..., 1::2], -LIMIT, LIMIT)
            return x_glu * jax.nn.sigmoid(ALPHA * x_glu) * (x_lin + 1.0)

        def _moe(t, gate_w, gate_b, mlp1_w, mlp1_b, mlp2_w, mlp2_b):
            T = t.shape[0]
            logits = t @ gate_w + gate_b
            top_v, top_i = jax.lax.top_k(logits, K)
            probs = jax.nn.softmax(top_v, axis=-1)
            w = jnp.zeros((T, E), t.dtype).at[jnp.arange(T)[:, None], top_i].set(probs)

            def body(acc, ew):
                w1, b1, w2, b2, we = ew
                h = _swiglu(t @ w1 + b1)
                y = h @ w2 + b2
                return (acc + we[:, None] * y, None)
            acc0 = jnp.zeros((T, t.shape[1]), t.dtype)
            acc, _ = jax.lax.scan(body, acc0, (mlp1_w, mlp1_b, mlp2_w, mlp2_b, w.T))
            return acc
        Bx, Sx, Dx = x.shape
        ms = jnp.mean(x * x, axis=-1, keepdims=True)
        t = (x * jax.lax.rsqrt(ms + EPS) * norm_scale).reshape(Bx * Sx, Dx)
        y = _moe(t, gate_w, gate_b, mlp1_w, mlp1_b, mlp2_w, mlp2_b)
        return x + y.reshape(Bx, Sx, Dx)

    def _L1_attn_ref(x, Wq, bq, Wk, bk, Wv, bv, Wo, bo):
        import jax, jax.numpy as jnp
        import numpy as np
        NUM_HEADS = 16
        TOP_K = 64
        B, S, E = x.shape
        H = NUM_HEADS
        hd = E // H
        scale = jnp.sqrt(jnp.float32(hd))

        def proj(W, b):
            return (x @ W.T + b).reshape(B, S, H, hd).transpose(0, 2, 1, 3)
        q = proj(Wq, bq)
        k = proj(Wk, bk)
        v = proj(Wv, bv)
        scores = jnp.einsum('bhqd,bhkd->bhqk', q, k) / scale
        top_scores, top_idx = jax.lax.top_k(scores, TOP_K)
        vg = jnp.take_along_axis(v[:, :, None, :, :], top_idx[..., None], axis=3)
        w = jax.nn.softmax(top_scores, axis=-1)
        out = jnp.einsum('bhqk,bhqkd->bhqd', w, vg)
        out = out.transpose(0, 2, 1, 3).reshape(B, S, E)
        return out @ Wo.T + bo

    def _L1_xattn_ref(x, context, ln_gamma, ln_beta, w_q, w_kv, w_out, b_out, gate):
        import jax, jax.numpy as jnp
        import numpy as np
        DIM = 256
        NUM_HEADS = 16
        DIM_HEAD = 64
        INNER = NUM_HEADS * DIM_HEAD
        SCALE = DIM_HEAD ** (-0.5)

        def _layernorm(x, gamma, beta, eps=1e-05):
            mu = jnp.mean(x, axis=-1, keepdims=True)
            var = jnp.mean(jnp.square(x - mu), axis=-1, keepdims=True)
            return (x - mu) * jax.lax.rsqrt(var + eps) * gamma + beta
        B, SQ, _ = x.shape
        SK = context.shape[1]
        xn = _layernorm(x, ln_gamma, ln_beta)
        q = (xn @ w_q).reshape(B, SQ, NUM_HEADS, DIM_HEAD)
        kv = context @ w_kv
        k, v = jnp.split(kv, 2, axis=-1)
        k = k.reshape(B, SK, NUM_HEADS, DIM_HEAD)
        v = v.reshape(B, SK, NUM_HEADS, DIM_HEAD)
        scores = jnp.einsum('bqhd,bkhd->bhqk', q * SCALE, k)
        attn = jax.nn.softmax(scores, axis=-1)
        out = jnp.einsum('bhqk,bkhd->bqhd', attn, v).reshape(B, SQ, INNER)
        out = out @ w_out + b_out
        return out * jnp.tanh(gate[0])

    def _L1_ffn_ref(x, weight, weight_scale, bias):
        import jax, jax.numpy as jnp
        import numpy as np
        FP8_MAX = 448.0
        FP8 = jnp.float8_e4m3fn
        amax = jnp.max(jnp.abs(x), axis=-1, keepdims=True)
        x_scale = jnp.maximum(amax, 1e-12) / FP8_MAX
        qinput = (x / x_scale).astype(FP8)
        A = qinput.astype(x.dtype) * x_scale
        Bm = weight.astype(x.dtype) * weight_scale
        out = jnp.einsum('bsk,nk->bsn', A, Bm) + bias
        return out.astype(x.dtype)
    x = _layernorm(x + _L0_attn_ref(x, L0_attn_w_qkv, L0_attn_b_qkv, L0_attn_w_out, L0_attn_b_out), axis=-1)
    x = _layernorm(x + _L0_xattn_ref(x, ctx_1024, ctx_1024, mask_BxS2_bf1, 64, L0_xattn_wq_w, L0_xattn_wq_b, L0_xattn_wk_w, L0_xattn_wk_b, L0_xattn_wv_w, L0_xattn_wv_b, L0_xattn_wo_w, L0_xattn_wo_b), axis=-1)
    x = _layernorm(x + _L0_ffn_ref(x, L0_ffn_norm_scale, L0_ffn_gate_w, L0_ffn_gate_b, L0_ffn_mlp1_w, L0_ffn_mlp1_b, L0_ffn_mlp2_w, L0_ffn_mlp2_b), axis=-1)
    x = _layernorm(x + _L1_attn_ref(x, L1_attn_Wq, L1_attn_bq, L1_attn_Wk, L1_attn_bk, L1_attn_Wv, L1_attn_bv, L1_attn_Wo, L1_attn_bo), axis=-1)
    x = _layernorm(x + _L1_xattn_ref(x, ctx_1024, L1_xattn_ln_gamma, L1_xattn_ln_beta, L1_xattn_w_q, L1_xattn_w_kv, L1_xattn_w_out, L1_xattn_b_out, L1_xattn_gate), axis=-1)
    x = _layernorm(x + _L1_ffn_ref(x, L1_ffn_weight, L1_ffn_weight_scale, L1_ffn_bias), axis=-1)
    return x

_drawn_inputs = setup_inputs


def setup_inputs(seed=0):
    import zlib

    import numpy as np

    out = dict(_drawn_inputs(seed))
    spreads = {'L0_attn_b_qkv': (0.0, 0.1),
     'L0_attn_b_out': (0.0, 0.1),
     'L0_xattn_wq_b': (0.0, 0.1),
     'L0_xattn_wk_b': (0.0, 2.0),
     'L0_xattn_wv_b': (0.0, 0.1),
     'L0_xattn_wo_b': (0.0, 0.1),
     'L0_ffn_norm_scale': (1.0, 0.6),
     'L0_ffn_gate_b': (0.0, 0.277),
     'L0_ffn_mlp1_b': (0.0, 0.661),
     'L0_ffn_mlp2_b': (0.0, 0.1),
     'L1_attn_bq': (0.0, 2.0),
     'L1_attn_bk': (0.0, 2.0),
     'L1_attn_bv': (0.0, 0.1),
     'L1_attn_bo': (0.0, 0.1),
     'L1_xattn_ln_gamma': (1.0, 0.6),
     'L1_xattn_ln_beta': (0.0, 0.718),
     'L1_xattn_b_out': (0.0, 0.1)}
    factors = {'L1_attn_Wq': 8.781, 'L1_attn_Wk': 2.85, 'L1_ffn_bias': 5.875}
    for name, (base, spread) in spreads.items():
        noise = np.random.default_rng([zlib.crc32(name.encode()), seed]).standard_normal(out[name].shape)
        drawn = base * np.exp(spread * noise) if base else spread * noise
        out[name] = jnp.asarray(drawn.astype(out[name].dtype))
    for name, factor in factors.items():
        out[name] = (out[name] * factor).astype(out[name].dtype)
    return out
```

```python
from contextlib import ExitStack

import concourse.bass as bass
from concourse import mybir

ALU = mybir.AluOpType
ACT = mybir.ActivationFunctionType
AX = mybir.AxisListType
F32 = mybir.dt.float32
BF16 = mybir.dt.bfloat16
I32 = mybir.dt.int32
U32 = mybir.dt.uint32
U8 = mybir.dt.uint8
RMAX = bass.bass_isa.ReduceOp.max

P = 128
D = 256
KC = D // P
S = 2048
NCTX = 1601
QT = S // P
CH = 512
QC = S // CH
H = 16
DH = D // H
TOPK = 64
NEG = -1.0e38
SPLITS = ((0, 0), (0, 1), (0, 2), (1, 0), (1, 1), (2, 0))
STACK = DH * len(SPLITS)
MASK_ROW = STACK
SHIFT_ROW = STACK + 1
ROWS = STACK + 4
SLOTS = 4
EPS = 1e-5


def tiles_of(n, size=P):
    return [(a, min(size, n - a)) for a in range(0, n, size)]


class Scope:

    def __init__(self, nc, stack, tag):
        self.nc, self.stack, self.tag, self.sems = nc, stack, tag, []
        stack.callback(self.clear)

    def sb(self, name, shape, dt=F32):
        return self.stack.enter_context(self.nc.sbuf_tensor(f"{self.tag}_{name}", shape, dt))

    def ps(self, name, shape):
        return self.stack.enter_context(self.nc.psum_tensor(f"{self.tag}_{name}", shape, F32))

    def sem(self, name):
        self.sems.append(self.nc.alloc_semaphore(f"{self.tag}_{name}"))
        return self.sems[-1]

    def clear(self):
        if self.sems:
            self.nc.clear_and_free_semaphores(self.sems)
            self.nc.all_engine_barrier()


def load_inputs(nc, G, A):
    with ExitStack() as stack:
        s = Scope(nc, stack, "load")
        ctx_tok = s.sb("ctx_tok", [P, len(tiles_of(NCTX)), D])
        bandf = s.sb("bandf", [P, 2, G.band.shape[2]])
        turned = [s.ps(f"turned{b}", [P, CH]) for b in range(2)]
        loaded, turns, evacs, ready = s.sem("loaded"), s.sem("turns"), s.sem("evacs"), s.sem("ready")
        ct = tiles_of(NCTX)
        jobs = []
        for c in range(KC):
            for g in range(0, QT, 4):
                jobs.append(([(G.x_tok[:, t, c * P:(c + 1) * P], P) for t in range(g, g + 4)],
                             G.xT, c, g * P))
            for g in range(0, len(ct), 4):
                jobs.append(([(ctx_tok[0:n, t, c * P:(c + 1) * P], n)
                              for t, (_, n) in list(enumerate(ct))[g:g + 4]], G.ctxT, c, g * P))
        block = stack.enter_context(nc.Block())
        full = NCTX // P

        @block.sync
        def _(sp):
            sp.dma_start(G.ident[:], A["const_ident"]).then_inc(loaded, 16)
            sp.dma_start(G.x_tok[:], A["x"][0].rearrange("(t p) d -> p t d", p=P)).then_inc(loaded, 16)
            sp.dma_start(ctx_tok[:, 0:full, :],
                         A["ctx_1024"][0, 0:full * P].rearrange("(t p) d -> p t d", p=P)).then_inc(loaded, 16)
            sp.dma_start(ctx_tok[0:NCTX - full * P, full, :], A["ctx_1024"][0, full * P:NCTX]).then_inc(loaded, 16)
            sp.dma_start(bandf[:], A["const_band"]).then_inc(loaded, 16)

        @block.gpsimd
        def _(pool):
            nc.gpsimd.memset(G.ones[:], 1.0).then_inc(ready, 1)
            nc.gpsimd.memset(G.zerob[:], 0.0).then_inc(ready, 1)

        @block.tensor
        def _(pe):
            pe.wait_ge(loaded, 5 * 16)
            for j, (srcs, _, _, _) in enumerate(jobs):
                if j >= 2:
                    pe.wait_ge(evacs, j - 1)
                at = 0
                for src, n in srcs:
                    mm = nc.tensor.transpose(turned[j % 2][:, at:at + n], src, G.ident[0:n, 0:n])
                    at += n
                mm.then_inc(turns, 1)

        @block.scalar
        def _(act):
            for j, (srcs, dst, c, at) in enumerate(jobs):
                act.wait_ge(turns, j + 1)
                n = sum(k for _, k in srcs)
                nc.scalar.activation(dst[:, c, at:at + n], turned[j % 2][:, 0:n], ACT.Copy).then_inc(evacs, 1)

        @block.vector
        def _(dve):
            dve.wait_ge(loaded, 5 * 16)
            nc.vector.tensor_copy(G.identb[:], G.ident[:]).then_inc(ready, 1)
            nc.vector.tensor_copy(G.band[:], bandf[:]).then_inc(ready, 1)


def project(nc, G, A, tag, srcT, nk, wq, wk, wv, bq, bk, bv, rope, mask, V):
    kt = tiles_of(nk)
    NQK = 2 * KC
    with ExitStack() as stack:
        s = Scope(nc, stack, tag)
        w_rows = s.sb("w_rows", [P, 3, KC, D])
        wT = s.sb("wT", [P, 3, KC, D])
        bias = s.sb("bias", [1, 3, D])
        if rope:
            wR = s.sb("wR", [P, 2, KC, D])
            biasR = s.sb("biasR", [1, 2, D])
            cos, sin = s.sb("cos", [P, S]), s.sb("sin", [P, S])
            part = s.sb("part", [P, 2, CH])
        full = s.sb("full", [P, 2, S])
        rest = s.sb("rest", [P, S])
        parts = s.sb("parts", [P, 2, 3, S], BF16)
        maskf = s.sb("maskf", [1, S])
        maskb = s.sb("maskb", [1, S], U8)
        banks = [s.ps(f"bank{b}", [P, CH]) for b in range(4)]
        vbanks = [s.ps(f"vbank{b}", [P, CH]) for b in range(2)]
        loaded, turned, w_ready = s.sem("loaded"), s.sem("turned"), s.sem("w_ready")
        formed, taken, whole, v_formed, v_taken, split, rest_done, stored, masked, v_clear = (
            s.sem(x) for x in ("formed", "taken", "whole", "v_formed", "v_taken", "split", "rest_done",
                               "stored0", "masked", "v_clear"))
        stored = [stored, s.sem("stored1")]
        roped, r_chain = s.sem("roped"), s.sem("r_chain")
        n_loads = 6 + (16 if rope else 0) + (1 if mask is not None else 0)
        units = [(w, oc) for w in range(2) for oc in range(KC)]
        chunks = [tiles_of(S, CH) if w == 0 else tiles_of(nk, CH) for w, _ in units]
        src = [G.xT, srcT]
        W_STEPS = 4 if rope else 1
        n_w = 3 + (2 * 2 if rope else 0) + (4 if rope else 0)
        per = 2 if rope else 1
        order = [(u, c) for u in range(len(units)) for c in range(len(chunks[u]))]
        ends = [sum(len(x) for x in chunks[:u + 1]) for u in range(len(units))]
        block = stack.enter_context(nc.Block())

        @block.sync
        def _(sp):
            for i, (w, b) in enumerate(((wq, bq), (wk, bk), (wv, bv))):
                sp.dma_start(w_rows[:, i], w.rearrange("(c p) d -> p c d", p=P)).then_inc(loaded, 16)
                sp.dma_start(bias[:, i], b).then_inc(loaded, 16)
            if rope:
                for g in range(P // DH):
                    sp.dma_start(cos[g * DH:(g + 1) * DH], A["const_rope"][0]).then_inc(loaded, 16)
                    sp.dma_start(sin[g * DH:(g + 1) * DH], A["const_rope"][1]).then_inc(loaded, 16)
            if mask is not None:
                sp.dma_start(maskb[:, 0:nk], mask.bitcast(U8)).then_inc(loaded, 16)
            for u, (w, oc) in enumerate(units):
                n = S if w == 0 else nk
                sp.wait_ge(split, 3 * (u + 1))
                dst = G.q_parts if w == 0 else G.k_parts
                for j in range(3):
                    sp.dma_start(dst[j, oc * P:(oc + 1) * P, 0:n], parts[:, u % 2, j, 0:n]).then_inc(stored[u % 2], 16)
            for u in range(2):
                sp.wait_ge(stored[u], 3 * 16 * len(units) // 2)

        @block.gpsimd
        def _(pool):
            last = len(kt) - 1
            nc.gpsimd.memset(V[:, last], 0.0).then_inc(v_clear, 1)
            pool.wait_ge(v_clear, 1)
            nc.gpsimd.memset(V[:, 0:last, :, DH:2 * DH], 1.0).then_inc(v_clear, 1)
            pool.wait_ge(v_clear, 2)
            nc.gpsimd.memset(V[0:kt[-1][1], last, :, DH:2 * DH], 1.0).then_inc(v_clear, 1)
            pool.wait_ge(v_clear, 3)
            nc.gpsimd.memset(maskf[:], NEG if mask is not None else 0.0).then_inc(v_clear, 1)

        @block.tensor
        def _(pe):
            pe.wait_ge(loaded, n_loads * 16)
            for i in range(3):
                if i == 2:
                    pe.wait_ge(w_ready, W_STEPS)
                for ic in range(KC):
                    for oc in range(KC):
                        mm = nc.tensor.transpose(banks[i % 2][:, ic * D + oc * P:ic * D + (oc + 1) * P],
                                                 w_rows[:, i, oc, ic * P:(ic + 1) * P], G.ident[:])
                mm.then_inc(turned, 1)
            pe.wait_ge(w_ready, n_w)
            for n, (u, c) in enumerate(order):
                w, oc = units[u]
                a, m = chunks[u][c]
                if n >= 4 // per:
                    pe.wait_ge(taken, n - 4 // per + 1)
                for r in range(per):
                    bank = banks[(n * per + r) % 4]
                    wt, bt = (wT, bias) if r == 0 else (wR, biasR)
                    for ic in range(KC):
                        nc.tensor.matmul(bank[:, 0:m], wt[:, w, ic, oc * P:(oc + 1) * P],
                                         src[w][:, ic, a:a + m], start=(ic == 0), stop=False)
                    mm = nc.tensor.matmul(bank[:, 0:m], bt[:, w, oc * P:(oc + 1) * P], G.ones[0:1, 0:m],
                                          start=False, stop=True)
                mm.then_inc(formed, 1)
            for t, (a, m) in enumerate(kt):
                if t >= 2:
                    pe.wait_ge(v_taken, t - 1)
                for ic in range(KC):
                    nc.tensor.matmul(vbanks[t % 2][0:m, 0:D], srcT[:, ic, a:a + m], wT[:, 2, ic, :],
                                     start=(ic == 0), stop=False)
                nc.tensor.matmul(vbanks[t % 2][0:m, 0:D], G.ones[0:1, 0:m], bias[:, 2, :],
                                 start=False, stop=True).then_inc(v_formed, 1)

        @block.scalar
        def _(act):
            for i in range(3):
                act.wait_ge(turned, i + 1)
                bank = banks[i % 2][:].rearrange("p (c d) -> p c d", c=KC)
                nc.scalar.activation(wT[:, i], bank, ACT.Copy).then_inc(w_ready, 1)
                if rope and i < 2:
                    pair = bank.rearrange("p c (f two) -> p c f two", two=2)
                    out = wR[:, i].rearrange("p c (f two) -> p c f two", two=2)
                    nc.scalar.activation(out[:, :, :, 0], pair[:, :, :, 1], ACT.Copy, scale=-1.0).then_inc(w_ready, 1)
                    nc.scalar.activation(out[:, :, :, 1], pair[:, :, :, 0], ACT.Copy).then_inc(w_ready, 1)
                    if i == 0:
                        act.wait_ge(loaded, n_loads * 16)
                    bp = bias[:, i].rearrange("p (f two) -> p f two", two=2)
                    bo = biasR[:, i].rearrange("p (f two) -> p f two", two=2)
                    nc.scalar.activation(bo[:, :, 0], bp[:, :, 1], ACT.Copy, scale=-1.0).then_inc(w_ready, 1)
                    nc.scalar.activation(bo[:, :, 1], bp[:, :, 0], ACT.Copy).then_inc(w_ready, 1)
            for u, (w, oc) in enumerate(units):
                n = S if w == 0 else nk
                if not rope:
                    if u >= 2:
                        act.wait_ge(rest_done, 2 * (u - 1))
                    for c, (a, m) in enumerate(chunks[u]):
                        at = (ends[u - 1] if u else 0) + c
                        act.wait_ge(formed, at + 1)
                        nc.scalar.activation(full[:, u % 2, a:a + m], banks[at % 4][:, 0:m], ACT.Copy,
                                             scale=0.25 if w == 0 else 1.0).then_inc(taken, 1)
                    act.wait_ge(taken, ends[u])
                else:
                    act.wait_ge(roped, ends[u])
                if u >= 2:
                    act.wait_ge(stored[u % 2], 3 * 16 * (u // 2))
                nc.scalar.activation(parts[:, u % 2, 0, 0:n], full[:, u % 2, 0:n], ACT.Copy).then_inc(split, 1)
                act.wait_ge(rest_done, 2 * u + 1)
                nc.scalar.activation(parts[:, u % 2, 1, 0:n], rest[:, 0:n], ACT.Copy).then_inc(split, 1)
                act.wait_ge(rest_done, 2 * u + 2)
                nc.scalar.activation(parts[:, u % 2, 2, 0:n], rest[:, 0:n], ACT.Copy).then_inc(split, 1)
            act.wait_ge(v_clear, 4)
            for t, (a, m) in enumerate(kt):
                act.wait_ge(v_formed, t + 1)
                nc.scalar.activation(V[0:m, t, :, 0:DH],
                                     vbanks[t % 2][0:m, 0:D].rearrange("p (h d) -> p h d", h=H),
                                     ACT.Copy).then_inc(v_taken, 1)

        @block.vector
        def _(dve):
            if rope:
                dve.wait_ge(loaded, n_loads * 16)
            for u, (w, oc) in enumerate(units):
                n = S if w == 0 else nk
                if rope:
                    scale = 0.25 if w == 0 else 1.0
                    for c, (a, m) in enumerate(chunks[u]):
                        at = (ends[u - 1] if u else 0) + c
                        dve.wait_ge(formed, at + 1)
                        if at:
                            dve.wait_ge(roped, at)
                        nc.vector.scalar_tensor_tensor(out=part[:, 0, 0:m], in0=banks[(2 * at) % 4][:, 0:m],
                                                       scalar=scale, in1=cos[:, a:a + m], op0=ALU.mult,
                                                       op1=ALU.mult).then_inc(r_chain, 1)
                        nc.vector.scalar_tensor_tensor(out=part[:, 1, 0:m], in0=banks[(2 * at + 1) % 4][:, 0:m],
                                                       scalar=scale, in1=sin[:, a:a + m], op0=ALU.mult,
                                                       op1=ALU.mult).then_inc(taken, 1)
                        dve.wait_ge(r_chain, at + 1)
                        dve.wait_ge(taken, at + 1)
                        nc.vector.tensor_tensor(full[:, u % 2, a:a + m], part[:, 0, 0:m], part[:, 1, 0:m],
                                                ALU.add).then_inc(roped, 1)
                dve.wait_ge(split, 3 * u + 1)
                if rope:
                    dve.wait_ge(roped, ends[u])
                nc.vector.tensor_tensor(rest[:, 0:n], full[:, u % 2, 0:n], parts[:, u % 2, 0, 0:n],
                                        ALU.subtract).then_inc(rest_done, 1)
                dve.wait_ge(split, 3 * u + 2)
                nc.vector.tensor_tensor(rest[:, 0:n], rest[:, 0:n], parts[:, u % 2, 1, 0:n],
                                        ALU.subtract).then_inc(rest_done, 1)
            dve.wait_ge(v_clear, 4)
            if mask is not None:
                dve.wait_ge(loaded, n_loads * 16)
                nc.vector.tensor_scalar(maskf[:, 0:nk], maskb[:, 0:nk], 1.0, -NEG, ALU.subtract,
                                        ALU.mult).then_inc(masked, 1)
                dve.wait_ge(masked, 1)
            nc.vector.tensor_copy(G.mask_row[:], maskf[:]).then_inc(masked, 1)


def load_head(nc, G, eng, h, nk, Kb, Qm, Qt, sem):
    slot = h & (SLOTS - 1)
    count = 0
    for j, (qp, kp) in enumerate(SPLITS):
        rows = slice(j * DH, (j + 1) * DH)
        eng.dma_start(Kb[rows, bass.ds(slot * S, nk)], G.k_parts[kp, bass.ds(h * DH, DH), 0:nk]).then_inc(sem, 16)
        count += 1
        for Q in (Qm, Qt):
            if Q is not None:
                eng.dma_start(Q[rows, bass.ds(slot * S, S)], G.q_parts[qp, bass.ds(h * DH, DH), :]).then_inc(sem, 16)
                count += 1
    return count


def attend_top(nc, G, tag, nk, V):
    kt = tiles_of(nk)
    NKT = len(kt)
    key_chunks = tiles_of(nk, CH)
    NSEG = 64
    seg_w = nk // NSEG
    segs = [(j * seg_w, seg_w if j < NSEG - 1 else nk - j * seg_w) for j in range(NSEG)]
    DEEP = 3
    ROUNDS = TOPK // 8 + 1
    G4 = QT // 4
    with ExitStack() as stack:
        s = Scope(nc, stack, tag)
        Kb = s.sb("k_stack", [ROWS, SLOTS * S], BF16)
        Qm = s.sb("q_stack_max", [ROWS, SLOTS * S], BF16)
        Qt = s.sb("q_stack_cut", [ROWS, SLOTS * S], BF16)
        score = s.sb("score", [P, 4, nk])
        cand = s.sb("cand", [P, NSEG + 3, 8])
        deep = s.sb("deep", [P, 9])
        eighth = s.sb("eighth", [P, 1])
        top = s.sb("top", [P, 8 * ROUNDS])
        flag, anyflag = s.sb("flag", [P, 4]), s.sb("anyflag", [P, 4])
        stat = s.sb("stat", [P, 2 * QT])
        statT = s.sb("statT", [2 * QT, P])
        stat_rest = s.sb("stat_rest", [2 * QT, P])
        stat_parts = s.sb("stat_parts", [2 * QT, 3, P], BF16)
        expd = s.sb("expd", [P, QC, CH])
        prob = s.sb("prob", [P, 2, QC, CH])
        Vh = s.sb("v_head", [P, 2, 2 * DH])
        O_out = s.sb("o_out", [P, CH])
        sA = [s.ps(f"by_query{b}", [P, CH]) for b in range(2)]
        yP = [s.ps(f"less_max{b}", [P, CH]) for b in range(2)]
        xP = [s.ps(f"less_cut{b}", [P, CH]) for b in range(2)]
        O = s.ps("o_sum", [P, CH])
        turned = s.ps("turned", [P, CH])
        (ready, loaded, a_formed, a_taken, s_free, y_formed, y_taken, x_formed, x_taken, staged, pv_done,
         o_formed, o_taken, o_stored, chain, flagged, reduced, stats_set, st_turned, st_split, st_loaded,
         passed) = (s.sem(x) for x in (
             "ready", "loaded", "a_formed", "a_taken", "s_free", "y_formed", "y_taken", "x_formed",
             "x_taken", "staged", "pv_done", "o_formed", "o_taken", "o_stored", "chain", "flagged",
             "reduced", "stats_set", "st_turned", "st_split", "st_loaded", "passed"))
        A_AHEAD, S_AHEAD, Y_AHEAD, X_AHEAD, PV_AHEAD, O_AHEAD = 2, 4, 2, 4, 2, 1
        READY = 6
        block = stack.enter_context(nc.Block())

        def hold(eng, *events):
            for sem, n in events:
                eng.wait_ge(sem, n)
            if eng in (nc.vector, nc.gpsimd, nc.sync):
                eng.sem_inc(passed, 1)

        def heads(eng, step, a_end=None, b_start=None, b_end=None, peel=False):
            def group(ha, hb, g):
                for u in range(4):
                    past = hb is not None and isinstance(g, int) and 4 * g + u >= NKT
                    if not past:
                        step(ha, hb, g, u)
                    elif ha is not None:
                        step(ha, None, g, u)

            full = NKT // 4

            def head(ha, hb):
                if b_start:
                    b_start(hb)
                if peel:
                    group(ha, hb, 0)
                with eng.Fori(1 if peel else 0, full) as g:
                    group(ha, hb, g)
                if full < G4:
                    group(ha, hb, full)
                if b_end:
                    b_end(hb)

            with eng.Fori(0, G4) as g:
                group(0, None, g)
            if a_end:
                a_end(0)
            with eng.Fori(0, H - 1) as h:
                head(h + 1, h)
                if a_end:
                    a_end(h + 1)
            head(None, H - 1)

        @block.sync
        def _(sp):
            per_head = 3 * len(SPLITS) * 16

            def load(h):
                load_head(nc, G, sp, h, nk, Kb, Qm, Qt, loaded)
                hold(sp, (loaded, per_head * (h + 1) + SLOTS * 16))

            def stats(h):
                hold(sp, (st_split, h + 1))
                slot = h & (SLOTS - 1)
                for j in range(3):
                    row = slice(SHIFT_ROW + j, SHIFT_ROW + j + 1)
                    sp.dma_start(Qm[row, bass.ds(slot * S, S)], stat_parts[0:QT, j]).then_inc(st_loaded, 16)
                    sp.dma_start(Qt[row, bass.ds(slot * S, S)], stat_parts[QT:2 * QT, j]).then_inc(st_loaded, 16)
                hold(sp, (st_loaded, 96 * (h + 1) + 16))

            sp.sem_inc(st_loaded, 16)
            sp.wait_ge(ready, READY)
            for slot in range(SLOTS):
                sp.dma_start(Kb[MASK_ROW:MASK_ROW + 1, slot * S:(slot + 1) * S], G.mask_row[:]).then_inc(loaded, 16)
            for h in range(4):
                load(h)
                if h >= 2:
                    stats(h - 2)
            with sp.Fori(2, H - 2) as h:
                hold(sp, (o_formed, h - 1))
                load(h + 2)
                stats(h)
            stats(H - 2)
            stats(H - 1)

        @block.gpsimd
        def _(pool):
            nc.gpsimd.memset(Kb[:], 0.0).then_inc(ready, 1)
            pool.wait_ge(ready, 1)
            nc.gpsimd.memset(Kb[MASK_ROW:ROWS, :], 1.0).then_inc(ready, 1)
            pool.wait_ge(ready, 2)
            nc.gpsimd.memset(Qm[MASK_ROW:ROWS, :], 1.0).then_inc(ready, 1)
            pool.wait_ge(ready, 3)
            nc.gpsimd.memset(Qt[MASK_ROW:ROWS, :], 1.0).then_inc(ready, 1)
            pool.wait_ge(ready, 4)
            nc.gpsimd.memset(deep[:, 8:9], -3.0e38).then_inc(ready, 1)
            pool.wait_ge(ready, 5)
            nc.gpsimd.memset(O_out[:], 0.0).then_inc(ready, 1)
            pool.wait_ge(ready, READY)

            def step(ha, hb, g, u):
                if hb is not None:
                    m = hb * NKT + 4 * g + u
                    hold(pool, (pv_done, m + PV_AHEAD - 1))
                    nc.gpsimd.tensor_copy(Vh[:, u % 2], V[:, bass.ds(4 * g + u, 1), bass.ds(hb, 1), :]).then_inc(staged, 1)
                if ha is not None:
                    n = ha * QT + 4 * g + u
                    hold(pool, (flagged, n + 1))
                    nc.gpsimd.partition_all_reduce(anyflag[:, u:u + 1], flag[:, u:u + 1], P, RMAX).then_inc(reduced, 1)

            def b_start(h):
                hold(pool, (pv_done, h * NKT + PV_AHEAD))

            heads(pool, step, b_start=b_start)

        @block.tensor
        def _(pe):
            pe.wait_ge(ready, READY)

            def by_query(h, g, u):
                n = h * QT + 4 * g + u
                slot = h & (SLOTS - 1)
                for c, (a, w) in enumerate(key_chunks):
                    hold(pe, (a_taken, 4 * n + c - 2 + 1 + A_AHEAD))
                    nc.tensor.matmul(sA[c % 2][:, 0:w],
                                     Qt[0:SHIFT_ROW, bass.ds(slot * S + (4 * g + u) * P, P)],
                                     Kb[0:SHIFT_ROW, bass.ds(slot * S + a, w)],
                                     start=True, stop=True).then_inc(a_formed, 1)

            def by_key(h, g, u):
                m = h * NKT + 4 * g + u
                slot = h & (SLOTS - 1)
                for c in range(QC):
                    for Q, bank, formed, taken, ahead in ((Qm, yP, y_formed, y_taken, Y_AHEAD),
                                                          (Qt, xP, x_formed, x_taken, X_AHEAD)):
                        hold(pe, (taken, 4 * m + c - 2 + 1 + ahead))
                        nc.tensor.matmul(bank[c % 2][:], Kb[:, bass.ds(slot * S + (4 * g + u) * P, P)],
                                         Q[:, bass.ds(slot * S + c * CH, CH)],
                                         start=True, stop=True).then_inc(formed, 1)

            def products(h, g, u):
                m = h * NKT + 4 * g + u
                hold(pe, (staged, m + 1),
                     (x_taken, 4 * (m + 1) + X_AHEAD))
                for c in range(QC):
                    mm = nc.tensor.matmul(O[32 * c:32 * (c + 1), :], Vh[:, u % 2], prob[:, u % 2, c],
                                          start=False, stop=False, skip_group_check=True)
                mm.then_inc(pv_done, 1)

            def step(ha, hb, g, u):
                first = isinstance(g, int) and g == 0 and u == 0
                if ha is not None:
                    by_query(ha, g, u)
                if hb is not None:
                    by_key(hb, g, u)
                    if not first:
                        products(hb, g if u else g - 1, (u - 1) % 4)

            def b_start(h):
                hold(pe, (o_taken, h + O_AHEAD))
                nc.tensor.matmul(O[:], G.zerob[:, 0:P], G.zerob[:], start=True, stop=False, skip_group_check=True)

            def b_end(h):
                products(h, (NKT - 1) // 4, (NKT - 1) % 4)
                hold(pe, (pv_done, (h + 1) * NKT + PV_AHEAD))
                pe.sem_inc(o_formed, 1)

            def a_end(h):
                hold(pe, (stats_set, h + 1))
                nc.tensor.transpose(turned[0:2 * QT, 0:P], stat[:], G.ident[:]).then_inc(st_turned, 1)

            def query_waits(step):
                def wrapped(ha, hb, g, u):
                    if ha is not None and u == 0:
                        hold(pe, (loaded, 3 * len(SPLITS) * 16 * (ha + 1) + SLOTS * 16))
                    if hb is not None and u == 0:
                        hold(pe, (st_loaded, 96 * (hb + 1) + 16))
                    step(ha, hb, g, u)
                return wrapped

            pe.sem_inc(pv_done, PV_AHEAD)
            heads(pe, query_waits(step), a_end=a_end, b_start=b_start, b_end=b_end, peel=True)

        @block.scalar
        def _(act):
            act.sem_inc(a_taken, A_AHEAD)
            act.sem_inc(y_taken, Y_AHEAD)
            act.sem_inc(o_taken, O_AHEAD)
            act.sem_inc(o_stored, 16)
            act.wait_ge(ready, READY)

            def step(ha, hb, g, u):
                if ha is not None:
                    n = ha * QT + 4 * g + u
                    hold(act, (s_free, n - 4 + 1 + S_AHEAD))
                    for c, (a, w) in enumerate(key_chunks):
                        hold(act, (a_formed, 4 * n + c + 1))
                        nc.scalar.activation(score[:, u, a:a + w], sA[c % 2][:, 0:w], ACT.Copy).then_inc(a_taken, 1)
                if hb is not None:
                    m = hb * NKT + 4 * g + u
                    for c in range(QC):
                        hold(act, (y_formed, 4 * m + c + 1),
                             (x_taken, 4 * m + c - 4 + 1 + X_AHEAD))
                        nc.scalar.activation(expd[:, c], yP[c % 2][:], ACT.Exp).then_inc(y_taken, 1)

            def b_end(h):
                hold(act, (o_formed, h + 1),
                     (o_stored, 64 * h + 16))
                nc.scalar.activation(O_out[:], O[:], ACT.Copy).then_inc(o_taken, 1)
                hold(act, (o_taken, h + 1 + O_AHEAD))
                for c in range(QC):
                    act.dma_start(G.sums[bass.ds(h, 1), :, c * CH:(c + 1) * CH],
                                  O_out[32 * c:32 * (c + 1), :]).then_inc(o_stored, 16)

            heads(act, step, b_end=b_end)
            act.wait_ge(o_stored, 64 * H + 16)

        @block.vector
        def _(dve):
            dve.sem_inc(s_free, S_AHEAD)
            dve.sem_inc(x_taken, X_AHEAD)
            dve.wait_ge(ready, READY)
            live = cand[:, :, 0:DEEP]

            def weigh(h, g, u, c):
                m = h * NKT + 4 * g + u
                hold(dve, (pv_done, m - 2 + 1 + PV_AHEAD),
                     (x_formed, 4 * m + c + 1),
                     (y_taken, 4 * m + c + 1 + Y_AHEAD))
                nc.vector.scalar_tensor_tensor(out=prob[:, u % 2, c], in0=xP[c % 2][:], scalar=0.0,
                                               in1=expd[:, c], op0=ALU.is_ge, op1=ALU.mult).then_inc(x_taken, 1)

            def rounds(values, between):
                at = between["at"]
                for r in range(ROUNDS):
                    dve.wait_ge(chain, at)
                    nc.vector.max(top[:, 8 * r:8 * r + 8], values).then_inc(chain, 1)
                    at += 1
                    if r < ROUNDS - 1:
                        if r in between:
                            between[r]()
                        dve.wait_ge(chain, at)
                        nc.vector.match_replace(values, top[:, 8 * r:8 * r + 8], values, -3.0e38).then_inc(chain, 1)
                        at += 1
                dve.wait_ge(chain, at)
                return at

            def record(g, u, at):
                i = 4 * g + u
                nc.vector.tensor_scalar(stat[:, bass.ds(i, 1)], top[:, 0:1], -1.0, None, ALU.mult).then_inc(chain, 1)
                nc.vector.tensor_scalar(stat[:, bass.ds(QT + i, 1)], top[:, TOPK - 1:TOPK], top[:, TOPK:TOPK + 1],
                                        -0.5, ALU.add, ALU.mult).then_inc(chain, 1)
                return at + 2

            def search(h, g, u, hb):
                n = h * QT + 4 * g + u
                nothing = lambda: None
                mask = (lambda c: (lambda: weigh(hb, g, u, c))) if hb is not None else (lambda c: nothing)
                dve.sem_clear(chain)
                hold(dve, (a_taken, 4 * (n + 1) + A_AHEAD))
                for j, (a, w) in enumerate(segs):
                    seg = nc.vector.max(cand[:, j], score[:, u, a:a + w])
                seg.then_inc(chain, 1)
                mask(0)()
                dve.wait_ge(chain, 1)
                nc.vector.max(deep[:, 0:8], cand[:, 0:NSEG, DEEP:8]).then_inc(chain, 1)
                nc.vector.tensor_reduce(eighth[:], cand[:, 0:NSEG, 7], AX.X, ALU.max).then_inc(chain, 1)
                dve.wait_ge(chain, 3)
                nc.vector.tensor_copy(cand[:, NSEG:NSEG + 3, 0:3], deep[:].rearrange("p (a b) -> p a b", a=3)).then_inc(chain, 1)
                at = rounds(live, {"at": 4, 0: mask(1), 1: mask(2), 2: mask(3)})
                at = record(g, u, at)
                dve.wait_ge(chain, at)
                nc.vector.tensor_scalar(flag[:, u:u + 1], eighth[:], deep[:, 7:8], top[:, TOPK:TOPK + 1],
                                        ALU.max, ALU.is_gt).then_inc(flagged, 1)
                hold(dve, (flagged, n + 1))

            def verify(h, g, u):
                n = h * QT + 4 * g + u
                hold(dve, (reduced, n + 1))
                found = dve.value_load(anyflag[0:1, u:u + 1].bitcast(I32), min_val=0, max_val=0x3F800000)
                with dve.If(found > 0):
                    dve.sem_clear(chain)
                    at = rounds_full(u)
                    at = record(g, u, at)
                    dve.wait_ge(chain, at)
                dve.sem_inc(s_free, 1)

            def rounds_full(u):
                dve.wait_ge(ready, READY)
                nc.vector.tensor_scalar(eighth[:], eighth[:], 1.0, None, ALU.mult).then_inc(chain, 1)
                return rounds(score[:, u], {"at": 1})

            def step(ha, hb, g, u):
                if ha is not None:
                    search(ha, g, u, hb)
                    if u:
                        verify(ha, g, u - 1)
                    if u == 3:
                        verify(ha, g, 3)
                else:
                    for c in range(QC):
                        weigh(hb, g, u, c)

            def a_end(h):
                dve.sem_inc(stats_set, 1)
                dve.sem_clear(chain)
                hold(dve, (st_turned, h + 1),
                     (st_loaded, 96 * h + 16))
                nc.vector.tensor_copy(statT[:], turned[0:2 * QT, 0:P]).then_inc(chain, 1)
                dve.wait_ge(chain, 1)
                nc.vector.tensor_copy(stat_parts[:, 0], statT[:]).then_inc(chain, 1)
                dve.wait_ge(chain, 2)
                nc.vector.tensor_tensor(stat_rest[:], statT[:], stat_parts[:, 0], ALU.subtract).then_inc(chain, 1)
                dve.wait_ge(chain, 3)
                nc.vector.tensor_copy(stat_parts[:, 1], stat_rest[:]).then_inc(chain, 1)
                dve.wait_ge(chain, 4)
                nc.vector.tensor_tensor(stat_rest[:], stat_rest[:], stat_parts[:, 1], ALU.subtract).then_inc(chain, 1)
                dve.wait_ge(chain, 5)
                nc.vector.tensor_copy(stat_parts[:, 2], stat_rest[:]).then_inc(st_split, 1)
                hold(dve, (st_split, h + 1))

            def b_start(h):
                hold(dve, (pv_done, h * NKT + PV_AHEAD))

            heads(dve, step, a_end=a_end)


def finish(nc, G, A, tag, wo, bo, den_eps):
    with ExitStack() as stack:
        s = Scope(nc, stack, tag)
        w_rows, wT = s.sb("w_rows", [P, KC, D]), s.sb("wT", [P, KC, D])
        bias = s.sb("bias", [1, D])
        num, den = s.sb("num", [P, KC, S]), s.sb("den", [P, KC, S])
        banks = [s.ps(f"bank{b}", [P, CH]) for b in range(4)]
        loaded, turned, w_ready, normed, formed, added = (s.sem(x) for x in (
            "loaded", "turned", "w_ready", "normed", "formed", "added"))
        block = stack.enter_context(nc.Block())
        LOADS = (2 + 2 * H) * 16
        STEPS = KC * (3 if den_eps else 2)

        @block.sync
        def _(sp):
            sp.dma_start(w_rows[:], wo.rearrange("(c p) d -> p c d", p=P)).then_inc(loaded, 16)
            sp.dma_start(bias[:], bo).then_inc(loaded, 16)
            for h in range(H):
                c, r = divmod(h * DH, P)
                sp.dma_start(num[r:r + DH, c], G.sums[h, 0:DH]).then_inc(loaded, 16)
                sp.dma_start(den[r:r + DH, c], G.sums[h, DH:2 * DH]).then_inc(loaded, 16)

        @block.tensor
        def _(pe):
            pe.wait_ge(loaded, LOADS)
            for ic in range(KC):
                for oc in range(KC):
                    mm = nc.tensor.transpose(banks[0][:, ic * D + oc * P:ic * D + (oc + 1) * P],
                                             w_rows[:, oc, ic * P:(ic + 1) * P], G.ident[:])
            mm.then_inc(turned, 1)
            pe.wait_ge(w_ready, 1)
            pe.wait_ge(normed, STEPS)
            for t in range(QT):
                if t >= 4:
                    pe.wait_ge(added, t - 3)
                bank = banks[t % 4][:, 0:D]
                for c in range(KC):
                    nc.tensor.matmul(bank, num[:, c, t * P:(t + 1) * P], wT[:, c], start=(c == 0), stop=False)
                nc.tensor.matmul(bank, G.ones[0:1, 0:P], bias[:], start=False, stop=True).then_inc(formed, 1)

        @block.scalar
        def _(act):
            act.wait_ge(turned, 1)
            nc.scalar.activation(wT[:], banks[0][:].rearrange("p (c d) -> p c d", c=KC), ACT.Copy).then_inc(w_ready, 1)

        @block.vector
        def _(dve):
            dve.wait_ge(loaded, LOADS)
            k = 0
            for c in range(KC):
                if den_eps:
                    nc.vector.tensor_scalar(den[:, c], den[:, c], den_eps, None, ALU.add).then_inc(normed, 1)
                    k += 1
                    dve.wait_ge(normed, k)
                nc.vector.reciprocal(den[:, c], den[:, c]).then_inc(normed, 1)
                k += 1
                dve.wait_ge(normed, k)
                nc.vector.tensor_tensor(num[:, c], num[:, c], den[:, c], ALU.mult).then_inc(normed, 1)
                k += 1
            for t in range(QT):
                dve.wait_ge(formed, t + 1)
                nc.vector.tensor_tensor(G.x_tok[:, t], banks[t % 4][:, 0:D], G.x_tok[:, t], ALU.add).then_inc(added, 1)
    layer_norm(nc, G, A, tag + "n")


def layer_norm(nc, G, A, tag, out=None, affine=None):
    with ExitStack() as stack:
        s = Scope(nc, stack, tag)
        bn = s.sb("bn", [P, QT, 6])
        mv = s.sb("mv", [P, QT, 2])
        dev = s.sb("dev", [P, QT])
        eps = s.sb("eps", [P, 1])
        y_tok = s.sb("y_tok", [P, QT, D]) if affine else G.x_tok
        if affine:
            rows = s.sb("rows", [2 * KC, P])
            cols = s.sb("cols", [P, 2 * KC])
        dstT = G.xn if affine else G.xT
        banks = [s.ps(f"bank{b}", [P, CH]) for b in range(2)]
        stats, agg, rooted, inv, normed, turned, taken, stored, loaded = (s.sem(x) for x in (
            "stats", "agg", "rooted", "inv", "normed", "turned", "taken", "stored", "loaded"))
        jobs = [(c, g) for g in range(0, QT, 4) for c in range(KC)]
        block = stack.enter_context(nc.Block())
        pre = 1 if affine else 0

        @block.vector
        def _(dve):
            nc.vector.memset(eps[:], EPS).then_inc(agg, 1)
            for t in range(QT):
                nc.vector.bn_stats(bn[:, t], G.x_tok[:, t]).then_inc(stats, 1)
            for t in range(QT):
                dve.wait_ge(stats, t + 1)
                nc.vector.bn_aggr(mv[:, t], bn[:, t]).then_inc(agg, 1)
            dve.wait_ge(rooted, 1)
            nc.vector.reciprocal(dev[:], dev[:]).then_inc(inv, 1)
            dve.wait_ge(inv, 1)
            dve.wait_ge(agg, QT + 1)
            for t in range(QT):
                nc.vector.tensor_scalar(y_tok[:, t], G.x_tok[:, t], mv[:, t, 0:1], dev[:, t:t + 1],
                                        ALU.subtract, ALU.mult).then_inc(normed, 1)

        @block.scalar
        def _(act):
            if affine:
                act.wait_ge(turned, 1)
                nc.scalar.activation(cols[:], banks[0][:, 0:2 * KC], ACT.Copy).then_inc(taken, 1)
            act.wait_ge(agg, QT + 1)
            nc.scalar.activation(dev[:], mv[:, :, 1], ACT.Sqrt, bias=eps[:]).then_inc(rooted, 1)
            if out is None:
                for j, (c, g) in enumerate(jobs):
                    act.wait_ge(turned, j + 1 + pre)
                    if affine:
                        act.wait_ge(taken, 1)
                        nc.scalar.activation(dstT[:, c, g * P:(g + 4) * P], banks[(j + pre) % 2][:], ACT.Identity,
                                             scale=cols[:, c:c + 1], bias=cols[:, KC + c:KC + c + 1]).then_inc(taken, 1)
                    else:
                        nc.scalar.activation(dstT[:, c, g * P:(g + 4) * P], banks[j % 2][:], ACT.Copy).then_inc(taken, 1)

        @block.tensor
        def _(pe):
            if affine:
                pe.wait_ge(loaded, 32)
                nc.tensor.transpose(banks[0][:, 0:2 * KC], rows[:], G.ident[0:2 * KC, 0:2 * KC]).then_inc(turned, 1)
            if out is None:
                for j, (c, g) in enumerate(jobs):
                    pe.wait_ge(normed, g + 4)
                    if j + pre >= 2:
                        pe.wait_ge(taken, j + pre - 1)
                    for k in range(4):
                        mm = nc.tensor.transpose(banks[(j + pre) % 2][:, k * P:(k + 1) * P],
                                                 y_tok[:, g + k, c * P:(c + 1) * P], G.ident[:])
                    mm.then_inc(turned, 1)

        @block.sync
        def _(sp):
            if affine:
                for j, v in enumerate(affine):
                    sp.dma_start(rows[j * KC:(j + 1) * KC], v.rearrange("(c p) -> c p", p=P)).then_inc(loaded, 16)
            if out is not None:
                for g in range(0, QT, 4):
                    sp.wait_ge(normed, g + 4)
                    sp.dma_start(out[0, g * P:(g + 4) * P].rearrange("(t p) d -> p t d", p=P),
                                 G.x_tok[:, g:g + 4]).then_inc(stored, 16)
                sp.wait_ge(stored, 16 * QT // 4)


def attend_causal(nc, G, tag, V):
    with ExitStack() as stack:
        s = Scope(nc, stack, tag)
        Kb = s.sb("k_stack", [ROWS, SLOTS * S], BF16)
        Qm = s.sb("q_stack", [ROWS, SLOTS * S], BF16)
        part_max = s.sb("part_max", [P, 2, QC])
        stat = s.sb("stat", [P, 32])
        statT = s.sb("statT", [32, P])
        stat_rest = s.sb("stat_rest", [32, P])
        stat_parts = s.sb("stat_parts", [32, 3, P], BF16)
        prob = s.sb("prob", [P, 2, QC, CH])
        Vh = s.sb("v_head", [P, 2, 2 * DH])
        O_out = s.sb("o_out", [P, CH])
        sA = [s.ps(f"by_query{b}", [P, CH]) for b in range(2)]
        yP = [s.ps(f"less_max{b}", [P, CH]) for b in range(2)]
        O = s.ps("o_sum", [P, CH])
        turned = s.ps("turned", [P, CH])
        (ready, loaded, a_formed, a_taken, y_formed, y_taken, staged, pv_done, o_formed, o_taken,
         o_stored, chain, maxed, stats_set, st_turned, st_split, st_loaded, passed) = (s.sem(x) for x in (
             "ready", "loaded", "a_formed", "a_taken", "y_formed", "y_taken", "staged", "pv_done",
             "o_formed", "o_taken", "o_stored", "chain", "maxed", "stats_set", "st_turned", "st_split",
             "st_loaded", "passed"))
        A_AHEAD, Y_AHEAD, PV_AHEAD, O_AHEAD, M_AHEAD = 2, 2, 2, 1, 1
        READY = 6
        PER_HEAD = 2 * QC * (QC + 1)
        block = stack.enter_context(nc.Block())

        def hold(eng, *events):
            for sem, n in events:
                eng.wait_ge(sem, n)
            if eng in (nc.vector, nc.gpsimd, nc.sync):
                eng.sem_inc(passed, 1)

        def a_index(h, L, ii):
            return h * PER_HEAD + 2 * L * (L + 1) + ii * (L + 1)

        def b_index(h, L, ii):
            return h * PER_HEAD + 16 * L - 2 * L * (L - 1) + ii * (QC - L)

        def heads(eng, step, a_end=None, b_start=None, b_end=None, peel=False):
            def level(ha, hb, L):
                def pair(jj):
                    for u in range(2):
                        step(ha, hb, L, jj, u)
                if peel and L == 0:
                    pair(0)
                    pair(1)
                else:
                    with eng.Fori(0, 2) as jj:
                        pair(jj)

            def head(ha, hb):
                if b_start and hb is not None:
                    b_start(hb)
                for L in range(QC):
                    level(ha, hb, L)
                if b_end and hb is not None:
                    b_end(hb)
                if a_end and ha is not None:
                    a_end(ha)

            head(0, None)
            with eng.Fori(0, H - 1) as h:
                head(h + 1, h)
            head(None, H - 1)

        @block.sync
        def _(sp):
            per_head = 2 * len(SPLITS) * 16

            def load(h):
                load_head(nc, G, sp, h, S, Kb, Qm, None, loaded)
                hold(sp, (loaded, per_head * (h + 1) + SLOTS * 16))

            def stats(h):
                hold(sp, (st_split, h + 1))
                slot = h & (SLOTS - 1)
                for j in range(3):
                    row = slice(SHIFT_ROW + j, SHIFT_ROW + j + 1)
                    sp.dma_start(Qm[row, bass.ds(slot * S, S)], stat_parts[0:QT, j]).then_inc(st_loaded, 16)
                hold(sp, (st_loaded, 48 * (h + 1) + 16))

            sp.sem_inc(st_loaded, 16)
            sp.wait_ge(ready, READY)
            for slot in range(SLOTS):
                sp.dma_start(Kb[MASK_ROW:MASK_ROW + 1, slot * S:(slot + 1) * S], G.mask_row[:]).then_inc(loaded, 16)
            for h in range(4):
                load(h)
                if h >= 2:
                    stats(h - 2)
            with sp.Fori(2, H - 2) as h:
                hold(sp, (o_formed, h - 1))
                load(h + 2)
                stats(h)
            stats(H - 2)
            stats(H - 1)

        @block.gpsimd
        def _(pool):
            nc.gpsimd.memset(Kb[:], 0.0).then_inc(ready, 1)
            pool.wait_ge(ready, 1)
            nc.gpsimd.memset(Kb[MASK_ROW:ROWS, :], 1.0).then_inc(ready, 1)
            pool.wait_ge(ready, 2)
            nc.gpsimd.memset(Qm[MASK_ROW:ROWS, :], 1.0).then_inc(ready, 1)
            pool.wait_ge(ready, 3)
            nc.gpsimd.memset(stat[:], 0.0).then_inc(ready, 1)
            pool.wait_ge(ready, 4)
            nc.gpsimd.memset(O_out[:], 0.0).then_inc(ready, 1)
            pool.wait_ge(ready, 5)
            nc.gpsimd.memset(part_max[:], 0.0).then_inc(ready, 1)
            pool.wait_ge(ready, READY)

            def step(ha, hb, L, jj, u):
                if hb is not None:
                    i = 4 * L + 2 * jj + u
                    hold(pool, (pv_done, hb * QT + i - 2 + 1 + PV_AHEAD))
                    nc.gpsimd.tensor_copy(Vh[:, u], V[:, bass.ds(i, 1), bass.ds(hb, 1), :]).then_inc(staged, 1)

            heads(pool, step)

        @block.tensor
        def _(pe):
            pe.sem_inc(pv_done, PV_AHEAD)
            pe.wait_ge(ready, READY)

            def by_query(h, L, jj, u):
                ii = 2 * jj + u
                slot = h & (SLOTS - 1)
                for c in range(L + 1):
                    hold(pe, (a_taken, a_index(h, L, ii) + c - 2 + 1 + A_AHEAD))
                    bank = sA[(u * (L + 1) + c) % 2]
                    mm = nc.tensor.matmul(bank[:], Qm[0:SHIFT_ROW, bass.ds(slot * S + (4 * L + ii) * P, P)],
                                          Kb[0:SHIFT_ROW, bass.ds(slot * S + c * CH, CH)],
                                          start=True, stop=(c < L))
                    if c == L:
                        mm = nc.tensor.matmul(bank[:], G.identb[:], G.band[:, 0, bass.ds((3 - ii) * P, CH)],
                                              start=False, stop=True)
                    mm.then_inc(a_formed, 1)

            def by_key(h, L, jj, u):
                ii = 2 * jj + u
                slot = h & (SLOTS - 1)
                for c in range(L, QC):
                    hold(pe, (y_taken, b_index(h, L, ii) + c - L - 2 + 1 + Y_AHEAD))
                    bank = yP[(u * (QC - L) + c - L) % 2]
                    mm = nc.tensor.matmul(bank[:], Kb[:, bass.ds(slot * S + (4 * L + ii) * P, P)],
                                          Qm[:, bass.ds(slot * S + c * CH, CH)], start=True, stop=(c > L))
                    if c == L:
                        mm = nc.tensor.matmul(bank[:], G.identb[:], G.band[:, 1, bass.ds((3 - ii) * P, CH)],
                                              start=False, stop=True)
                    mm.then_inc(y_formed, 1)

            def products(h, L, jj, u):
                ii = 2 * jj + u
                hold(pe, (staged, h * QT + 4 * L + ii + 1),
                     (y_taken, b_index(h, L, ii) + QC - L + Y_AHEAD))
                for c in range(L, QC):
                    mm = nc.tensor.matmul(O[32 * c:32 * (c + 1), :], Vh[:, u], prob[:, u, c],
                                          start=False, stop=False, skip_group_check=True)
                mm.then_inc(pv_done, 1)

            def step(ha, hb, L, jj, u):
                if ha is not None:
                    if u == 0:
                        hold(pe, (loaded, 2 * len(SPLITS) * 16 * (ha + 1) + SLOTS * 16))
                    by_query(ha, L, jj, u)
                if hb is not None:
                    if u == 0:
                        hold(pe, (st_loaded, 48 * (hb + 1) + 16))
                    by_key(hb, L, jj, u)
                    first = L == 0 and isinstance(jj, int) and jj == 0 and u == 0
                    if u:
                        products(hb, L, jj, 0)
                        products(hb, L, jj, 1)

            def b_start(h):
                hold(pe, (o_taken, h + O_AHEAD))
                nc.tensor.matmul(O[:], G.zerob[:, 0:P], G.zerob[:], start=True, stop=False, skip_group_check=True)

            def b_end(h):
                hold(pe, (pv_done, (h + 1) * QT + PV_AHEAD))
                pe.sem_inc(o_formed, 1)

            def a_end(h):
                hold(pe, (stats_set, h + 1))
                nc.tensor.transpose(turned[0:32, 0:P], stat[:], G.ident[:]).then_inc(st_turned, 1)

            heads(pe, step, a_end=a_end, b_start=b_start, b_end=b_end)

        @block.scalar
        def _(act):
            act.sem_inc(y_taken, Y_AHEAD)
            act.sem_inc(o_taken, O_AHEAD)
            act.sem_inc(o_stored, 16)
            act.wait_ge(ready, READY)

            def step(ha, hb, L, jj, u):
                if hb is not None:
                    ii = 2 * jj + u
                    hold(act, (pv_done, hb * QT + 4 * L + ii - 2 + 1 + PV_AHEAD))
                    for c in range(L, QC):
                        hold(act, (y_formed, b_index(hb, L, ii) + c - L + 1))
                        nc.scalar.activation(prob[:, u, c], yP[(u * (QC - L) + c - L) % 2][:],
                                             ACT.Exp).then_inc(y_taken, 1)

            def b_end(h):
                hold(act, (o_formed, h + 1),
                     (o_stored, 64 * h + 16))
                nc.scalar.activation(O_out[:], O[:], ACT.Copy).then_inc(o_taken, 1)
                hold(act, (o_taken, h + 1 + O_AHEAD))
                for c in range(QC):
                    act.dma_start(G.sums[bass.ds(h, 1), :, c * CH:(c + 1) * CH],
                                  O_out[32 * c:32 * (c + 1), :]).then_inc(o_stored, 16)

            heads(act, step, b_end=b_end)
            act.wait_ge(o_stored, 64 * H + 16)

        @block.vector
        def _(dve):
            dve.sem_inc(a_taken, A_AHEAD)
            dve.sem_inc(maxed, M_AHEAD)
            dve.wait_ge(ready, READY)

            def step(ha, hb, L, jj, u):
                if ha is not None:
                    ii = 2 * jj + u
                    i = 4 * L + ii
                    hold(dve, (maxed, ha * QT + i - 1 + M_AHEAD))
                    for c in range(L + 1):
                        hold(dve, (a_formed, a_index(ha, L, ii) + c + 1))
                        nc.vector.tensor_reduce(part_max[:, u, c:c + 1], sA[(u * (L + 1) + c) % 2][:],
                                                AX.X, ALU.max).then_inc(a_taken, 1)
                    hold(dve, (a_taken, a_index(ha, L, ii) + L + 1 + A_AHEAD))
                    nc.vector.tensor_reduce(stat[:, bass.ds(i, 1)], part_max[:, u, 0:L + 1], AX.X, ALU.max,
                                            negate=True).then_inc(maxed, 1)

            def a_end(h):
                hold(dve, (maxed, (h + 1) * QT + M_AHEAD))
                dve.sem_inc(stats_set, 1)
                dve.sem_clear(chain)
                hold(dve, (st_turned, h + 1),
                     (st_loaded, 48 * h + 16))
                nc.vector.tensor_copy(statT[:], turned[0:32, 0:P]).then_inc(chain, 1)
                dve.wait_ge(chain, 1)
                nc.vector.tensor_copy(stat_parts[:, 0], statT[:]).then_inc(chain, 1)
                dve.wait_ge(chain, 2)
                nc.vector.tensor_tensor(stat_rest[:], statT[:], stat_parts[:, 0], ALU.subtract).then_inc(chain, 1)
                dve.wait_ge(chain, 3)
                nc.vector.tensor_copy(stat_parts[:, 1], stat_rest[:]).then_inc(chain, 1)
                dve.wait_ge(chain, 4)
                nc.vector.tensor_tensor(stat_rest[:], stat_rest[:], stat_parts[:, 1], ALU.subtract).then_inc(chain, 1)
                dve.wait_ge(chain, 5)
                nc.vector.tensor_copy(stat_parts[:, 2], stat_rest[:]).then_inc(st_split, 1)
                hold(dve, (st_split, h + 1))

            heads(dve, step, a_end=a_end)


EXPERTS = 8
HID = 512
LIMIT = 7.0
ALPHA = 1.702


def moe_gate(nc, G, A, M):
    with ExitStack() as stack:
        s = Scope(nc, stack, "gate")
        square = s.sb("square", [P, 2, D])
        sums, rms = s.sb("sums", [P, QT]), s.sb("rms", [P, QT])
        eps = s.sb("eps", [P, 1])
        t_tok = s.sb("t_tok", [P, QT, D])
        scale_rows, scale = s.sb("scale_rows", [KC, P]), s.sb("scale", [P, KC])
        gate_w, gate_b = s.sb("gate_w", [P, KC, EXPERTS]), s.sb("gate_b", [1, EXPERTS])
        b1_rows = s.sb("b1_rows", [4 * EXPERTS, 2 * P])
        b2 = s.sb("b2", [EXPERTS, D])
        ids = s.sb("ids", [P, EXPERTS])
        logits = s.sb("logits", [P, QT, EXPERTS])
        best, where = s.sb("best", [P, QT, 8]), s.sb("where", [P, QT, 8], U32)
        wheref = s.sb("wheref", [P, QT, 8])
        gap, e2, total = s.sb("gap", [P, QT]), s.sb("e2", [P, QT]), s.sb("total", [P, QT])
        p1, p2 = s.sb("p1", [P, QT]), s.sb("p2", [P, QT])
        w2nd = s.sb("w2nd", [P, QT, EXPERTS])
        wT = s.sb("wT", [EXPERTS, S])
        banks = [s.ps(f"bank{b}", [P, CH]) for b in range(3)]
        small = s.ps("small", [P, CH])
        logit_bank = s.ps("logit_bank", [P, CH])
        (loaded, squared, rooted, inv, scaled, turned, taken, small_formed, small_taken, logged, step, expd,
         weighed, w_turned, w_taken, y_formed, added) = (s.sem(x) for x in (
             "loaded", "squared", "rooted", "inv", "scaled", "turned", "taken", "small_formed",
             "small_taken", "logged", "step", "expd", "weighed", "w_turned", "w_taken", "y_formed", "added"))
        jobs = [(c, g) for g in range(0, QT, 4) for c in range(KC)]
        LOADS = 6 * 16
        block = stack.enter_context(nc.Block())

        @block.sync
        def _(sp):
            sp.dma_start(scale_rows[:], A["L0_ffn_norm_scale"].rearrange("(c p) -> c p", p=P)).then_inc(loaded, 16)
            sp.dma_start(gate_w[:], A["L0_ffn_gate_w"].rearrange("(c p) e -> p c e", p=P)).then_inc(loaded, 16)
            sp.dma_start(gate_b[:], A["L0_ffn_gate_b"].rearrange("(o n) -> o n", o=1)).then_inc(loaded, 16)
            sp.dma_start(b1_rows[:], A["L0_ffn_mlp1_b"].rearrange("e (j n) -> (e j) n", n=2 * P)).then_inc(loaded, 16)
            sp.dma_start(b2[:], A["L0_ffn_mlp2_b"]).then_inc(loaded, 16)
            sp.dma_start(ids[:], A["const_experts"]).then_inc(loaded, 16)

        @block.scalar
        def _(act):
            act.wait_ge(small_formed, 1)
            nc.scalar.activation(scale[:], small[:, 0:KC], ACT.Copy).then_inc(small_taken, 1)
            nc.scalar.activation(M.b_glu[:], small[:, 64:64 + 4 * EXPERTS], ACT.Copy).then_inc(small_taken, 1)
            nc.scalar.activation(M.b_lin[:], small[:, 128:128 + 4 * EXPERTS], ACT.Copy, bias=1.0).then_inc(small_taken, 1)
            for t in range(QT):
                if t >= 2:
                    act.wait_ge(squared, t - 1)
                nc.scalar.activation(square[:, t % 2], G.x_tok[:, t], ACT.Square,
                                     accum_out=sums[:, t:t + 1]).then_inc(squared, 1)
            act.wait_ge(squared, QT)
            act.wait_ge(step, 1)
            nc.scalar.activation(rms[:], sums[:], ACT.Sqrt, bias=eps[:], scale=1.0 / D).then_inc(rooted, 1)
            act.wait_ge(small_taken, 1)
            for j, (c, g) in enumerate(jobs):
                act.wait_ge(turned, j + 1)
                nc.scalar.activation(M.tT[:, c, g * P:(g + 4) * P], banks[j % 2][:], ACT.Copy,
                                     scale=scale[:, c:c + 1]).then_inc(taken, 1)
            act.wait_ge(step, 4)
            nc.scalar.activation(e2[:], gap[:], ACT.Exp).then_inc(expd, 1)
            for g in range(QT // 4):
                act.wait_ge(w_turned, g + 1)
                nc.scalar.activation(wT[:, g * CH:(g + 1) * CH], banks[g % 2][0:EXPERTS, :], ACT.Copy).then_inc(w_taken, 1)

        @block.tensor
        def _(pe):
            pe.wait_ge(loaded, LOADS)
            nc.tensor.transpose(small[:, 0:KC], scale_rows[:], G.ident[0:KC, 0:KC])
            rows = b1_rows[:].rearrange("r (p two) -> r p two", two=2)
            n = 4 * EXPERTS
            nc.tensor.transpose(small[:, 64:64 + n], rows[:, :, 0], G.ident[0:n, 0:n])
            nc.tensor.transpose(small[:, 128:128 + n], rows[:, :, 1], G.ident[0:n, 0:n]).then_inc(small_formed, 1)
            for j, (c, g) in enumerate(jobs):
                pe.wait_ge(scaled, g + 4)
                if j >= 2:
                    pe.wait_ge(taken, j - 1)
                for k in range(4):
                    mm = nc.tensor.transpose(banks[j % 2][:, k * P:(k + 1) * P],
                                             t_tok[:, g + k, c * P:(c + 1) * P], G.ident[:])
                mm.then_inc(turned, 1)
            pe.wait_ge(taken, len(jobs))
            for t in range(QT):
                to = logit_bank[:, t * EXPERTS:(t + 1) * EXPERTS]
                for c in range(KC):
                    nc.tensor.matmul(to, M.tT[:, c, t * P:(t + 1) * P], gate_w[:, c], start=(c == 0), stop=False)
                mm = nc.tensor.matmul(to, G.ones[0:1, 0:P], gate_b[:], start=False, stop=True)
            mm.then_inc(logged, 1)
            pe.wait_ge(weighed, 1)
            for g in range(QT // 4):
                if g >= 2:
                    pe.wait_ge(w_taken, g - 1)
                for k in range(4):
                    mm = nc.tensor.transpose(banks[g % 2][0:EXPERTS, k * P:(k + 1) * P], M.w[:, 4 * g + k], G.ident[:])
                mm.then_inc(w_turned, 1)
            pe.wait_ge(w_taken, QT // 4)
            for t in range(QT):
                if t >= 2:
                    pe.wait_ge(added, t - 1)
                nc.tensor.matmul((banks[2], small)[t % 2][:, 0:D], wT[:, t * P:(t + 1) * P], b2[:],
                                 start=True, stop=True).then_inc(y_formed, 1)

        @block.vector
        def _(dve):
            nc.vector.memset(eps[:], EPS).then_inc(step, 1)
            dve.wait_ge(rooted, 1)
            nc.vector.reciprocal(rms[:], rms[:]).then_inc(inv, 1)
            dve.wait_ge(inv, 1)
            for t in range(QT):
                nc.vector.tensor_scalar(t_tok[:, t], G.x_tok[:, t], rms[:, t:t + 1], None, ALU.mult).then_inc(scaled, 1)
            dve.wait_ge(logged, 1)
            nc.vector.tensor_copy(logits[:], logit_bank[:, 0:QT * EXPERTS].rearrange("p (t e) -> p t e", e=EXPERTS)).then_inc(step, 1)
            dve.wait_ge(step, 2)
            for t in range(QT):
                mx = nc.vector.max(best[:, t], logits[:, t])
            mx.then_inc(step, 1)
            dve.wait_ge(step, 3)
            nc.vector.tensor_tensor(gap[:], best[:, :, 1], best[:, :, 0], ALU.subtract).then_inc(step, 1)
            for t in range(QT):
                mi = nc.vector.max_index(where[:, t], best[:, t], logits[:, t])
            mi.then_inc(step, 1)
            dve.wait_ge(step, 5)
            nc.vector.tensor_copy(wheref[:], where[:]).then_inc(step, 1)
            dve.wait_ge(expd, 1)
            nc.vector.tensor_scalar(total[:], e2[:], 1.0, None, ALU.add).then_inc(step, 1)
            dve.wait_ge(step, 7)
            nc.vector.reciprocal(p1[:], total[:]).then_inc(step, 1)
            dve.wait_ge(step, 8)
            nc.vector.tensor_tensor(p2[:], p1[:], e2[:], ALU.mult).then_inc(step, 1)
            dve.wait_ge(step, 9)
            dve.wait_ge(loaded, LOADS)
            for t in range(QT):
                nc.vector.tensor_scalar(M.w[:, t], ids[:], wheref[:, t, 0:1], p1[:, t:t + 1], ALU.is_equal, ALU.mult)
                last = nc.vector.tensor_scalar(w2nd[:, t], ids[:], wheref[:, t, 1:2], p2[:, t:t + 1], ALU.is_equal, ALU.mult)
            last.then_inc(step, 1)
            dve.wait_ge(step, 10)
            nc.vector.tensor_tensor(M.w[:], M.w[:], w2nd[:], ALU.add).then_inc(weighed, 1)
            for t in range(QT):
                dve.wait_ge(y_formed, t + 1)
                nc.vector.scalar_tensor_tensor(out=G.x_tok[:, t], in0=G.x_tok[:, t], scalar=2.0,
                                               in1=(banks[2], small)[t % 2][:, 0:D],
                                               op0=ALU.mult, op1=ALU.add).then_inc(added, 1)


def moe_experts(nc, G, A, M):
    HT = HID // P
    with ExitStack() as stack:
        s = Scope(nc, stack, "moe")
        w1 = [s.sb(f"w1_{u}", [P, KC, 2 * HID]) for u in range(2)]
        w2 = [s.sb(f"w2_{u}", [P, HT, D]) for u in range(2)]
        glu, sig, lin = s.sb("glu", [P, 2, CH]), s.sb("sig", [P, 2, CH]), s.sb("lin", [P, 2, CH])
        act_glu = s.sb("act_glu", [P, 2, CH])
        hid = s.sb("hid", [P, 2, HT, CH])
        gP = [s.ps(f"glu{b}", [P, CH]) for b in range(2)]
        lP = [s.ps(f"lin{b}", [P, CH]) for b in range(2)]
        yP = [[s.ps(f"y{b}{k}", [P, CH]) for k in range(2)] for b in range(2)]
        (ready, g_formed, l_formed, g_taken, l_taken, sigged, gated, hidden, y_formed, y_taken, passed) = (
            s.sem(x) for x in ("ready", "g_formed", "l_formed", "g_taken", "l_taken", "sigged", "gated",
                               "hidden", "y_formed", "y_taken", "passed"))
        w_loaded = [s.sem(f"w_loaded{u}") for u in range(2)]
        G_AHEAD, H_AHEAD, Y_AHEAD = 2, 2, 4
        block = stack.enter_context(nc.Block())

        def hold(eng, *events):
            for sem, n in events:
                eng.wait_ge(sem, n)
            if eng in (nc.gpsimd, nc.sync):
                eng.sem_inc(passed, 1)

        def pairs(eng, body):
            with eng.Fori(0, EXPERTS // 2) as ep:
                for u in range(2):
                    with eng.Fori(0, QC // 2) as cc:
                        body(ep, u, cc, (ep * 2 + u) * (QC // 2) + cc)

        @block.sync
        def _(sp):
            src1 = A["L0_ffn_mlp1_w"].rearrange("e (c p) n -> e p c n", p=P)
            src2 = A["L0_ffn_mlp2_w"].rearrange("e (c p) n -> e p c n", p=P)

            def load(e, u):
                for ic in range(KC):
                    sp.dma_start(w1[u][:, ic], src1[bass.ds(e, 1), :, ic]).then_inc(w_loaded[u], 16)
                for ic in range(HT):
                    sp.dma_start(w2[u][:, ic], src2[bass.ds(e, 1), :, ic]).then_inc(w_loaded[u], 16)

            for u in range(2):
                load(u, u)
            with sp.Fori(1, EXPERTS // 2) as ep:
                for u in range(2):
                    e = ep * 2 + u
                    hold(sp, (y_formed, 2 * QC * (e - 1)))
                    load(e, u)

        @block.tensor
        def _(pe):
            def pair(ep, u, cc, p):
                hold(pe, (w_loaded[u], (ep + 1) * 16 * (KC + HT)))
                taps = w1[u][:].rearrange("p c (j m two) -> p c j m two", j=HT, two=2)
                for c2 in range(2):
                    for j in range(HT):
                        z = p * 2 * HT + c2 * HT + j
                        hold(pe, (g_taken, z - 2 + 1 + G_AHEAD), (l_taken, z - 2 + 1 + G_AHEAD))
                        for two, bank, formed in ((0, gP, g_formed), (1, lP, l_formed)):
                            for ic in range(KC):
                                mm = nc.tensor.matmul(bank[j % 2][:], taps[:, ic, j, :, two],
                                                      M.tT[:, ic, bass.ds(cc * 2 * CH + c2 * CH, CH)],
                                                      start=(ic == 0), stop=(ic == KC - 1))
                            mm.then_inc(formed, 1)
                for c2 in range(2):
                    q = p * 2 + c2
                    hold(pe, (hidden, (q + 1) * HT + H_AHEAD), (y_taken, 2 * q - 4 + 2 + Y_AHEAD))
                    for k in range(4):
                        to = yP[c2][k // 2][:, (k % 2) * D:(k % 2 + 1) * D]
                        for j in range(HT):
                            mm = nc.tensor.matmul(to, hid[:, c2, j, k * P:(k + 1) * P], w2[u][:, j],
                                                  start=(j == 0), stop=(j == HT - 1))
                        if k % 2:
                            mm.then_inc(y_formed, 1)
            pairs(pe, pair)

        @block.scalar
        def _(act):
            def pair(ep, u, cc, p):
                for c2 in range(2):
                    for j in range(HT):
                        z = p * 2 * HT + c2 * HT + j
                        hold(act, (g_taken, z + 1 + G_AHEAD), (gated, z - 2 + 1 + G_AHEAD))
                        nc.scalar.activation(sig[:, j % 2], glu[:, j % 2], ACT.Sigmoid, scale=ALPHA).then_inc(sigged, 1)
            pairs(act, pair)

        @block.gpsimd
        def _(pool):
            pool.sem_inc(gated, G_AHEAD)

            def pair(ep, u, cc, p):
                for c2 in range(2):
                    for j in range(HT):
                        z = p * 2 * HT + c2 * HT + j
                        hold(pool, (sigged, z + 1), (hidden, z - 2 + 1 + H_AHEAD))
                        nc.gpsimd.tensor_tensor(act_glu[:, j % 2], glu[:, j % 2], sig[:, j % 2], ALU.mult).then_inc(gated, 1)
            pairs(pool, pair)

        @block.vector
        def _(dve):
            dve.sem_inc(g_taken, G_AHEAD)
            dve.sem_inc(l_taken, G_AHEAD)
            dve.sem_inc(hidden, H_AHEAD)
            dve.sem_inc(y_taken, Y_AHEAD)

            def pair(ep, u, cc, p):
                def hide(zz):
                    c2, j = divmod(zz, HT)
                    z = p * 2 * HT + zz
                    hold(dve, (gated, z + 1 + G_AHEAD), (l_taken, z + 1 + G_AHEAD))
                    nc.vector.scalar_tensor_tensor(out=hid[:, c2, j], in0=lin[:, j % 2], scalar=1.0 - LIMIT,
                                                   in1=act_glu[:, j % 2], op0=ALU.max, op1=ALU.mult).then_inc(hidden, 1)
                hold(dve, (y_taken, 4 * p + Y_AHEAD))
                for zz in range(2 * HT):
                    c2, j = divmod(zz, HT)
                    z = p * 2 * HT + zz
                    col = bass.ds((ep * 2 + u) * HT + j, 1)
                    hold(dve, (g_formed, z + 1), (gated, z - 2 + 1 + G_AHEAD))
                    nc.vector.tensor_scalar(glu[:, j % 2], gP[j % 2][:], M.b_glu[:, col], LIMIT, ALU.add,
                                            ALU.min).then_inc(g_taken, 1)
                    hold(dve, (l_formed, z + 1), (hidden, z - 2 + 1 + H_AHEAD))
                    nc.vector.tensor_scalar(lin[:, j % 2], lP[j % 2][:], M.b_lin[:, col], LIMIT + 1.0, ALU.add,
                                            ALU.min).then_inc(l_taken, 1)
                    if zz:
                        hide(zz - 1)
                hide(2 * HT - 1)
                for c2 in range(2):
                    for k in range(4):
                        if k % 2 == 0:
                            hold(dve, (y_formed, 2 * (p * 2 + c2) + k // 2 + 1))
                        t = cc * 8 + c2 * 4 + k
                        row = G.x_tok[:, bass.ds(t, 1), :]
                        add = nc.vector.scalar_tensor_tensor(out=row, in0=yP[c2][k // 2][:, (k % 2) * D:(k % 2 + 1) * D],
                                                       scalar=M.w[:, bass.ds(t, 1), bass.ds(ep * 2 + u, 1)],
                                                       in1=row, op0=ALU.mult, op1=ALU.add)
                        if k % 2:
                            add.then_inc(y_taken, 1)
            pairs(dve, pair)


XH = 64
XI = H * XH
XC = XI // P
XSLOTS = 2
X_MASK, X_SHIFT = XH, XH + 1
XROWS = XH + 2


def project_wide(nc, G, A, V):
    kt = tiles_of(NCTX)
    with ExitStack() as stack:
        s = Scope(nc, stack, "l1xp")
        wq, wk = s.sb("wq", [P, KC, XI]), s.sb("wk", [P, KC, XI])
        full = s.sb("full", [P, 2, S])
        rest = s.sb("rest", [P, S])
        parts = s.sb("parts", [P, 2, 2, S], BF16)
        banks = [s.ps(f"bank{b}", [P, CH]) for b in range(4)]
        vbanks = [s.ps(f"vbank{b}", [P, CH]) for b in range(4)]
        loaded, v_loaded, formed, taken, split, rest_done, v_formed, v_taken, v_clear = (s.sem(x) for x in (
            "loaded", "v_loaded", "formed", "taken", "split", "rest_done", "v_formed", "v_taken", "v_clear"))
        stored = [s.sem(f"stored{b}") for b in range(2)]
        units = [(w, oc) for w in range(2) for oc in range(XC)]
        chunks = [tiles_of(S, CH) if w == 0 else tiles_of(NCTX, CH) for w, _ in units]
        ends = [sum(len(x) for x in chunks[:u + 1]) for u in range(len(units))]
        order = [(u, c) for u in range(len(units)) for c in range(len(chunks[u]))]
        v_jobs = [(t, half) for t in range(len(kt)) for half in range(XI // CH)]
        w_kv = A["L1_xattn_w_kv"].rearrange("(c p) n -> p c n", p=P)
        block = stack.enter_context(nc.Block())

        @block.sync
        def _(sp):
            sp.dma_start(wq[:], A["L1_xattn_w_q"].rearrange("(c p) n -> p c n", p=P)).then_inc(loaded, 16)
            sp.dma_start(wk[:], w_kv[:, :, 0:XI]).then_inc(loaded, 16)
            for u, (w, oc) in enumerate(units):
                if u == XC:
                    sp.wait_ge(formed, ends[XC - 1])
                    sp.dma_start(wq[:], w_kv[:, :, XI:2 * XI]).then_inc(v_loaded, 16)
                n = S if w == 0 else NCTX
                sp.wait_ge(split, 2 * (u + 1))
                dst = G.wide_q if w == 0 else G.wide_k
                dst_parts = G.wide_q_parts if w == 0 else G.wide_k_parts
                sp.dma_start(dst[oc * P:(oc + 1) * P, 0:n], full[:, u % 2, 0:n]).then_inc(stored[u % 2], 16)
                for j in range(2):
                    sp.dma_start(dst_parts[j, oc * P:(oc + 1) * P, 0:n], parts[:, u % 2, j, 0:n]).then_inc(stored[u % 2], 16)
            for u in range(2):
                sp.wait_ge(stored[u], 3 * 16 * len(units) // 2)

        @block.gpsimd
        def _(pool):
            nc.gpsimd.memset(V[:, len(kt) - 1], 0.0).then_inc(v_clear, 1)

        @block.tensor
        def _(pe):
            pe.wait_ge(loaded, 32)
            for n, (u, c) in enumerate(order):
                w, oc = units[u]
                a, m = chunks[u][c]
                if n >= 4:
                    pe.wait_ge(taken, n - 3)
                for ic in range(KC):
                    mm = nc.tensor.matmul(banks[n % 4][:, 0:m], (wq, wk)[w][:, ic, oc * P:(oc + 1) * P],
                                          (G.xn, G.ctxT)[w][:, ic, a:a + m], start=(ic == 0), stop=(ic == KC - 1))
                mm.then_inc(formed, 1)
            pe.wait_ge(v_loaded, 16)
            for n, (t, half) in enumerate(v_jobs):
                a, m = kt[t]
                if n >= 4:
                    pe.wait_ge(v_taken, n - 3)
                for ic in range(KC):
                    mm = nc.tensor.matmul(vbanks[n % 4][0:m, :], G.ctxT[:, ic, a:a + m],
                                          wq[:, ic, half * CH:(half + 1) * CH], start=(ic == 0), stop=(ic == KC - 1))
                mm.then_inc(v_formed, 1)

        @block.scalar
        def _(act):
            for u, (w, oc) in enumerate(units):
                n = S if w == 0 else NCTX
                if u >= 2:
                    act.wait_ge(stored[u % 2], 3 * 16 * (u // 2))
                    act.wait_ge(rest_done, u - 1)
                for c, (a, m) in enumerate(chunks[u]):
                    at = (ends[u - 1] if u else 0) + c
                    act.wait_ge(formed, at + 1)
                    nc.scalar.activation(full[:, u % 2, a:a + m], banks[at % 4][:, 0:m], ACT.Copy,
                                         scale=0.125 if w == 0 else 1.0).then_inc(taken, 1)
                act.wait_ge(taken, ends[u])
                nc.scalar.activation(parts[:, u % 2, 0, 0:n], full[:, u % 2, 0:n], ACT.Copy).then_inc(split, 1)
                act.wait_ge(rest_done, u + 1)
                nc.scalar.activation(parts[:, u % 2, 1, 0:n], rest[:, 0:n], ACT.Copy).then_inc(split, 1)

        @block.vector
        def _(dve):
            for u, (w, oc) in enumerate(units):
                n = S if w == 0 else NCTX
                dve.wait_ge(split, 2 * u + 1)
                nc.vector.tensor_tensor(rest[:, 0:n], full[:, u % 2, 0:n], parts[:, u % 2, 0, 0:n],
                                        ALU.subtract).then_inc(rest_done, 1)
            dve.wait_ge(v_clear, 1)
            for n, (t, half) in enumerate(v_jobs):
                dve.wait_ge(v_formed, n + 1)
                m = kt[t][1]
                nc.vector.tensor_copy(V[0:m, t, half * CH:(half + 1) * CH], vbanks[n % 4][0:m, :]).then_inc(v_taken, 1)


def attend_wide(nc, G, V):
    kt = tiles_of(NCTX)
    NKT = len(kt)
    key_chunks = tiles_of(NCTX, CH)
    NCH = len(key_chunks)
    with ExitStack() as stack:
        s = Scope(nc, stack, "l1xc")
        k32, q32 = s.sb("k32", [XROWS, XSLOTS * NKT * P]), s.sb("q32", [XROWS, XSLOTS * S])
        qa = s.sb("q_hm", [P, XSLOTS * S], BF16)
        kh = s.sb("k_hh", [P, XSLOTS * S], BF16)
        km = s.sb("k_m0", [P, XSLOTS * S], BF16)
        part_max = s.sb("part_max", [P, 2, NCH])
        stat, statT = s.sb("stat", [P, 32]), s.sb("statT", [32, P])
        prob = s.sb("prob", [P, 2, QC, CH])
        Kh, Vh = s.sb("k_tile", [XROWS, 2, P]), s.sb("v_tile", [P, 2, XH])
        O_out = s.sb("o_out", [P, 3, CH])
        sA = [s.ps(f"by_query{b}", [P, CH]) for b in range(2)]
        yP = [s.ps(f"less_max{b}", [P, CH]) for b in range(2)]
        O = [s.ps(f"o_sum{b}", [P, CH]) for b in range(2)]
        Den = s.ps("den", [P, CH])
        turned = s.ps("turned", [P, CH])
        (ready, a_loaded, b_loaded, a_formed, a_taken, y_formed, y_taken, k_staged, v_staged, pv_done,
         o_formed, o_taken, o_stored, maxed, stats_set, st_turned, st_out, st_loaded, passed) = (s.sem(x) for x in (
             "ready", "a_loaded", "b_loaded", "a_formed", "a_taken", "y_formed", "y_taken", "k_staged",
             "v_staged", "pv_done", "o_formed", "o_taken", "o_stored", "maxed", "stats_set", "st_turned",
             "st_out", "st_loaded", "passed"))
        AHEAD = 2
        READY = 11
        A_LOADS, B_LOADS = 5 * 16, 2 * 16
        block = stack.enter_context(nc.Block())

        def hold(eng, *events):
            for sem, n in events:
                eng.wait_ge(sem, n)
            if eng in (nc.vector, nc.gpsimd, nc.sync):
                eng.sem_inc(passed, 1)

        def heads(eng, step, a_end=None, b_start=None, b_end=None):
            def pair(ha, hb, g, last=False):
                for u in range(2):
                    step(ha, hb if not (last and u) else None, g, u)

            def head(ha, hb):
                if b_start and hb is not None:
                    b_start(hb)
                if hb is None:
                    with eng.Fori(0, QT // 2) as g:
                        pair(ha, None, g)
                else:
                    with eng.Fori(0, NKT // 2) as g:
                        pair(ha, hb, g)
                    pair(ha, hb, NKT // 2, last=True)
                    if ha is not None:
                        for g in range(NKT // 2 + 1, QT // 2):
                            pair(ha, None, g)
                if b_end and hb is not None:
                    b_end(hb)
                if a_end and ha is not None:
                    a_end(ha)

            head(0, None)
            with eng.Fori(0, H - 1) as h:
                head(h + 1, h)
            head(None, H - 1)

        @block.sync
        def _(sp):
            def load_a(h):
                at = bass.ds((h & (XSLOTS - 1)) * S, S)
                atk = bass.ds((h & (XSLOTS - 1)) * S, NCTX)
                rows = bass.ds(h * XH, XH)
                sp.dma_start(qa[0:XH, at], G.wide_q_parts[0, rows, :]).then_inc(a_loaded, 16)
                sp.dma_start(qa[XH:P, at], G.wide_q_parts[1, rows, :]).then_inc(a_loaded, 16)
                sp.dma_start(kh[0:XH, atk], G.wide_k_parts[0, rows, 0:NCTX]).then_inc(a_loaded, 16)
                sp.dma_start(kh[XH:P, atk], G.wide_k_parts[0, rows, 0:NCTX]).then_inc(a_loaded, 16)
                sp.dma_start(km[0:XH, atk], G.wide_k_parts[1, rows, 0:NCTX]).then_inc(a_loaded, 16)
                hold(sp, (a_loaded, A_LOADS * (h + 1)))

            def load_b(h):
                slot = h & (XSLOTS - 1)
                rows = bass.ds(h * XH, XH)
                sp.dma_start(k32[0:XH, bass.ds(slot * NKT * P, NCTX)], G.wide_k[rows, 0:NCTX]).then_inc(b_loaded, 16)
                sp.dma_start(q32[0:XH, bass.ds(slot * S, S)], G.wide_q[rows, :]).then_inc(b_loaded, 16)
                hold(sp, (b_loaded, B_LOADS * (h + 1)))

            def stats(h):
                hold(sp, (st_out, h + 1))
                slot = h & (XSLOTS - 1)
                sp.dma_start(q32[X_SHIFT:X_SHIFT + 1, bass.ds(slot * S, S)], statT[0:QT]).then_inc(st_loaded, 16)
                hold(sp, (st_loaded, 16 * (h + 1) + 16))

            sp.sem_inc(st_loaded, 16)
            sp.wait_ge(ready, READY)
            load_a(0)
            load_b(0)
            load_a(1)
            load_b(1)
            stats(0)
            with sp.Fori(1, H - 1) as h:
                hold(sp, (stats_set, h))
                load_a(h + 1)
                hold(sp, (o_formed, h))
                load_b(h + 1)
                stats(h)
            stats(H - 1)

        @block.gpsimd
        def _(pool):
            last = NCTX - (NKT - 1) * P
            steps = [(k32[:], 0.0), (k32[X_MASK:XROWS], 1.0), (q32[X_MASK:XROWS], 1.0), (km[:], 0.0),
                     (stat[:], 0.0), (O_out[:], 0.0), (part_max[:], 0.0)]
            for slot in range(XSLOTS):
                at = slot * NKT * P
                steps += [(k32[X_MASK:X_MASK + 1, at:at + NCTX], 0.0),
                          (k32[X_MASK:X_MASK + 1, at + NCTX:at + NKT * P], NEG)]
            for j, (what, value) in enumerate(steps):
                if j:
                    pool.wait_ge(ready, j)
                nc.gpsimd.memset(what, value).then_inc(ready, 1)
            pool.wait_ge(ready, len(steps))
            assert len(steps) == READY

            def step(ha, hb, g, u):
                if hb is not None:
                    i = 2 * g + u
                    m = hb * NKT + i
                    slot = hb & (XSLOTS - 1)
                    if u == 0:
                        hold(pool, (b_loaded, B_LOADS * (hb + 1)))
                    hold(pool, (pv_done, m + AHEAD - 1))
                    nc.gpsimd.tensor_copy(Kh[:, u], k32[:, bass.ds(slot * NKT * P + i * P, P)]).then_inc(k_staged, 1)
                    hold(pool, (k_staged, m + 1))
                    nc.gpsimd.tensor_copy(Vh[:, u], V[:, bass.ds(i, 1), bass.ds(hb * XH, XH)]).then_inc(v_staged, 1)
                    hold(pool, (v_staged, m + 1))

            def b_start(h):
                hold(pool, (pv_done, h * NKT + AHEAD))

            heads(pool, step, b_start=b_start)

        @block.tensor
        def _(pe):
            pe.sem_inc(pv_done, AHEAD)
            pe.wait_ge(ready, READY)

            def by_query(h, g, u):
                n = h * QT + 2 * g + u
                slot = h & (XSLOTS - 1)
                for c, (a, w) in enumerate(key_chunks):
                    hold(pe, (a_taken, NCH * n + c - 2 + 1 + AHEAD))
                    bank = sA[c % 2][:, 0:w]
                    lhs = qa[:, bass.ds(slot * S + (2 * g + u) * P, P)]
                    nc.tensor.matmul(bank, lhs, kh[:, bass.ds(slot * S + a, w)], start=True, stop=False)
                    nc.tensor.matmul(bank, lhs, km[:, bass.ds(slot * S + a, w)], start=False, stop=True).then_inc(a_formed, 1)

            def by_key(h, g, u):
                m = h * NKT + 2 * g + u
                slot = h & (XSLOTS - 1)
                hold(pe, (k_staged, m + 1))
                for c in range(QC):
                    hold(pe, (y_taken, QC * m + c - 2 + 1 + AHEAD))
                    nc.tensor.matmul(yP[c % 2][:], Kh[:, u], q32[:, bass.ds(slot * S + c * CH, CH)],
                                     start=True, stop=True).then_inc(y_formed, 1)

            def products(h, g, u):
                m = h * NKT + 2 * g + u
                hold(pe, (v_staged, m + 1), (y_taken, QC * (m + 1) + AHEAD))
                for c in range(QC):
                    half = (c % 2) * XH
                    nc.tensor.matmul(O[c // 2][half:half + XH, :], Vh[:, u], prob[:, u, c],
                                     start=False, stop=False, skip_group_check=True)
                for c in range(QC):
                    mm = nc.tensor.matmul(Den[32 * c:32 * (c + 1), :], G.ones[:, 0:32], prob[:, u, c],
                                          start=False, stop=False, skip_group_check=True)
                mm.then_inc(pv_done, 1)

            def step(ha, hb, g, u):
                if ha is not None:
                    if u == 0:
                        hold(pe, (a_loaded, A_LOADS * (ha + 1)))
                    by_query(ha, g, u)
                if hb is not None:
                    if u == 0:
                        hold(pe, (st_loaded, 16 * (hb + 1) + 16))
                    by_key(hb, g, u)
                    products(hb, g, u)

            def b_start(h):
                hold(pe, (o_taken, h + 1))
                for bank in (O[0], O[1], Den):
                    nc.tensor.matmul(bank[:], G.zerob[:, 0:P], G.zerob[:], start=True, stop=False, skip_group_check=True)

            def b_end(h):
                hold(pe, (pv_done, (h + 1) * NKT + AHEAD))
                pe.sem_inc(o_formed, 1)

            def a_end(h):
                hold(pe, (stats_set, h + 1))
                nc.tensor.transpose(turned[0:32, 0:P], stat[:], G.ident[:]).then_inc(st_turned, 1)

            heads(pe, step, a_end=a_end, b_start=b_start, b_end=b_end)

        @block.scalar
        def _(act):
            act.sem_inc(y_taken, AHEAD)
            act.sem_inc(o_taken, 1)
            act.sem_inc(o_stored, 16)
            act.wait_ge(ready, READY)

            def step(ha, hb, g, u):
                if hb is not None:
                    m = hb * NKT + 2 * g + u
                    hold(act, (pv_done, m - 1 + AHEAD))
                    for c in range(QC):
                        hold(act, (y_formed, QC * m + c + 1))
                        nc.scalar.activation(prob[:, u, c], yP[c % 2][:], ACT.Exp).then_inc(y_taken, 1)

            def b_start(h):
                hold(act, (pv_done, h * NKT + AHEAD))

            def b_end(h):
                hold(act, (o_formed, h + 1), (o_stored, 128 * h + 16))
                for b in range(2):
                    nc.scalar.activation(O_out[:, b], O[b][:], ACT.Copy)
                nc.scalar.activation(O_out[:, 2], Den[:], ACT.Copy).then_inc(o_taken, 1)
                hold(act, (o_taken, h + 2))
                for c in range(QC):
                    half = (c % 2) * XH
                    act.dma_start(G.wide_sums[bass.ds(h, 1), 0:XH, c * CH:(c + 1) * CH],
                                  O_out[half:half + XH, c // 2]).then_inc(o_stored, 16)
                    act.dma_start(G.wide_sums[bass.ds(h, 1), XH:XH + 32, c * CH:(c + 1) * CH],
                                  O_out[32 * c:32 * (c + 1), 2]).then_inc(o_stored, 16)

            heads(act, step, b_start=b_start, b_end=b_end)
            act.wait_ge(o_stored, 128 * H + 16)

        @block.vector
        def _(dve):
            dve.sem_inc(a_taken, AHEAD)
            dve.sem_inc(maxed, 1)
            dve.wait_ge(ready, READY)

            def step(ha, hb, g, u):
                if ha is not None:
                    i = 2 * g + u
                    n = ha * QT + i
                    for c, (a, w) in enumerate(key_chunks):
                        hold(dve, (a_formed, NCH * n + c + 1))
                        nc.vector.tensor_reduce(part_max[:, u, c:c + 1], sA[c % 2][:, 0:w], AX.X, ALU.max).then_inc(a_taken, 1)
                    hold(dve, (a_taken, NCH * (n + 1) + AHEAD))
                    nc.vector.tensor_reduce(stat[:, bass.ds(i, 1)], part_max[:, u], AX.X, ALU.max,
                                            negate=True).then_inc(maxed, 1)
                    hold(dve, (maxed, n + 2))

            def a_end(h):
                dve.sem_inc(stats_set, 1)
                hold(dve, (st_turned, h + 1), (st_loaded, 16 * h + 16))
                nc.vector.tensor_copy(statT[:], turned[0:32, 0:P]).then_inc(st_out, 1)
                hold(dve, (st_out, h + 1))

            heads(dve, step, a_end=a_end)


def finish_wide(nc, G, A):
    with ExitStack() as stack:
        s = Scope(nc, stack, "l1xf")
        w = s.sb("w", [P, XC, D])
        bias, gate = s.sb("bias", [1, D]), s.sb("gate", [1, 1])
        tgate = s.sb("tgate", [P, 1])
        num, den = s.sb("num", [P, XC, S]), s.sb("den", [P, 2, S])
        banks = [s.ps(f"bank{b}", [P, CH]) for b in range(4)]
        gate_bank = s.ps("gate_bank", [P, CH])
        w_loaded, inv, normed, gated, gate_ready, formed, added = (s.sem(x) for x in (
            "w_loaded", "inv", "normed", "gated", "gate_ready", "formed", "added"))
        loaded = [s.sem(f"loaded{b}") for b in range(2)]
        block = stack.enter_context(nc.Block())

        @block.sync
        def _(sp):
            sp.dma_start(w[:], A["L1_xattn_w_out"].rearrange("(c p) d -> p c d", p=P)).then_inc(w_loaded, 16)
            sp.dma_start(bias[:], A["L1_xattn_b_out"].rearrange("(o n) -> o n", o=1)).then_inc(w_loaded, 16)
            sp.dma_start(gate[:], A["L1_xattn_gate"].rearrange("(o n) -> o n", o=1)).then_inc(w_loaded, 16)
            for c in range(XC):
                if c >= 2:
                    sp.wait_ge(normed, c - 1)
                for j in range(2):
                    h = 2 * c + j
                    sp.dma_start(num[j * XH:(j + 1) * XH, c], G.wide_sums[h, 0:XH]).then_inc(loaded[c % 2], 16)
                    for r in range(2):
                        sp.dma_start(den[j * XH + 32 * r:j * XH + 32 * (r + 1), c % 2],
                                     G.wide_sums[h, XH:XH + 32]).then_inc(loaded[c % 2], 16)

        @block.tensor
        def _(pe):
            pe.wait_ge(w_loaded, 48)
            nc.tensor.matmul(gate_bank[:, 0:1], G.ones[0:1, 0:P], gate[:], start=True, stop=True).then_inc(gated, 1)
            pe.wait_ge(normed, XC)
            for t in range(QT):
                if t >= 4:
                    pe.wait_ge(added, t - 3)
                bank = banks[t % 4][:, 0:D]
                for c in range(XC):
                    nc.tensor.matmul(bank, num[:, c, t * P:(t + 1) * P], w[:, c], start=(c == 0), stop=False)
                nc.tensor.matmul(bank, G.ones[0:1, 0:P], bias[:], start=False, stop=True).then_inc(formed, 1)

        @block.scalar
        def _(act):
            act.wait_ge(gated, 1)
            nc.scalar.activation(tgate[:], gate_bank[:, 0:1], ACT.Tanh).then_inc(gate_ready, 1)

        @block.vector
        def _(dve):
            for c in range(XC):
                dve.wait_ge(loaded[c % 2], 6 * 16 * (c // 2 + 1))
                nc.vector.reciprocal(den[:, c % 2], den[:, c % 2]).then_inc(inv, 1)
                dve.wait_ge(inv, c + 1)
                nc.vector.tensor_tensor(num[:, c], num[:, c], den[:, c % 2], ALU.mult).then_inc(normed, 1)
            dve.wait_ge(gate_ready, 1)
            for t in range(QT):
                dve.wait_ge(formed, t + 1)
                nc.vector.scalar_tensor_tensor(out=G.x_tok[:, t], in0=banks[t % 4][:, 0:D], scalar=tgate[:],
                                               in1=G.x_tok[:, t], op0=ALU.mult, op1=ALU.add).then_inc(added, 1)


FP8_MAX = 448.0


def fp8_linear(nc, G, A):
    with ExitStack() as stack:
        s = Scope(nc, stack, "fp8")
        code = s.sb("code", [P, KC * D], U8)
        bits, field = s.sb("bits", [P, KC * D], I32), s.sb("field", [P, 3, KC * D], I32)
        fieldf = s.sb("fieldf", [P, 3, KC * D])
        power = s.sb("power", [P, KC * D], I32)
        weight = s.sb("weight", [P, KC, D])
        wT = s.sb("wT", [P, KC, D], BF16)
        row = s.sb("row", [1, D + 1])
        spread = s.sb("spread", [P, D + 1])
        amax, scale, inv_scale, out_scale = (s.sb(x, [P, QT]) for x in ("amax", "scale", "inv_scale", "out_scale"))
        y, magic = s.sb("y", [P, QT * D]), s.sb("magic", [P, QT * D])
        qT = s.sb("qT", [P, KC, S], BF16)
        banks = [s.ps(f"bank{b}", [P, CH]) for b in range(2)]
        out_banks = [s.ps(f"out{b}", [P, CH]) for b in range(4)]
        row_bank = s.ps("row_bank", [P, CH])
        (loaded, step, w_set, turned, taken, spread_formed, spread_set, quant, formed, added, based) = (
            s.sem(x) for x in ("loaded", "step", "w_set", "turned", "taken", "spread_formed", "spread_set",
                               "quant", "formed", "added", "based"))
        jobs = [(c, g) for g in range(0, QT, 4) for c in range(KC)]
        block = stack.enter_context(nc.Block())

        @block.sync
        def _(sp):
            sp.dma_start(code[:].rearrange("p (c n) -> p c n", c=KC),
                         A["L1_ffn_weight"].bitcast(U8).rearrange("(c p) n -> p c n", p=P)).then_inc(loaded, 16)
            sp.dma_start(row[:, 0:D], A["L1_ffn_bias"].rearrange("(o n) -> o n", o=1)).then_inc(loaded, 16)
            sp.dma_start(row[:, D:D + 1], A["L1_ffn_weight_scale"].rearrange("(o n) -> o n", o=1)).then_inc(loaded, 16)

        @block.tensor
        def _(pe):
            pe.wait_ge(loaded, 48)
            nc.tensor.matmul(row_bank[:, 0:D + 1], G.ones[0:1, 0:P], row[:], start=True, stop=True).then_inc(spread_formed, 1)
            pe.wait_ge(w_set, 1)
            for ic in range(KC):
                for oc in range(KC):
                    mm = nc.tensor.transpose(banks[0][:, ic * D + oc * P:ic * D + (oc + 1) * P],
                                             weight[:, oc, ic * P:(ic + 1) * P], G.ident[:])
            mm.then_inc(turned, 1)
            for j, (c, g) in enumerate(jobs):
                pe.wait_ge(quant, 1)
                if j:
                    pe.wait_ge(taken, j)
                for k in range(4):
                    at = (g + k) * D + c * P
                    mm = nc.tensor.transpose(banks[(j + 1) % 2][:, k * P:(k + 1) * P], y[:, at:at + P], G.ident[:])
                mm.then_inc(turned, 1)
            pe.wait_ge(taken, len(jobs) + 1)
            for t in range(QT):
                if t >= 4:
                    pe.wait_ge(added, t - 3)
                for c in range(KC):
                    mm = nc.tensor.matmul(out_banks[t % 4][:, 0:D], qT[:, c, t * P:(t + 1) * P], wT[:, c],
                                          start=(c == 0), stop=(c == KC - 1))
                mm.then_inc(formed, 1)

        @block.scalar
        def _(act):
            act.wait_ge(spread_formed, 1)
            nc.scalar.activation(spread[:], row_bank[:, 0:D + 1], ACT.Copy).then_inc(spread_set, 1)
            act.wait_ge(turned, 1)
            nc.scalar.activation(wT[:], banks[0][:].rearrange("p (c d) -> p c d", c=KC), ACT.Copy).then_inc(taken, 1)
            for j, (c, g) in enumerate(jobs):
                act.wait_ge(turned, j + 2)
                nc.scalar.activation(qT[:, c, g * P:(g + 4) * P], banks[(j + 1) % 2][:], ACT.Copy).then_inc(taken, 1)

        @block.vector
        def _(dve):
            count = [0]

            def then(ins):
                count[0] += 1
                ins.then_inc(step, 1)
                dve.wait_ge(step, count[0])

            dve.wait_ge(loaded, 48)
            then(nc.vector.tensor_copy(bits[:], code[:]))
            then(nc.vector.tensor_scalar(field[:, 0], bits[:], 7, None, ALU.logical_shift_right))
            then(nc.vector.tensor_scalar(field[:, 1], bits[:], 3, 15, ALU.logical_shift_right, ALU.bitwise_and))
            then(nc.vector.tensor_scalar(field[:, 2], bits[:], 7, None, ALU.bitwise_and))
            then(nc.vector.tensor_copy(fieldf[:], field[:]))
            sign, expo, mant = (fieldf[:, j] for j in range(3))
            flat = weight[:].rearrange("p c d -> p (c d)")
            then(nc.vector.tensor_scalar(flat, expo, 0.0, 8.0, ALU.is_gt, ALU.mult))
            then(nc.vector.tensor_tensor(flat, flat, mant, ALU.add))
            then(nc.vector.tensor_scalar(expo, expo, 1.0, 117.0, ALU.max, ALU.add))
            then(nc.vector.tensor_copy(power[:], expo))
            then(nc.vector.tensor_scalar(power[:], power[:], 23, None, ALU.logical_shift_left))
            then(nc.vector.tensor_tensor(flat, flat, power[:].bitcast(F32), ALU.mult))
            then(nc.vector.tensor_scalar(sign, sign, -2.0, 1.0, ALU.mult, ALU.add))
            nc.vector.tensor_tensor(flat, flat, sign, ALU.mult).then_inc(w_set, 1)
            for t in range(QT):
                mx = nc.vector.tensor_reduce(amax[:, t:t + 1], G.x_tok[:, t], AX.X, ALU.max, apply_absolute_value=True)
            then(mx)
            then(nc.vector.tensor_scalar(scale[:], amax[:], 1e-12, 1.0 / FP8_MAX, ALU.max, ALU.mult))
            then(nc.vector.reciprocal(inv_scale[:], scale[:]))
            dve.wait_ge(spread_set, 1)
            for t in range(QT):
                ins = nc.vector.tensor_scalar(y[:, t * D:(t + 1) * D], G.x_tok[:, t], inv_scale[:, t:t + 1], None, ALU.mult)
            then(ins)
            then(nc.vector.tensor_scalar(out_scale[:], scale[:], spread[:, D:D + 1], None, ALU.mult))
            for t in range(QT):
                ins = nc.vector.tensor_tensor(G.x_tok[:, t], G.x_tok[:, t], spread[:, 0:D], ALU.add)
            then(ins)
            then(nc.vector.tensor_scalar(magic[:].bitcast(I32), y[:].bitcast(I32), 0x7F800000, None, ALU.bitwise_and))
            then(nc.vector.tensor_scalar(magic[:], magic[:], 2.0 ** -6, 1.5 * 2.0 ** 20, ALU.max, ALU.mult))
            then(nc.vector.tensor_tensor(y[:], y[:], magic[:], ALU.add))
            nc.vector.tensor_tensor(y[:], y[:], magic[:], ALU.subtract).then_inc(quant, 1)
            for t in range(QT):
                dve.wait_ge(formed, t + 1)
                nc.vector.scalar_tensor_tensor(out=G.x_tok[:, t], in0=out_banks[t % 4][:, 0:D],
                                               scalar=out_scale[:, t:t + 1], in1=G.x_tok[:, t],
                                               op0=ALU.mult, op1=ALU.add).then_inc(added, 1)


class Resident:
    pass


def decoder(nc, A, out, stages=99):
    G = Resident()
    with ExitStack() as stack:
        s = Scope(nc, stack, "keep")
        G.x_tok = s.sb("x_tok", [P, QT, D])
        G.xT = s.sb("xT", [P, KC, S])
        G.ctxT = s.sb("ctxT", [P, KC, NCTX])
        G.ident = s.sb("ident", [P, P])
        G.identb = s.sb("identb", [P, P], BF16)
        G.band = s.sb("band", [P, 2, 3 * P + CH], BF16)
        G.ones = s.sb("ones", [P, CH])
        G.zerob = s.sb("zerob", [P, CH], BF16)
        G.mask_row = s.sb("mask_row", [1, S], BF16)
        G.q_parts = nc.dram_tensor("q_parts", (3, D, S), BF16, kind="Internal").ap()
        G.k_parts = nc.dram_tensor("k_parts", (3, D, S), BF16, kind="Internal").ap()
        G.wide_q = nc.dram_tensor("wide_q", (XI, S), F32, kind="Internal").ap()
        G.wide_k = nc.dram_tensor("wide_k", (XI, S), F32, kind="Internal").ap()
        G.wide_q_parts = nc.dram_tensor("wide_q_parts", (2, XI, S), BF16, kind="Internal").ap()
        G.wide_k_parts = nc.dram_tensor("wide_k_parts", (2, XI, S), BF16, kind="Internal").ap()
        G.wide_sums = nc.dram_tensor("wide_sums", (H, XH + 32, S), F32, kind="Internal").ap()
        G.sums = nc.dram_tensor("sums", (H, 2 * DH, S), F32, kind="Internal").ap()

        load_inputs(nc, G, A)
        with ExitStack() as layer:
            V = Scope(nc, layer, "l0a").sb("v", [P, QT, H, 2 * DH])
            w, b = A["L0_attn_w_qkv"], A["L0_attn_b_qkv"].rearrange("(o n) -> o n", o=1)
            project(nc, G, A, "l0ap", G.xT, S, w[0:D], w[D:2 * D], w[2 * D:3 * D],
                    b[:, 0:D], b[:, D:2 * D], b[:, 2 * D:3 * D], True, None, V)
            attend_causal(nc, G, "l0ac", V)
        row = lambda name: A[name].rearrange("(o n) -> o n", o=1)
        finish(nc, G, A, "l0af", A["L0_attn_w_out"], row("L0_attn_b_out"), 1e-8)
        if stages > 1:
            with ExitStack() as layer:
                V = Scope(nc, layer, "l0x").sb("v", [P, len(tiles_of(NCTX)), H, 2 * DH])
                project(nc, G, A, "l0xp", G.ctxT, NCTX, A["L0_xattn_wq_w"], A["L0_xattn_wk_w"],
                        A["L0_xattn_wv_w"], row("L0_xattn_wq_b"), row("L0_xattn_wk_b"),
                        row("L0_xattn_wv_b"), False, A["mask_BxS2_bf1"], V)
                attend_top(nc, G, "l0xc", NCTX, V)
            finish(nc, G, A, "l0xf", A["L0_xattn_wo_w"], row("L0_xattn_wo_b"), None)
        if stages > 2:
            with ExitStack() as layer:
                M = Resident()
                keep = Scope(nc, layer, "moek")
                M.tT = keep.sb("tT", [P, KC, S])
                M.w = keep.sb("w", [P, QT, EXPERTS])
                M.b_glu = keep.sb("b_glu", [P, 4 * EXPERTS])
                M.b_lin = keep.sb("b_lin", [P, 4 * EXPERTS])
                moe_gate(nc, G, A, M)
                moe_experts(nc, G, A, M)
            layer_norm(nc, G, A, "l0n")
        if stages > 3:
            with ExitStack() as layer:
                V = Scope(nc, layer, "l1a").sb("v", [P, QT, H, 2 * DH])
                project(nc, G, A, "l1ap", G.xT, S, A["L1_attn_Wq"], A["L1_attn_Wk"], A["L1_attn_Wv"],
                        row("L1_attn_bq"), row("L1_attn_bk"), row("L1_attn_bv"), False, None, V)
                attend_top(nc, G, "l1ac", S, V)
            finish(nc, G, A, "l1af", A["L1_attn_Wo"], row("L1_attn_bo"), None)
        if stages > 4:
            with ExitStack() as layer:
                V = Scope(nc, layer, "l1x").sb("v", [P, len(tiles_of(NCTX)), XI])
                with ExitStack() as inner:
                    G.xn = Scope(nc, inner, "l1xn").sb("xn", [P, KC, S])
                    layer_norm(nc, G, A, "l1xl", affine=(A["L1_xattn_ln_gamma"], A["L1_xattn_ln_beta"]))
                    project_wide(nc, G, A, V)
                attend_wide(nc, G, V)
            finish_wide(nc, G, A)
            layer_norm(nc, G, A, "l1xm")
        if stages > 5:
            fp8_linear(nc, G, A)
        layer_norm(nc, G, A, "last", out)


_INS = ['x', 'ctx_1024', 'mask_BxS2_bf1', 'L0_attn_w_qkv', 'L0_attn_b_qkv', 'L0_attn_w_out', 'L0_attn_b_out',
        'L0_xattn_wq_w', 'L0_xattn_wq_b', 'L0_xattn_wk_w', 'L0_xattn_wk_b', 'L0_xattn_wv_w', 'L0_xattn_wv_b',
        'L0_xattn_wo_w', 'L0_xattn_wo_b', 'L0_ffn_norm_scale', 'L0_ffn_gate_w', 'L0_ffn_gate_b',
        'L0_ffn_mlp1_w', 'L0_ffn_mlp1_b', 'L0_ffn_mlp2_w', 'L0_ffn_mlp2_b', 'L1_attn_Wq', 'L1_attn_bq',
        'L1_attn_Wk', 'L1_attn_bk', 'L1_attn_Wv', 'L1_attn_bv', 'L1_attn_Wo', 'L1_attn_bo',
        'L1_xattn_ln_gamma', 'L1_xattn_ln_beta', 'L1_xattn_w_q', 'L1_xattn_w_kv', 'L1_xattn_w_out',
        'L1_xattn_b_out', 'L1_xattn_gate', 'L1_ffn_weight', 'L1_ffn_weight_scale', 'L1_ffn_bias']
_OUTS = [((1, S, D), 'float32')]


def shape_constants():
    import numpy as np
    p = np.arange(P)[:, None]
    z = np.arange(3 * P + CH)[None, :] - 3 * P
    band = np.stack([np.where(z > p, NEG, 0.0), np.where(z < p, NEG, 0.0)], 1).astype(np.float32)
    freq = (np.float32(10000.0) ** (-np.arange(0, DH, 2, dtype=np.float32) / np.float32(DH))).astype(np.float32)
    angle = np.arange(S, dtype=np.float32)[None, :] * np.repeat(freq, 2)[:, None]
    rope = np.stack([np.cos(angle), np.sin(angle)]).astype(np.float32)
    experts = np.broadcast_to(np.arange(8, dtype=np.float32), (P, 8))
    return {"const_ident": np.eye(P, dtype=np.float32), "const_band": band, "const_rope": rope,
            "const_experts": np.ascontiguousarray(experts)}


def kernel(**inputs):
    import numpy as _np
    import concourse.bacc as _bacc
    from concourse import mybir as _mybir
    from concourse.bass_utils import run_bass_kernel_spmd as _run

    nc = _bacc.Bacc("TRN2", target_bir_lowering=False, num_devices=1)
    arrays, args = {}, {}
    for name, a in [(n, inputs[n]) for n in _INS] + list(shape_constants().items()):
        a = _np.ascontiguousarray(a)
        a = a.reshape(a.shape or (1,))
        arrays[f"in_{name}_dram"] = a
        args[name] = nc.dram_tensor(f"in_{name}_dram", a.shape, _mybir.dt.from_np(a.dtype), kind="ExternalInput").ap()
    (shape, dtype), = _OUTS
    out = nc.dram_tensor("out_0_dram", shape, _mybir.dt.from_np(_np.dtype(dtype)), kind="ExternalOutput").ap()
    decoder(nc, args, out)
    r = _run(nc, [arrays], core_ids=[0])
    return r.results[0]["out_0_dram"]
```

```python
from contextlib import ExitStack

import concourse.bass as bass
from concourse import mybir

ALU = mybir.AluOpType
ACT = mybir.ActivationFunctionType
AX = mybir.AxisListType
F32 = mybir.dt.float32
BF16 = mybir.dt.bfloat16
I32 = mybir.dt.int32
U32 = mybir.dt.uint32
U8 = mybir.dt.uint8
RMAX = bass.bass_isa.ReduceOp.max

P = 128
D = 256
KC = D // P
S = 2048
NCTX = 1601
QT = S // P
CH = 512
QC = S // CH
H = 16
DH = D // H
TOPK = 64
NEG = -1.0e18
SPLITS = ((0, 0), (0, 1), (0, 2), (1, 0), (1, 1), (2, 0))
STACK = DH * len(SPLITS)
MASK_ROW = STACK
SHIFT_ROW = STACK + 1
ROWS = STACK + 4
STEEP = 1.0e20
SLOTS = 4
EPS = 1e-5


def tiles_of(n, size=P):
    return [(a, min(size, n - a)) for a in range(0, n, size)]


class Scope:

    def __init__(self, nc, stack, tag):
        self.nc, self.stack, self.tag, self.sems = nc, stack, tag, []
        stack.callback(self.clear)

    def sb(self, name, shape, dt=F32):
        return self.stack.enter_context(self.nc.sbuf_tensor(f"{self.tag}_{name}", shape, dt))

    def ps(self, name, shape):
        return self.stack.enter_context(self.nc.psum_tensor(f"{self.tag}_{name}", shape, F32))

    def sem(self, name):
        self.sems.append(self.nc.alloc_semaphore(f"{self.tag}_{name}"))
        return self.sems[-1]

    def clear(self):
        if self.sems:
            self.nc.clear_and_free_semaphores(self.sems)
            self.nc.all_engine_barrier()


def load_inputs(nc, G, A):
    with ExitStack() as stack:
        s = Scope(nc, stack, "load")
        ctx_tok = s.sb("ctx_tok", [P, len(tiles_of(NCTX)), D])
        bandf = s.sb("bandf", [P, 2, G.band.shape[2]])
        turned = [s.ps(f"turned{b}", [P, CH]) for b in range(2)]
        loaded, turns, evacs, ready = s.sem("loaded"), s.sem("turns"), s.sem("evacs"), s.sem("ready")
        ct = tiles_of(NCTX)
        jobs = []
        for c in range(KC):
            for g in range(0, QT, 4):
                jobs.append(([(G.x_tok[:, t, c * P:(c + 1) * P], P) for t in range(g, g + 4)],
                             G.xT, c, g * P))
            for g in range(0, len(ct), 4):
                jobs.append(([(ctx_tok[0:n, t, c * P:(c + 1) * P], n)
                              for t, (_, n) in list(enumerate(ct))[g:g + 4]], G.ctxT, c, g * P))
        block = stack.enter_context(nc.Block())
        full = NCTX // P

        @block.sync
        def _(sp):
            sp.dma_start(G.ident[:], A["const_ident"]).then_inc(loaded, 16)
            sp.dma_start(G.x_tok[:], A["x"][0].rearrange("(t p) d -> p t d", p=P)).then_inc(loaded, 16)
            sp.dma_start(ctx_tok[:, 0:full, :],
                         A["ctx_1024"][0, 0:full * P].rearrange("(t p) d -> p t d", p=P)).then_inc(loaded, 16)
            sp.dma_start(ctx_tok[0:NCTX - full * P, full, :], A["ctx_1024"][0, full * P:NCTX]).then_inc(loaded, 16)
            sp.dma_start(bandf[:], A["const_band"]).then_inc(loaded, 16)

        @block.gpsimd
        def _(pool):
            nc.gpsimd.memset(G.ones[:], 1.0).then_inc(ready, 1)
            nc.gpsimd.memset(G.zerob[:], 0.0).then_inc(ready, 1)

        @block.tensor
        def _(pe):
            pe.wait_ge(loaded, 5 * 16)
            for j, (srcs, _, _, _) in enumerate(jobs):
                if j >= 2:
                    pe.wait_ge(evacs, j - 1)
                at = 0
                for src, n in srcs:
                    mm = nc.tensor.transpose(turned[j % 2][:, at:at + n], src, G.ident[0:n, 0:n])
                    at += n
                mm.then_inc(turns, 1)

        @block.scalar
        def _(act):
            for j, (srcs, dst, c, at) in enumerate(jobs):
                act.wait_ge(turns, j + 1)
                n = sum(k for _, k in srcs)
                nc.scalar.activation(dst[:, c, at:at + n], turned[j % 2][:, 0:n], ACT.Copy).then_inc(evacs, 1)

        @block.vector
        def _(dve):
            dve.wait_ge(loaded, 5 * 16)
            nc.vector.tensor_copy(G.identb[:], G.ident[:]).then_inc(ready, 1)
            nc.vector.tensor_copy(G.band[:], bandf[:]).then_inc(ready, 1)


def project(nc, G, A, tag, srcT, nk, wq, wk, wv, bq, bk, bv, rope, mask, V):
    kt = tiles_of(nk)
    with ExitStack() as stack:
        s = Scope(nc, stack, tag)
        w_rows = s.sb("w_rows", [P, 3, KC, D])
        wT = s.sb("wT", [P, 3, KC, D])
        bias = s.sb("bias", [1, 3, D])
        if rope:
            wR = s.sb("wR", [P, 2, KC, D])
            biasR = s.sb("biasR", [1, 2, D])
            cos, sin = s.sb("cos", [P, S]), s.sb("sin", [P, S])
            part = s.sb("part", [P, 2, CH])
        full = s.sb("full", [P, 2, S])
        rest = s.sb("rest", [P, S])
        parts = s.sb("parts", [P, 2, 3, S], BF16)
        maskf = s.sb("maskf", [1, S])
        maskb = s.sb("maskb", [1, S], U8)
        banks = [s.ps(f"bank{b}", [P, CH]) for b in range(4)]
        vbanks = [s.ps(f"vbank{b}", [P, CH]) for b in range(2)]
        loaded, turned, w_ready = s.sem("loaded"), s.sem("turned"), s.sem("w_ready")
        formed, taken, v_formed, v_taken, split, rest_done, stored, masked, v_clear = (
            s.sem(x) for x in ("formed", "taken", "v_formed", "v_taken", "split", "rest_done",
                               "stored0", "masked", "v_clear"))
        stored = [stored, s.sem("stored1")]
        roped, r_chain = s.sem("roped"), s.sem("r_chain")
        n_loads = 6 + (16 if rope else 0) + (1 if mask is not None else 0)
        units = [(w, oc) for w in range(2) for oc in range(KC)]
        chunks = [tiles_of(S, CH) if w == 0 else tiles_of(nk, CH) for w, _ in units]
        src = [G.xT, srcT]
        W_STEPS = 4 if rope else 1
        n_w = 3 + (2 * 2 if rope else 0) + (4 if rope else 0)
        per = 2 if rope else 1
        order = [(u, c) for u in range(len(units)) for c in range(len(chunks[u]))]
        ends = [sum(len(x) for x in chunks[:u + 1]) for u in range(len(units))]
        block = stack.enter_context(nc.Block())

        @block.sync
        def _(sp):
            for i, (w, b) in enumerate(((wq, bq), (wk, bk), (wv, bv))):
                sp.dma_start(w_rows[:, i], w.rearrange("(c p) d -> p c d", p=P)).then_inc(loaded, 16)
                sp.dma_start(bias[:, i], b).then_inc(loaded, 16)
            if rope:
                for g in range(P // DH):
                    sp.dma_start(cos[g * DH:(g + 1) * DH], A["const_rope"][0]).then_inc(loaded, 16)
                    sp.dma_start(sin[g * DH:(g + 1) * DH], A["const_rope"][1]).then_inc(loaded, 16)
            if mask is not None:
                sp.dma_start(maskb[:, 0:nk], mask.bitcast(U8)).then_inc(loaded, 16)
            for u, (w, oc) in enumerate(units):
                n = S if w == 0 else nk
                sp.wait_ge(split, 3 * (u + 1))
                dst = G.q_parts if w == 0 else G.k_parts
                for j in range(3):
                    sp.dma_start(dst[j, oc * P:(oc + 1) * P, 0:n], parts[:, u % 2, j, 0:n]).then_inc(stored[u % 2], 16)
            for u in range(2):
                sp.wait_ge(stored[u], 3 * 16 * len(units) // 2)

        @block.gpsimd
        def _(pool):
            last = len(kt) - 1
            nc.gpsimd.memset(V[:, last], 0.0).then_inc(v_clear, 1)
            pool.wait_ge(v_clear, 1)
            nc.gpsimd.memset(V[:, 0:last, :, DH:2 * DH], 1.0).then_inc(v_clear, 1)
            pool.wait_ge(v_clear, 2)
            nc.gpsimd.memset(V[0:kt[-1][1], last, :, DH:2 * DH], 1.0).then_inc(v_clear, 1)
            pool.wait_ge(v_clear, 3)
            nc.gpsimd.memset(maskf[:], NEG if mask is not None else 0.0).then_inc(v_clear, 1)

        @block.tensor
        def _(pe):
            pe.wait_ge(loaded, n_loads * 16)
            for i in range(3):
                if i == 2:
                    pe.wait_ge(w_ready, W_STEPS)
                for ic in range(KC):
                    for oc in range(KC):
                        mm = nc.tensor.transpose(banks[i % 2][:, ic * D + oc * P:ic * D + (oc + 1) * P],
                                                 w_rows[:, i, oc, ic * P:(ic + 1) * P], G.ident[:])
                mm.then_inc(turned, 1)
            pe.wait_ge(w_ready, n_w)
            for n, (u, c) in enumerate(order):
                w, oc = units[u]
                a, m = chunks[u][c]
                if n >= 4 // per:
                    pe.wait_ge(taken, n - 4 // per + 1)
                for r in range(per):
                    bank = banks[(n * per + r) % 4]
                    wt, bt = (wT, bias) if r == 0 else (wR, biasR)
                    for ic in range(KC):
                        nc.tensor.matmul(bank[:, 0:m], wt[:, w, ic, oc * P:(oc + 1) * P],
                                         src[w][:, ic, a:a + m], start=(ic == 0), stop=False)
                    mm = nc.tensor.matmul(bank[:, 0:m], bt[:, w, oc * P:(oc + 1) * P], G.ones[0:1, 0:m],
                                          start=False, stop=True)
                mm.then_inc(formed, 1)
            for t, (a, m) in enumerate(kt):
                if t >= 2:
                    pe.wait_ge(v_taken, t - 1)
                for ic in range(KC):
                    nc.tensor.matmul(vbanks[t % 2][0:m, 0:D], srcT[:, ic, a:a + m], wT[:, 2, ic, :],
                                     start=(ic == 0), stop=False)
                nc.tensor.matmul(vbanks[t % 2][0:m, 0:D], G.ones[0:1, 0:m], bias[:, 2, :],
                                 start=False, stop=True).then_inc(v_formed, 1)

        @block.scalar
        def _(act):
            for i in range(3):
                act.wait_ge(turned, i + 1)
                bank = banks[i % 2][:].rearrange("p (c d) -> p c d", c=KC)
                nc.scalar.activation(wT[:, i], bank, ACT.Copy).then_inc(w_ready, 1)
                if rope and i < 2:
                    pair = bank.rearrange("p c (f two) -> p c f two", two=2)
                    out = wR[:, i].rearrange("p c (f two) -> p c f two", two=2)
                    nc.scalar.activation(out[:, :, :, 0], pair[:, :, :, 1], ACT.Copy, scale=-1.0).then_inc(w_ready, 1)
                    nc.scalar.activation(out[:, :, :, 1], pair[:, :, :, 0], ACT.Copy).then_inc(w_ready, 1)
                    if i == 0:
                        act.wait_ge(loaded, n_loads * 16)
                    bp = bias[:, i].rearrange("p (f two) -> p f two", two=2)
                    bo = biasR[:, i].rearrange("p (f two) -> p f two", two=2)
                    nc.scalar.activation(bo[:, :, 0], bp[:, :, 1], ACT.Copy, scale=-1.0).then_inc(w_ready, 1)
                    nc.scalar.activation(bo[:, :, 1], bp[:, :, 0], ACT.Copy).then_inc(w_ready, 1)
            for u, (w, oc) in enumerate(units):
                n = S if w == 0 else nk
                if not rope:
                    if u >= 2:
                        act.wait_ge(rest_done, 2 * (u - 1))
                    for c, (a, m) in enumerate(chunks[u]):
                        at = (ends[u - 1] if u else 0) + c
                        act.wait_ge(formed, at + 1)
                        nc.scalar.activation(full[:, u % 2, a:a + m], banks[at % 4][:, 0:m], ACT.Copy,
                                             scale=0.25 if w == 0 else 1.0).then_inc(taken, 1)
                    act.wait_ge(taken, ends[u])
                else:
                    act.wait_ge(roped, ends[u])
                if u >= 2:
                    act.wait_ge(stored[u % 2], 3 * 16 * (u // 2))
                nc.scalar.activation(parts[:, u % 2, 0, 0:n], full[:, u % 2, 0:n], ACT.Copy).then_inc(split, 1)
                act.wait_ge(rest_done, 2 * u + 1)
                nc.scalar.activation(parts[:, u % 2, 1, 0:n], rest[:, 0:n], ACT.Copy).then_inc(split, 1)
                act.wait_ge(rest_done, 2 * u + 2)
                nc.scalar.activation(parts[:, u % 2, 2, 0:n], rest[:, 0:n], ACT.Copy).then_inc(split, 1)
            act.wait_ge(v_clear, 4)
            for t, (a, m) in enumerate(kt):
                act.wait_ge(v_formed, t + 1)
                nc.scalar.activation(V[0:m, t, :, 0:DH],
                                     vbanks[t % 2][0:m, 0:D].rearrange("p (h d) -> p h d", h=H),
                                     ACT.Copy).then_inc(v_taken, 1)

        @block.vector
        def _(dve):
            if rope:
                dve.wait_ge(loaded, n_loads * 16)
            for u, (w, oc) in enumerate(units):
                n = S if w == 0 else nk
                if rope:
                    scale = 0.25 if w == 0 else 1.0
                    for c, (a, m) in enumerate(chunks[u]):
                        at = (ends[u - 1] if u else 0) + c
                        dve.wait_ge(formed, at + 1)
                        if at:
                            dve.wait_ge(roped, at)
                        nc.vector.scalar_tensor_tensor(out=part[:, 0, 0:m], in0=banks[(2 * at) % 4][:, 0:m],
                                                       scalar=scale, in1=cos[:, a:a + m], op0=ALU.mult,
                                                       op1=ALU.mult).then_inc(r_chain, 1)
                        nc.vector.scalar_tensor_tensor(out=part[:, 1, 0:m], in0=banks[(2 * at + 1) % 4][:, 0:m],
                                                       scalar=scale, in1=sin[:, a:a + m], op0=ALU.mult,
                                                       op1=ALU.mult).then_inc(taken, 1)
                        dve.wait_ge(r_chain, at + 1)
                        dve.wait_ge(taken, at + 1)
                        nc.vector.tensor_tensor(full[:, u % 2, a:a + m], part[:, 0, 0:m], part[:, 1, 0:m],
                                                ALU.add).then_inc(roped, 1)
                dve.wait_ge(split, 3 * u + 1)
                if rope:
                    dve.wait_ge(roped, ends[u])
                nc.vector.tensor_tensor(rest[:, 0:n], full[:, u % 2, 0:n], parts[:, u % 2, 0, 0:n],
                                        ALU.subtract).then_inc(rest_done, 1)
                dve.wait_ge(split, 3 * u + 2)
                nc.vector.tensor_tensor(rest[:, 0:n], rest[:, 0:n], parts[:, u % 2, 1, 0:n],
                                        ALU.subtract).then_inc(rest_done, 1)
            dve.wait_ge(v_clear, 4)
            if mask is not None:
                dve.wait_ge(loaded, n_loads * 16)
                nc.vector.tensor_scalar(maskf[:, 0:nk], maskb[:, 0:nk], 1.0, -NEG, ALU.subtract,
                                        ALU.mult).then_inc(masked, 1)
                dve.wait_ge(masked, 1)
            nc.vector.tensor_copy(G.mask_row[:], maskf[:]).then_inc(masked, 1)


def load_head(nc, G, eng, h, nk, Kb, Qm, Qt, sem):
    slot = h & (SLOTS - 1)
    count = 0
    for j, (qp, kp) in enumerate(SPLITS):
        rows = slice(j * DH, (j + 1) * DH)
        eng.dma_start(Kb[rows, bass.ds(slot * S, nk)], G.k_parts[kp, bass.ds(h * DH, DH), 0:nk]).then_inc(sem, 16)
        count += 1
        for Q in (Qm, Qt):
            if Q is not None:
                eng.dma_start(Q[rows, bass.ds(slot * S, S)], G.q_parts[qp, bass.ds(h * DH, DH), :]).then_inc(sem, 16)
                count += 1
    return count


def attend_top(nc, G, tag, nk, V):
    kt = tiles_of(nk)
    NKT = len(kt)
    key_chunks = tiles_of(nk, CH)
    NSEG = 64
    seg_w = nk // NSEG
    segs = [(j * seg_w, seg_w if j < NSEG - 1 else nk - j * seg_w) for j in range(NSEG)]
    DEEP = 3
    ROUNDS = TOPK // 8 + 1
    G4 = QT // 4
    LAG = 3
    TAIL = NKT - (QT - LAG)
    TURN_AT = 2 if TAIL else 1
    with ExitStack() as stack:
        s = Scope(nc, stack, tag)
        Kb = s.sb("k_stack", [ROWS, SLOTS * S], BF16)
        Qm = s.sb("q_stack_max", [ROWS, SLOTS * S], BF16)
        Qt = s.sb("q_stack_cut", [ROWS, SLOTS * S], BF16)
        score = s.sb("score", [P, 4, nk])
        cand = s.sb("cand", [P, 2, NSEG + 3, 8])
        deeps = [s.sb(f"deep{b}", [P, 9]) for b in range(2)]
        eighths = [s.sb(f"eighth{b}", [P, 1]) for b in range(2)]
        tops = [s.sb(f"top{b}", [P, 8 * ROUNDS]) for b in range(2)]
        top_full = s.sb("top_full", [P, 8 * ROUNDS])
        flag, anyflag = s.sb("flag", [P, 4]), s.sb("anyflag", [P, 4])
        stat = s.sb("stat", [P, 2 * QT])
        stat_head = s.sb("stat_head", [P, 2 * QT])
        statT = s.sb("statT", [2 * QT, P])
        stat_rest = s.sb("stat_rest", [2 * QT, P])
        stat_parts = s.sb("stat_parts", [2 * QT, 3, P], BF16)
        expd = s.sb("expd", [P, 2, CH])
        chosen = s.sb("chosen", [P, 2, CH])
        prob = s.sb("prob", [P, 2, QC, CH])
        Vh = s.sb("v_head", [P, 2, 2 * DH])
        O_out = s.sb("o_out", [P, CH])
        sA = [s.ps(f"by_query{b}", [P, CH]) for b in range(2)]
        yP = [s.ps(f"less_max{b}", [P, CH]) for b in range(2)]
        xP = [s.ps(f"less_cut_ps{b}", [P, CH]) for b in range(2)]
        O = s.ps("o_sum", [P, CH])
        turned = s.ps("turned", [P, CH])
        (ready, loaded, a_formed, a_taken, s_free, y_formed, y_taken, x_formed, x_taken, weighed, staged,
         pv_done, o_formed, o_taken, o_stored, recorded, flagged, reduced, stats_set, st_turned, st_split,
         st_loaded, chose, passed) = (s.sem(x) for x in (
             "ready", "loaded", "a_formed", "a_taken", "s_free", "y_formed", "y_taken", "x_formed",
             "x_taken", "weighed", "staged", "pv_done", "o_formed", "o_taken", "o_stored", "recorded",
             "flagged", "reduced", "stats_set", "st_turned", "st_split", "st_loaded", "chose", "passed"))
        chains = [s.sem("chain0"), s.sem("chain1")]
        full_chain, turn_chain = s.sem("full_chain"), s.sem("turn_chain")
        A_AHEAD, S_AHEAD, Y_AHEAD, X_AHEAD, W_AHEAD, PV_AHEAD, O_AHEAD = 2, 4, 2, 2, 2, 2, 1
        READY = 7
        block = stack.enter_context(nc.Block())

        def hold(eng, *events):
            for sem, n in events:
                eng.wait_ge(sem, n)
            if eng in (nc.vector, nc.gpsimd, nc.sync):
                eng.sem_inc(passed, 1)

        def heads(eng, search, products, turn, b_start, b_end):
            def head(ha, hb, before):
                for u in range(LAG):
                    if ha is not None:
                        search(ha, 0, u)
                    if before is not None and u < TAIL:
                        products(before, QT - LAG + u, (QT - LAG + u) % 2)
                if before is not None:
                    b_end(before)
                turn(hb)
                b_start(hb)
                if ha is not None:
                    search(ha, 0, LAG)
                products(hb, 0, 0)
                with eng.Fori(1, G4) as g:
                    for u in range(4):
                        if ha is not None:
                            search(ha, g, u)
                        products(hb, 4 * g + (u - LAG), (u - LAG) % 2)
                if not TAIL:
                    b_end(hb)

            for u in range(4):
                search(0, 0, u)
            with eng.Fori(1, G4) as g:
                for u in range(4):
                    search(0, g, u)
            if TAIL:
                head(1, 0, None)
                with eng.Fori(1, H - 1) as h:
                    head(h + 1, h, h - 1)
                head(None, H - 1, H - 2)
                for j in range(QT - LAG, NKT):
                    products(H - 1, j, j % 2)
                b_end(H - 1)
            else:
                with eng.Fori(0, H - 1) as h:
                    head(h + 1, h, None)
                head(None, H - 1, None)

        @block.sync
        def _(sp):
            per_head = 3 * len(SPLITS) * 16

            def load(h):
                load_head(nc, G, sp, h, nk, Kb, Qm, Qt, loaded)
                hold(sp, (loaded, per_head * (h + 1) + SLOTS * 16))

            def stats(h):
                hold(sp, (st_split, h + 1))
                slot = h & (SLOTS - 1)
                for j in range(3):
                    row = slice(SHIFT_ROW + j, SHIFT_ROW + j + 1)
                    sp.dma_start(Qm[row, bass.ds(slot * S, S)], stat_parts[0:QT, j]).then_inc(st_loaded, 16)
                    sp.dma_start(Qt[row, bass.ds(slot * S, S)], stat_parts[QT:2 * QT, j]).then_inc(st_loaded, 16)
                hold(sp, (st_loaded, 96 * (h + 1) + 16))

            sp.sem_inc(st_loaded, 16)
            sp.wait_ge(ready, READY)
            for slot in range(SLOTS):
                sp.dma_start(Kb[MASK_ROW:MASK_ROW + 1, slot * S:(slot + 1) * S], G.mask_row[:]).then_inc(loaded, 16)
            for h in range(SLOTS):
                load(h)
            stats(0)
            stats(1)
            with sp.Fori(2, H - 2) as h:
                stats(h)
                hold(sp, (o_formed, h - 1))
                load(h + 2)
            stats(H - 2)
            stats(H - 1)

        @block.gpsimd
        def _(pool):
            nc.gpsimd.memset(Kb[:], 0.0).then_inc(ready, 1)
            pool.wait_ge(ready, 1)
            nc.gpsimd.memset(Kb[MASK_ROW:ROWS, :], 1.0).then_inc(ready, 1)
            pool.wait_ge(ready, 2)
            nc.gpsimd.memset(Qm[MASK_ROW:ROWS, :], 1.0).then_inc(ready, 1)
            pool.wait_ge(ready, 3)
            nc.gpsimd.memset(Qt[MASK_ROW:ROWS, :], 1.0).then_inc(ready, 1)
            pool.wait_ge(ready, 4)
            for b in range(2):
                nc.gpsimd.memset(deeps[b][:, 8:9], -3.0e38).then_inc(ready, 1)
            pool.wait_ge(ready, 6)
            nc.gpsimd.memset(O_out[:], 0.0).then_inc(ready, 1)
            pool.wait_ge(ready, READY)
            pool.sem_inc(weighed, W_AHEAD)

            def reduce(n, u):
                hold(pool, (flagged, n + 1))
                nc.gpsimd.partition_all_reduce(anyflag[:, u:u + 1], flag[:, u:u + 1], P, RMAX).then_inc(reduced, 1)

            def search(h, g, u):
                if not (isinstance(g, int) and isinstance(h, int) and h == 0) or u >= 2:
                    reduce(h * QT + 4 * g + u - 2, (u - 2) % 4)

            def products(h, j, b):
                m = h * NKT + j
                hold(pool, (pv_done, m - 2 + 1 + PV_AHEAD))
                nc.gpsimd.tensor_copy(Vh[:, b], V[:, bass.ds(j, 1), bass.ds(h, 1), :]).then_inc(staged, 1)
                for c in range(QC):
                    hold(pool, (chose, 4 * m + c + 1), (y_taken, 4 * m + c + 1 + Y_AHEAD))
                    nc.gpsimd.tensor_tensor(prob[:, b, c], expd[:, c % 2], chosen[:, c % 2],
                                            ALU.mult).then_inc(weighed, 1)

            def turn(h):
                if isinstance(h, int) and h == H - 1:
                    reduce(H * QT - 2, 2)
                    reduce(H * QT - 1, 3)

            def b_start(h):
                hold(pool, (pv_done, h * NKT + PV_AHEAD))

            heads(pool, search, products, turn, b_start, lambda h: None)

        @block.tensor
        def _(pe):
            pe.wait_ge(ready, READY)

            def search(h, g, u):
                if isinstance(g, int) and g == 0 and u == 0:
                    hold(pe, (loaded, 3 * len(SPLITS) * 16 * (h + 1) + SLOTS * 16))
                n = h * QT + 4 * g + u
                slot = h & (SLOTS - 1)
                for c, (a, w) in enumerate(key_chunks):
                    hold(pe, (a_taken, 4 * n + c - 2 + 1 + A_AHEAD))
                    nc.tensor.matmul(sA[c % 2][:, 0:w],
                                     Qt[0:SHIFT_ROW, bass.ds(slot * S + (4 * g + u) * P, P)],
                                     Kb[0:SHIFT_ROW, bass.ds(slot * S + a, w)],
                                     start=True, stop=True).then_inc(a_formed, 1)

            def by_key(h, j):
                m = h * NKT + j
                slot = h & (SLOTS - 1)
                for c in range(QC):
                    for Q, bank, formed, taken, ahead in ((Qm, yP, y_formed, y_taken, Y_AHEAD),
                                                          (Qt, xP, x_formed, x_taken, X_AHEAD)):
                        hold(pe, (taken, 4 * m + c - 2 + 1 + ahead))
                        nc.tensor.matmul(bank[c % 2][:], Kb[:, bass.ds(slot * S + j * P, P)],
                                         Q[:, bass.ds(slot * S + c * CH, CH)],
                                         start=True, stop=True).then_inc(formed, 1)

            def sums(h, j, b):
                m = h * NKT + j
                hold(pe, (staged, m + 1),
                     (weighed, 4 * (m + 1) + W_AHEAD))
                for c in range(QC):
                    mm = nc.tensor.matmul(O[32 * c:32 * (c + 1), :], Vh[:, b], prob[:, b, c],
                                          start=False, stop=False, skip_group_check=True)
                mm.then_inc(pv_done, 1)

            def products(h, j, b):
                if isinstance(j, int) and j == 0:
                    hold(pe, (st_loaded, 96 * (h + 1) + 16))
                by_key(h, j)
                if not (isinstance(j, int) and j == 0):
                    sums(h, j - 1, 1 - b)

            def turn(h):
                hold(pe, (stats_set, h + 1))
                nc.tensor.transpose(turned[0:2 * QT, 0:P], stat_head[:], G.ident[:]).then_inc(st_turned, 1)

            def b_start(h):
                hold(pe, (o_taken, h + O_AHEAD))
                nc.tensor.matmul(O[:], G.zerob[:, 0:P], G.zerob[:], start=True, stop=False, skip_group_check=True)

            def b_end(h):
                sums(h, NKT - 1, (NKT - 1) % 2)
                hold(pe, (pv_done, (h + 1) * NKT + PV_AHEAD))
                pe.sem_inc(o_formed, 1)

            pe.sem_inc(pv_done, PV_AHEAD)
            heads(pe, search, products, turn, b_start, b_end)

        @block.scalar
        def _(act):
            act.sem_inc(a_taken, A_AHEAD)
            act.sem_inc(y_taken, Y_AHEAD)
            act.sem_inc(x_taken, X_AHEAD)
            act.sem_inc(o_taken, O_AHEAD)
            act.sem_inc(o_stored, 16)
            act.wait_ge(ready, READY)

            def search(h, g, u):
                n = h * QT + 4 * g + u
                hold(act, (s_free, n - 4 + 1 + S_AHEAD))
                for c, (a, w) in enumerate(key_chunks):
                    hold(act, (a_formed, 4 * n + c + 1))
                    nc.scalar.activation(score[:, u, a:a + w], sA[c % 2][:, 0:w], ACT.Copy).then_inc(a_taken, 1)

            def products(h, j, b):
                m = h * NKT + j
                for c in range(QC):
                    hold(act, (x_formed, 4 * m + c + 1),
                         (weighed, 4 * m + c - 2 + 1 + W_AHEAD))
                    nc.scalar.activation(chosen[:, c % 2], xP[c % 2][:], ACT.Relu, scale=-STEEP).then_inc(x_taken, 1)
                    hold(act, (y_formed, 4 * m + c + 1))
                    nc.scalar.activation(expd[:, c % 2], yP[c % 2][:], ACT.Exp).then_inc(y_taken, 1)
                    hold(act, (x_taken, 4 * m + c + 1 + X_AHEAD))
                    nc.scalar.activation(chosen[:, c % 2], chosen[:, c % 2], ACT.Exp, scale=-1.0).then_inc(chose, 1)

            def b_end(h):
                hold(act, (o_formed, h + 1),
                     (o_stored, 64 * h + 16))
                nc.scalar.activation(O_out[:], O[:], ACT.Copy).then_inc(o_taken, 1)
                hold(act, (o_taken, h + 1 + O_AHEAD))
                for c in range(QC):
                    act.dma_start(G.sums[bass.ds(h, 1), :, c * CH:(c + 1) * CH],
                                  O_out[32 * c:32 * (c + 1), :]).then_inc(o_stored, 16)

            heads(act, search, products, lambda h: None, lambda h: None, b_end)
            act.wait_ge(o_stored, 64 * H + 16)

        @block.vector
        def _(dve):
            dve.sem_inc(s_free, S_AHEAD)
            dve.wait_ge(ready, READY)

            def largest(values, into, count, at, between=lambda r: None):
                for r in range(2 * ROUNDS - 1):
                    some = into[:, 8 * (r // 2):8 * (r // 2) + 8]
                    between(r)
                    if at + r:
                        dve.wait_ge(count, at + r)
                    if r % 2 == 0:
                        nc.vector.max(some, values).then_inc(count, 1)
                    else:
                        nc.vector.match_replace(values, some, values, -3.0e38).then_inc(count, 1)
                return at + 2 * ROUNDS - 1

            def record(i, source, count):
                nc.vector.tensor_scalar(stat[:, bass.ds(i, 1)], source[:, 0:1], -1.0, None, ALU.mult).then_inc(count, 1)
                nc.vector.tensor_scalar(stat[:, bass.ds(QT + i, 1)], source[:, TOPK - 1:TOPK],
                                        source[:, TOPK:TOPK + 1], -0.5, ALU.add, ALU.mult).then_inc(count, 1)

            def tile(n, u, i1, i2, h_done, h_turned):
                new, old = cand[:, u % 2], cand[:, (u - 1) % 2]
                count, other = chains[u % 2], chains[(u + 1) % 2]
                deep, eighth, top = (x[(u - 1) % 2] for x in (deeps, eighths, tops))
                steps = 2 * ROUNDS + 1

                def some_segments(r):
                    for j in range(NSEG * r // steps, NSEG * (r + 1) // steps):
                        if n is not None:
                            a, w = segs[j]
                            seg = nc.vector.max(new[:, j], score[:, u, a:a + w])
                            if j == NSEG - 1:
                                seg.then_inc(count, 1)

                if n is not None:
                    hold(dve, (a_taken, 4 * (n + 1) + A_AHEAD))
                if i1 is None:
                    for r in range(steps):
                        some_segments(r)
                    dve.wait_ge(count, 1)
                    dve.sem_inc(passed, 1)
                    return
                nc.vector.max(deep[:, 0:8], old[:, 0:NSEG, DEEP:8]).then_inc(count, 1)
                nc.vector.tensor_reduce(eighth[:], old[:, 0:NSEG, 7], AX.X, ALU.max).then_inc(count, 1)
                some_segments(0)
                if i2 is not None:
                    check(H * QT - 2 if n is None else n - 2, (u - 2) % 4, i2)
                    if h_done is not None:
                        nc.vector.tensor_copy(stat_head[:], stat[:]).then_inc(stats_set, 1)
                dve.wait_ge(count, 2)
                nc.vector.tensor_copy(old[:, NSEG:NSEG + 3, 0:3], deep[:].rearrange("p (a b) -> p a b", a=3)).then_inc(count, 1)
                dve.sem_clear(other)
                at = largest(old[:, :, 0:DEEP], top, count, 3, lambda r: some_segments(r + 1))
                if n is not None:
                    some_segments(steps - 1)
                    at += 1
                if h_done is not None:
                    hold(dve, (stats_set, h_done + 1))
                if h_turned is not None:
                    split_shifts(h_turned)
                dve.wait_ge(count, at)
                record(i1, top, recorded)
                nc.vector.tensor_scalar(flag[:, (u - 1) % 4:(u - 1) % 4 + 1], eighth[:], deep[:, 7:8],
                                        top[:, TOPK:TOPK + 1], ALU.max, ALU.is_gt).then_inc(flagged, 1)

            def check(n, u, i):
                hold(dve, (reduced, n + 1))
                found = dve.value_load(anyflag[0:1, u:u + 1].bitcast(I32))
                with dve.If(found > 0):
                    dve.sem_clear(full_chain)
                    at = largest(score[:, u], top_full, full_chain, 0)
                    dve.wait_ge(full_chain, at)
                    record(i, top_full, full_chain)
                    dve.wait_ge(full_chain, at + 2)
                dve.sem_inc(s_free, 1)

            def split_shifts(h):
                dve.sem_clear(turn_chain)
                hold(dve, (st_turned, h + 1),
                     (st_loaded, 96 * h + 16))
                nc.vector.tensor_copy(statT[:], turned[0:2 * QT, 0:P]).then_inc(turn_chain, 1)
                dve.wait_ge(turn_chain, 1)
                nc.vector.tensor_copy(stat_parts[:, 0], statT[:]).then_inc(turn_chain, 1)
                dve.wait_ge(turn_chain, 2)
                nc.vector.tensor_tensor(stat_rest[:], statT[:], stat_parts[:, 0], ALU.subtract).then_inc(turn_chain, 1)
                dve.wait_ge(turn_chain, 3)
                nc.vector.tensor_copy(stat_parts[:, 1], stat_rest[:]).then_inc(turn_chain, 1)
                dve.wait_ge(turn_chain, 4)
                nc.vector.tensor_tensor(stat_rest[:], stat_rest[:], stat_parts[:, 1], ALU.subtract).then_inc(turn_chain, 1)
                dve.wait_ge(turn_chain, 5)
                nc.vector.tensor_copy(stat_parts[:, 2], stat_rest[:]).then_inc(st_split, 1)
                hold(dve, (st_split, h + 1))

            def group(h, g, first, prev_head):
                for u in range(4):
                    n = h * QT + 4 * g + u
                    if isinstance(g, int):
                        i1 = (u - 1) % QT if u >= 1 or not first else None
                        i2 = (u - 2) % QT if u >= 2 or not first else None
                    else:
                        i1, i2 = 4 * g + (u - 1), 4 * g + (u - 2)
                    tile(n, u, i1, i2, prev_head if u == 1 else None, prev_head if u == TURN_AT else None)

            group(0, 0, True, None)
            with dve.Fori(1, G4) as g:
                group(0, g, False, None)
            with dve.Fori(0, H - 1) as h:
                group(h + 1, 0, False, h)
                with dve.Fori(1, G4) as g:
                    group(h + 1, g, False, None)
            tile(None, 0, QT - 1, QT - 2, None, None)
            check(H * QT - 1, 3, QT - 1)
            nc.vector.tensor_copy(stat_head[:], stat[:]).then_inc(stats_set, 1)
            split_shifts(H - 1)


def finish(nc, G, A, tag, wo, bo, den_eps):
    with ExitStack() as stack:
        s = Scope(nc, stack, tag)
        w_rows, wT = s.sb("w_rows", [P, KC, D]), s.sb("wT", [P, KC, D])
        bias = s.sb("bias", [1, D])
        num, den = s.sb("num", [P, KC, S]), s.sb("den", [P, KC, S])
        banks = [s.ps(f"bank{b}", [P, CH]) for b in range(4)]
        loaded, turned, w_ready, normed, formed, added = (s.sem(x) for x in (
            "loaded", "turned", "w_ready", "normed", "formed", "added"))
        block = stack.enter_context(nc.Block())
        LOADS = (2 + 2 * H) * 16
        STEPS = KC * (3 if den_eps else 2)

        @block.sync
        def _(sp):
            sp.dma_start(w_rows[:], wo.rearrange("(c p) d -> p c d", p=P)).then_inc(loaded, 16)
            sp.dma_start(bias[:], bo).then_inc(loaded, 16)
            for h in range(H):
                c, r = divmod(h * DH, P)
                sp.dma_start(num[r:r + DH, c], G.sums[h, 0:DH]).then_inc(loaded, 16)
                sp.dma_start(den[r:r + DH, c], G.sums[h, DH:2 * DH]).then_inc(loaded, 16)

        @block.tensor
        def _(pe):
            pe.wait_ge(loaded, LOADS)
            for ic in range(KC):
                for oc in range(KC):
                    mm = nc.tensor.transpose(banks[0][:, ic * D + oc * P:ic * D + (oc + 1) * P],
                                             w_rows[:, oc, ic * P:(ic + 1) * P], G.ident[:])
            mm.then_inc(turned, 1)
            pe.wait_ge(w_ready, 1)
            pe.wait_ge(normed, STEPS)
            for t in range(QT):
                if t >= 4:
                    pe.wait_ge(added, t - 3)
                bank = banks[t % 4][:, 0:D]
                for c in range(KC):
                    nc.tensor.matmul(bank, num[:, c, t * P:(t + 1) * P], wT[:, c], start=(c == 0), stop=False)
                nc.tensor.matmul(bank, G.ones[0:1, 0:P], bias[:], start=False, stop=True).then_inc(formed, 1)

        @block.scalar
        def _(act):
            act.wait_ge(turned, 1)
            nc.scalar.activation(wT[:], banks[0][:].rearrange("p (c d) -> p c d", c=KC), ACT.Copy).then_inc(w_ready, 1)

        @block.vector
        def _(dve):
            dve.wait_ge(loaded, LOADS)
            k = 0
            for c in range(KC):
                if den_eps:
                    nc.vector.tensor_scalar(den[:, c], den[:, c], den_eps, None, ALU.add).then_inc(normed, 1)
                    k += 1
                    dve.wait_ge(normed, k)
                nc.vector.reciprocal(den[:, c], den[:, c]).then_inc(normed, 1)
                k += 1
                dve.wait_ge(normed, k)
                nc.vector.tensor_tensor(num[:, c], num[:, c], den[:, c], ALU.mult).then_inc(normed, 1)
                k += 1
            for t in range(QT):
                dve.wait_ge(formed, t + 1)
                nc.vector.tensor_tensor(G.x_tok[:, t], banks[t % 4][:, 0:D], G.x_tok[:, t], ALU.add).then_inc(added, 1)
    layer_norm(nc, G, A, tag + "n")


def layer_norm(nc, G, A, tag, out=None, affine=None):
    with ExitStack() as stack:
        s = Scope(nc, stack, tag)
        bn = s.sb("bn", [P, QT, 6])
        mv = s.sb("mv", [P, QT, 2])
        dev = s.sb("dev", [P, QT])
        eps = s.sb("eps", [P, 1])
        y_tok = s.sb("y_tok", [P, QT, D]) if affine else G.x_tok
        if affine:
            rows = s.sb("rows", [2 * KC, P])
            cols = s.sb("cols", [P, 2 * KC])
        dstT = G.xn if affine else G.xT
        banks = [s.ps(f"bank{b}", [P, CH]) for b in range(2)]
        stats, agg, rooted, inv, normed, turned, taken, stored, loaded = (s.sem(x) for x in (
            "stats", "agg", "rooted", "inv", "normed", "turned", "taken", "stored", "loaded"))
        jobs = [(c, g) for g in range(0, QT, 4) for c in range(KC)]
        block = stack.enter_context(nc.Block())
        pre = 1 if affine else 0

        @block.vector
        def _(dve):
            nc.vector.memset(eps[:], EPS).then_inc(agg, 1)
            for t in range(QT):
                nc.vector.bn_stats(bn[:, t], G.x_tok[:, t]).then_inc(stats, 1)
            for t in range(QT):
                dve.wait_ge(stats, t + 1)
                nc.vector.bn_aggr(mv[:, t], bn[:, t]).then_inc(agg, 1)
            dve.wait_ge(rooted, 1)
            nc.vector.reciprocal(dev[:], dev[:]).then_inc(inv, 1)
            dve.wait_ge(inv, 1)
            dve.wait_ge(agg, QT + 1)
            for t in range(QT):
                nc.vector.tensor_scalar(y_tok[:, t], G.x_tok[:, t], mv[:, t, 0:1], dev[:, t:t + 1],
                                        ALU.subtract, ALU.mult).then_inc(normed, 1)

        @block.scalar
        def _(act):
            if affine:
                act.wait_ge(turned, 1)
                nc.scalar.activation(cols[:], banks[0][:, 0:2 * KC], ACT.Copy).then_inc(taken, 1)
            act.wait_ge(agg, QT + 1)
            nc.scalar.activation(dev[:], mv[:, :, 1], ACT.Sqrt, bias=eps[:]).then_inc(rooted, 1)
            if out is None:
                for j, (c, g) in enumerate(jobs):
                    act.wait_ge(turned, j + 1 + pre)
                    if affine:
                        act.wait_ge(taken, 1)
                        nc.scalar.activation(dstT[:, c, g * P:(g + 4) * P], banks[(j + pre) % 2][:], ACT.Identity,
                                             scale=cols[:, c:c + 1], bias=cols[:, KC + c:KC + c + 1]).then_inc(taken, 1)
                    else:
                        nc.scalar.activation(dstT[:, c, g * P:(g + 4) * P], banks[j % 2][:], ACT.Copy).then_inc(taken, 1)

        @block.tensor
        def _(pe):
            if affine:
                pe.wait_ge(loaded, 32)
                nc.tensor.transpose(banks[0][:, 0:2 * KC], rows[:], G.ident[0:2 * KC, 0:2 * KC]).then_inc(turned, 1)
            if out is None:
                for j, (c, g) in enumerate(jobs):
                    pe.wait_ge(normed, g + 4)
                    if j + pre >= 2:
                        pe.wait_ge(taken, j + pre - 1)
                    for k in range(4):
                        mm = nc.tensor.transpose(banks[(j + pre) % 2][:, k * P:(k + 1) * P],
                                                 y_tok[:, g + k, c * P:(c + 1) * P], G.ident[:])
                    mm.then_inc(turned, 1)

        @block.sync
        def _(sp):
            if affine:
                for j, v in enumerate(affine):
                    sp.dma_start(rows[j * KC:(j + 1) * KC], v.rearrange("(c p) -> c p", p=P)).then_inc(loaded, 16)
            if out is not None:
                for g in range(0, QT, 4):
                    sp.wait_ge(normed, g + 4)
                    sp.dma_start(out[0, g * P:(g + 4) * P].rearrange("(t p) d -> p t d", p=P),
                                 G.x_tok[:, g:g + 4]).then_inc(stored, 16)
                sp.wait_ge(stored, 16 * QT // 4)


def attend_causal(nc, G, tag, V):
    with ExitStack() as stack:
        s = Scope(nc, stack, tag)
        Kb = s.sb("k_stack", [ROWS, SLOTS * S], BF16)
        Qm = s.sb("q_stack", [ROWS, SLOTS * S], BF16)
        part_max = s.sb("part_max", [P, 2, QC])
        stat = s.sb("stat", [P, 32])
        statT = s.sb("statT", [32, P])
        stat_rest = s.sb("stat_rest", [32, P])
        stat_parts = s.sb("stat_parts", [32, 3, P], BF16)
        prob = s.sb("prob", [P, 2, QC, CH])
        Vh = s.sb("v_head", [P, 2, 2 * DH])
        O_out = s.sb("o_out", [P, CH])
        sA = [s.ps(f"by_query{b}", [P, CH]) for b in range(4)]
        yP = [s.ps(f"less_max{b}", [P, CH]) for b in range(2)]
        O = s.ps("o_sum", [P, CH])
        turned = s.ps("turned", [P, CH])
        (ready, loaded, a_formed, a_taken, y_formed, y_taken, staged, pv_done, o_formed, o_taken,
         o_stored, chain, maxed, stats_set, st_turned, st_split, st_loaded, passed) = (s.sem(x) for x in (
             "ready", "loaded", "a_formed", "a_taken", "y_formed", "y_taken", "staged", "pv_done",
             "o_formed", "o_taken", "o_stored", "chain", "maxed", "stats_set", "st_turned", "st_split",
             "st_loaded", "passed"))
        A_AHEAD, Y_AHEAD, PV_AHEAD, O_AHEAD, M_AHEAD = 4, 2, 2, 1, 1
        READY = 6
        LAG = 4
        PER_HEAD = 2 * QC * (QC + 1)
        block = stack.enter_context(nc.Block())

        def hold(eng, *events):
            for sem, n in events:
                eng.wait_ge(sem, n)
            if eng in (nc.vector, nc.gpsimd, nc.sync):
                eng.sem_inc(passed, 1)

        def a_index(h, L, ii):
            return h * PER_HEAD + 2 * L * (L + 1) + ii * (L + 1)

        def b_index(h, L, ii):
            return h * PER_HEAD + 16 * L - 2 * L * (L - 1) + ii * (QC - L)

        def heads(eng, step, a_end=None, b_end=None):
            def level(ha, hb, L):
                def pair(jj):
                    for u in range(2):
                        step(ha, hb, L, jj, u)
                for jj in range(2):
                    pair(jj)

            def head(ha, hb):
                for L in range(QC):
                    level(ha, hb, L)
                if b_end and hb is not None:
                    b_end(hb)
                if a_end and ha is not None:
                    a_end(ha)

            head(0, None)
            with eng.Fori(0, H - 1) as h:
                head(h + 1, h)
            head(None, H - 1)

        @block.sync
        def _(sp):
            per_head = 2 * len(SPLITS) * 16

            def load(h):
                load_head(nc, G, sp, h, S, Kb, Qm, None, loaded)
                hold(sp, (loaded, per_head * (h + 1) + SLOTS * 16))

            def stats(h):
                hold(sp, (st_split, h + 1))
                slot = h & (SLOTS - 1)
                for j in range(3):
                    row = slice(SHIFT_ROW + j, SHIFT_ROW + j + 1)
                    sp.dma_start(Qm[row, bass.ds(slot * S, S)], stat_parts[0:QT, j]).then_inc(st_loaded, 16)
                hold(sp, (st_loaded, 48 * (h + 1) + 16))

            sp.sem_inc(st_loaded, 16)
            sp.wait_ge(ready, READY)
            for slot in range(SLOTS):
                sp.dma_start(Kb[MASK_ROW:MASK_ROW + 1, slot * S:(slot + 1) * S], G.mask_row[:]).then_inc(loaded, 16)
            for h in range(SLOTS):
                load(h)
                if h >= 2:
                    stats(h - 2)
            with sp.Fori(2, H - 2) as h:
                stats(h)
                hold(sp, (o_formed, h - 1))
                load(h + 2)
            stats(H - 2)
            stats(H - 1)

        @block.gpsimd
        def _(pool):
            nc.gpsimd.memset(Kb[:], 0.0).then_inc(ready, 1)
            pool.wait_ge(ready, 1)
            nc.gpsimd.memset(Kb[MASK_ROW:ROWS, :], 1.0).then_inc(ready, 1)
            pool.wait_ge(ready, 2)
            nc.gpsimd.memset(Qm[MASK_ROW:ROWS, :], 1.0).then_inc(ready, 1)
            pool.wait_ge(ready, 3)
            nc.gpsimd.memset(stat[:], 0.0).then_inc(ready, 1)
            pool.wait_ge(ready, 4)
            nc.gpsimd.memset(O_out[:], 0.0).then_inc(ready, 1)
            pool.wait_ge(ready, 5)
            nc.gpsimd.memset(part_max[:], 0.0).then_inc(ready, 1)
            pool.wait_ge(ready, READY)

            def step(ha, hb, L, jj, u):
                if hb is not None:
                    i = 4 * L + 2 * jj + u
                    hold(pool, (pv_done, hb * QT + i - 2 + 1 + PV_AHEAD))
                    nc.gpsimd.tensor_copy(Vh[:, u], V[:, bass.ds(i, 1), bass.ds(hb, 1), :]).then_inc(staged, 1)

            heads(pool, step)

        @block.tensor
        def _(pe):
            pe.sem_inc(pv_done, PV_AHEAD)
            pe.wait_ge(ready, READY)

            def by_query(h, i, c):
                L, ii, slot = i // 4, i % 4, h & (SLOTS - 1)
                hold(pe, (a_taken, a_index(h, L, ii) + c - 4 + 1 + A_AHEAD))
                bank = sA[(a_index(0, L, ii) + c) % 4]
                mm = nc.tensor.matmul(bank[:], Qm[0:SHIFT_ROW, bass.ds(slot * S + i * P, P)],
                                      Kb[0:SHIFT_ROW, bass.ds(slot * S + c * CH, CH)],
                                      start=True, stop=(c < L))
                if c == L:
                    mm = nc.tensor.matmul(bank[:], G.identb[:], G.band[:, 0, (3 - ii) * P:(3 - ii) * P + CH],
                                          start=False, stop=True)
                mm.then_inc(a_formed, 1)

            def by_key(h, i, c):
                L, ii, slot = i // 4, i % 4, h & (SLOTS - 1)
                hold(pe, (y_taken, b_index(h, L, ii) + c - L - 2 + 1 + Y_AHEAD))
                bank = yP[(i % 2 * (QC - L) + c - L) % 2]
                mm = nc.tensor.matmul(bank[:], Kb[:, bass.ds(slot * S + i * P, P)],
                                      Qm[:, bass.ds(slot * S + c * CH, CH)], start=True, stop=(c > L))
                if c == L:
                    mm = nc.tensor.matmul(bank[:], G.identb[:], G.band[:, 1, (3 - ii) * P:(3 - ii) * P + CH],
                                          start=False, stop=True)
                mm.then_inc(y_formed, 1)

            def sums(h, i):
                L, ii = i // 4, i % 4
                hold(pe, (staged, h * QT + i + 1),
                     (y_taken, b_index(h, L, ii) + QC - L + Y_AHEAD))
                for c in range(L, QC):
                    mm = nc.tensor.matmul(O[32 * c:32 * (c + 1), :], Vh[:, i % 2], prob[:, i % 2, c],
                                          start=False, stop=False, skip_group_check=True)
                mm.then_inc(pv_done, 1)

            def head(ha, hb):
                if ha is not None:
                    hold(pe, (loaded, 2 * len(SPLITS) * 16 * (ha + 1) + SLOTS * 16))
                    for i in range(LAG):
                        for c in range(i // 4 + 1):
                            by_query(ha, i, c)
                if hb is not None:
                    b_start(hb)
                    hold(pe, (st_loaded, 48 * (hb + 1) + 16))
                for i in range(QT):
                    L, ahead = i // 4, i + LAG
                    for c in range(QC):
                        if hb is not None and L + c < QC:
                            by_key(hb, i, L + c)
                        if ha is not None and ahead < QT and c <= ahead // 4:
                            by_query(ha, ahead, c)
                        if hb is not None and i and c == 1:
                            sums(hb, i - 1)
                if hb is not None:
                    b_end(hb)
                if ha is not None:
                    a_end(ha)

            def b_start(h):
                hold(pe, (o_taken, h + O_AHEAD))
                nc.tensor.matmul(O[:], G.zerob[:, 0:P], G.zerob[:], start=True, stop=False, skip_group_check=True)

            def b_end(h):
                sums(h, QT - 1)
                hold(pe, (pv_done, (h + 1) * QT + PV_AHEAD))
                pe.sem_inc(o_formed, 1)

            def a_end(h):
                hold(pe, (stats_set, h + 1))
                nc.tensor.transpose(turned[0:32, 0:P], stat[:], G.ident[:]).then_inc(st_turned, 1)

            head(0, None)
            with pe.Fori(0, H - 1) as h:
                head(h + 1, h)
            head(None, H - 1)

        @block.scalar
        def _(act):
            act.sem_inc(y_taken, Y_AHEAD)
            act.sem_inc(o_taken, O_AHEAD)
            act.sem_inc(o_stored, 16)
            act.wait_ge(ready, READY)

            def step(ha, hb, L, jj, u):
                if hb is not None:
                    ii = 2 * jj + u
                    hold(act, (pv_done, hb * QT + 4 * L + ii - 2 + 1 + PV_AHEAD))
                    for c in range(L, QC):
                        hold(act, (y_formed, b_index(hb, L, ii) + c - L + 1))
                        nc.scalar.activation(prob[:, u, c], yP[(u * (QC - L) + c - L) % 2][:],
                                             ACT.Exp).then_inc(y_taken, 1)

            def b_end(h):
                hold(act, (o_formed, h + 1),
                     (o_stored, 64 * h + 16))
                nc.scalar.activation(O_out[:], O[:], ACT.Copy).then_inc(o_taken, 1)
                hold(act, (o_taken, h + 1 + O_AHEAD))
                for c in range(QC):
                    act.dma_start(G.sums[bass.ds(h, 1), :, c * CH:(c + 1) * CH],
                                  O_out[32 * c:32 * (c + 1), :]).then_inc(o_stored, 16)

            heads(act, step, b_end=b_end)
            act.wait_ge(o_stored, 64 * H + 16)

        @block.vector
        def _(dve):
            dve.sem_inc(a_taken, A_AHEAD)
            dve.sem_inc(maxed, M_AHEAD)
            dve.wait_ge(ready, READY)

            def step(ha, hb, L, jj, u):
                if ha is not None:
                    ii = 2 * jj + u
                    i = 4 * L + ii
                    hold(dve, (maxed, ha * QT + i - 1 + M_AHEAD))
                    for c in range(L + 1):
                        hold(dve, (a_formed, a_index(ha, L, ii) + c + 1))
                        nc.vector.tensor_reduce(part_max[:, u, c:c + 1], sA[(a_index(0, L, ii) + c) % 4][:],
                                                AX.X, ALU.max).then_inc(a_taken, 1)
                    hold(dve, (a_taken, a_index(ha, L, ii) + L + 1 + A_AHEAD))
                    nc.vector.tensor_reduce(stat[:, bass.ds(i, 1)], part_max[:, u, 0:L + 1], AX.X, ALU.max,
                                            negate=True).then_inc(maxed, 1)

            def a_end(h):
                hold(dve, (maxed, (h + 1) * QT + M_AHEAD))
                dve.sem_inc(stats_set, 1)
                dve.sem_clear(chain)
                hold(dve, (st_turned, h + 1),
                     (st_loaded, 48 * h + 16))
                nc.vector.tensor_copy(statT[:], turned[0:32, 0:P]).then_inc(chain, 1)
                dve.wait_ge(chain, 1)
                nc.vector.tensor_copy(stat_parts[:, 0], statT[:]).then_inc(chain, 1)
                dve.wait_ge(chain, 2)
                nc.vector.tensor_tensor(stat_rest[:], statT[:], stat_parts[:, 0], ALU.subtract).then_inc(chain, 1)
                dve.wait_ge(chain, 3)
                nc.vector.tensor_copy(stat_parts[:, 1], stat_rest[:]).then_inc(chain, 1)
                dve.wait_ge(chain, 4)
                nc.vector.tensor_tensor(stat_rest[:], stat_rest[:], stat_parts[:, 1], ALU.subtract).then_inc(chain, 1)
                dve.wait_ge(chain, 5)
                nc.vector.tensor_copy(stat_parts[:, 2], stat_rest[:]).then_inc(st_split, 1)
                hold(dve, (st_split, h + 1))

            heads(dve, step, a_end=a_end)


EXPERTS = 8
HID = 512
LIMIT = 7.0
ALPHA = 1.702


def moe_gate(nc, G, A, M):
    with ExitStack() as stack:
        s = Scope(nc, stack, "gate")
        square = s.sb("square", [P, 2, D])
        sums, rms = s.sb("sums", [P, QT]), s.sb("rms", [P, QT])
        eps = s.sb("eps", [P, 1])
        t_tok = s.sb("t_tok", [P, QT, D])
        scale_rows, scale = s.sb("scale_rows", [KC, P]), s.sb("scale", [P, KC])
        gate_w, gate_b = s.sb("gate_w", [P, KC, EXPERTS]), s.sb("gate_b", [1, EXPERTS])
        b1_rows = s.sb("b1_rows", [4 * EXPERTS, 2 * P])
        b2 = s.sb("b2", [EXPERTS, D])
        ids = s.sb("ids", [P, EXPERTS])
        logits = s.sb("logits", [P, QT, EXPERTS])
        best, where = s.sb("best", [P, QT, 8]), s.sb("where", [P, QT, 8], U32)
        wheref = s.sb("wheref", [P, QT, 8])
        gap, e2, total = s.sb("gap", [P, QT]), s.sb("e2", [P, QT]), s.sb("total", [P, QT])
        p1, p2 = s.sb("p1", [P, QT]), s.sb("p2", [P, QT])
        w2nd = s.sb("w2nd", [P, QT, EXPERTS])
        wT = s.sb("wT", [EXPERTS, S])
        banks = [s.ps(f"bank{b}", [P, CH]) for b in range(3)]
        small = s.ps("small", [P, CH])
        logit_bank = s.ps("logit_bank", [P, CH])
        (loaded, squared, rooted, inv, scaled, turned, taken, small_formed, small_taken, logged, step, expd,
         weighed, w_turned, w_taken, y_formed, added) = (s.sem(x) for x in (
             "loaded", "squared", "rooted", "inv", "scaled", "turned", "taken", "small_formed",
             "small_taken", "logged", "step", "expd", "weighed", "w_turned", "w_taken", "y_formed", "added"))
        jobs = [(c, g) for g in range(0, QT, 4) for c in range(KC)]
        LOADS = 6 * 16
        block = stack.enter_context(nc.Block())

        @block.sync
        def _(sp):
            sp.dma_start(scale_rows[:], A["L0_ffn_norm_scale"].rearrange("(c p) -> c p", p=P)).then_inc(loaded, 16)
            sp.dma_start(gate_w[:], A["L0_ffn_gate_w"].rearrange("(c p) e -> p c e", p=P)).then_inc(loaded, 16)
            sp.dma_start(gate_b[:], A["L0_ffn_gate_b"].rearrange("(o n) -> o n", o=1)).then_inc(loaded, 16)
            sp.dma_start(b1_rows[:], A["L0_ffn_mlp1_b"].rearrange("e (j n) -> (e j) n", n=2 * P)).then_inc(loaded, 16)
            sp.dma_start(b2[:], A["L0_ffn_mlp2_b"]).then_inc(loaded, 16)
            sp.dma_start(ids[:], A["const_experts"]).then_inc(loaded, 16)

        @block.scalar
        def _(act):
            act.wait_ge(small_formed, 1)
            nc.scalar.activation(scale[:], small[:, 0:KC], ACT.Copy).then_inc(small_taken, 1)
            nc.scalar.activation(M.b_glu[:], small[:, 64:64 + 4 * EXPERTS], ACT.Copy).then_inc(small_taken, 1)
            nc.scalar.activation(M.b_lin[:], small[:, 128:128 + 4 * EXPERTS], ACT.Copy, bias=1.0).then_inc(small_taken, 1)
            for t in range(QT):
                if t >= 2:
                    act.wait_ge(squared, t - 1)
                nc.scalar.activation(square[:, t % 2], G.x_tok[:, t], ACT.Square,
                                     accum_out=sums[:, t:t + 1]).then_inc(squared, 1)
            act.wait_ge(squared, QT)
            act.wait_ge(step, 1)
            nc.scalar.activation(rms[:], sums[:], ACT.Sqrt, bias=eps[:], scale=1.0 / D).then_inc(rooted, 1)
            act.wait_ge(small_taken, 1)
            for j, (c, g) in enumerate(jobs):
                act.wait_ge(turned, j + 1)
                nc.scalar.activation(M.tT[:, c, g * P:(g + 4) * P], banks[j % 2][:], ACT.Copy,
                                     scale=scale[:, c:c + 1]).then_inc(taken, 1)
            act.wait_ge(step, 4)
            nc.scalar.activation(e2[:], gap[:], ACT.Exp).then_inc(expd, 1)
            for g in range(QT // 4):
                act.wait_ge(w_turned, g + 1)
                nc.scalar.activation(wT[:, g * CH:(g + 1) * CH], banks[g % 2][0:EXPERTS, :], ACT.Copy).then_inc(w_taken, 1)

        @block.tensor
        def _(pe):
            pe.wait_ge(loaded, LOADS)
            nc.tensor.transpose(small[:, 0:KC], scale_rows[:], G.ident[0:KC, 0:KC])
            rows = b1_rows[:].rearrange("r (p two) -> r p two", two=2)
            n = 4 * EXPERTS
            nc.tensor.transpose(small[:, 64:64 + n], rows[:, :, 0], G.ident[0:n, 0:n])
            nc.tensor.transpose(small[:, 128:128 + n], rows[:, :, 1], G.ident[0:n, 0:n]).then_inc(small_formed, 1)
            for j, (c, g) in enumerate(jobs):
                pe.wait_ge(scaled, g + 4)
                if j >= 2:
                    pe.wait_ge(taken, j - 1)
                for k in range(4):
                    mm = nc.tensor.transpose(banks[j % 2][:, k * P:(k + 1) * P],
                                             t_tok[:, g + k, c * P:(c + 1) * P], G.ident[:])
                mm.then_inc(turned, 1)
            pe.wait_ge(taken, len(jobs))
            for t in range(QT):
                to = logit_bank[:, t * EXPERTS:(t + 1) * EXPERTS]
                for c in range(KC):
                    nc.tensor.matmul(to, M.tT[:, c, t * P:(t + 1) * P], gate_w[:, c], start=(c == 0), stop=False)
                mm = nc.tensor.matmul(to, G.ones[0:1, 0:P], gate_b[:], start=False, stop=True)
            mm.then_inc(logged, 1)
            pe.wait_ge(weighed, 1)
            for g in range(QT // 4):
                if g >= 2:
                    pe.wait_ge(w_taken, g - 1)
                for k in range(4):
                    mm = nc.tensor.transpose(banks[g % 2][0:EXPERTS, k * P:(k + 1) * P], M.w[:, 4 * g + k], G.ident[:])
                mm.then_inc(w_turned, 1)
            pe.wait_ge(w_taken, QT // 4)
            for t in range(QT):
                if t >= 2:
                    pe.wait_ge(added, t - 1)
                nc.tensor.matmul((banks[2], small)[t % 2][:, 0:D], wT[:, t * P:(t + 1) * P], b2[:],
                                 start=True, stop=True).then_inc(y_formed, 1)

        @block.vector
        def _(dve):
            nc.vector.memset(eps[:], EPS).then_inc(step, 1)
            dve.wait_ge(rooted, 1)
            nc.vector.reciprocal(rms[:], rms[:]).then_inc(inv, 1)
            dve.wait_ge(inv, 1)
            for t in range(QT):
                nc.vector.tensor_scalar(t_tok[:, t], G.x_tok[:, t], rms[:, t:t + 1], None, ALU.mult).then_inc(scaled, 1)
            dve.wait_ge(logged, 1)
            nc.vector.tensor_copy(logits[:], logit_bank[:, 0:QT * EXPERTS].rearrange("p (t e) -> p t e", e=EXPERTS)).then_inc(step, 1)
            dve.wait_ge(step, 2)
            for t in range(QT):
                mx = nc.vector.max(best[:, t], logits[:, t])
            mx.then_inc(step, 1)
            dve.wait_ge(step, 3)
            nc.vector.tensor_tensor(gap[:], best[:, :, 1], best[:, :, 0], ALU.subtract).then_inc(step, 1)
            for t in range(QT):
                mi = nc.vector.max_index(where[:, t], best[:, t], logits[:, t])
            mi.then_inc(step, 1)
            dve.wait_ge(step, 5)
            nc.vector.tensor_copy(wheref[:], where[:]).then_inc(step, 1)
            dve.wait_ge(expd, 1)
            nc.vector.tensor_scalar(total[:], e2[:], 1.0, None, ALU.add).then_inc(step, 1)
            dve.wait_ge(step, 7)
            nc.vector.reciprocal(p1[:], total[:]).then_inc(step, 1)
            dve.wait_ge(step, 8)
            nc.vector.tensor_tensor(p2[:], p1[:], e2[:], ALU.mult).then_inc(step, 1)
            dve.wait_ge(step, 9)
            dve.wait_ge(loaded, LOADS)
            for t in range(QT):
                nc.vector.tensor_scalar(M.w[:, t], ids[:], wheref[:, t, 0:1], p1[:, t:t + 1], ALU.is_equal, ALU.mult)
                last = nc.vector.tensor_scalar(w2nd[:, t], ids[:], wheref[:, t, 1:2], p2[:, t:t + 1], ALU.is_equal, ALU.mult)
            last.then_inc(step, 1)
            dve.wait_ge(step, 10)
            nc.vector.tensor_tensor(M.w[:], M.w[:], w2nd[:], ALU.add).then_inc(weighed, 1)
            for t in range(QT):
                dve.wait_ge(y_formed, t + 1)
                nc.vector.scalar_tensor_tensor(out=G.x_tok[:, t], in0=G.x_tok[:, t], scalar=2.0,
                                               in1=(banks[2], small)[t % 2][:, 0:D],
                                               op0=ALU.mult, op1=ALU.add).then_inc(added, 1)


def moe_experts(nc, G, A, M):
    HT = HID // P
    with ExitStack() as stack:
        s = Scope(nc, stack, "moe")
        w1 = [s.sb(f"w1_{u}", [P, KC, 2 * HID]) for u in range(2)]
        w2 = [s.sb(f"w2_{u}", [P, HT, D]) for u in range(2)]
        glu, sig, lin = s.sb("glu", [P, 2, CH]), s.sb("sig", [P, 2, CH]), s.sb("lin", [P, 2, CH])
        act_glu = s.sb("act_glu", [P, 2, CH])
        hid = s.sb("hid", [P, 2, HT, CH])
        gP = [s.ps(f"glu{b}", [P, CH]) for b in range(2)]
        lP = [s.ps(f"lin{b}", [P, CH]) for b in range(2)]
        yP = [[s.ps(f"y{b}{k}", [P, CH]) for k in range(2)] for b in range(2)]
        (g_formed, l_formed, g_taken, l_taken, sigged, gated, hidden, y_formed, y_taken, passed) = (
            s.sem(x) for x in ("g_formed", "l_formed", "g_taken", "l_taken", "sigged", "gated",
                               "hidden", "y_formed", "y_taken", "passed"))
        w_loaded = [s.sem(f"w_loaded{u}") for u in range(2)]
        G_AHEAD, H_AHEAD, Y_AHEAD = 2, 2, 4
        block = stack.enter_context(nc.Block())

        def hold(eng, *events):
            for sem, n in events:
                eng.wait_ge(sem, n)
            if eng in (nc.gpsimd, nc.sync):
                eng.sem_inc(passed, 1)

        def pairs(eng, body):
            with eng.Fori(0, EXPERTS // 2) as ep:
                for u in range(2):
                    with eng.Fori(0, QC // 2) as cc:
                        body(ep, u, cc, (ep * 2 + u) * (QC // 2) + cc)

        @block.sync
        def _(sp):
            src1 = A["L0_ffn_mlp1_w"].rearrange("e (c p) n -> e p c n", p=P)
            src2 = A["L0_ffn_mlp2_w"].rearrange("e (c p) n -> e p c n", p=P)

            def load(e, u):
                for ic in range(KC):
                    sp.dma_start(w1[u][:, ic], src1[bass.ds(e, 1), :, ic]).then_inc(w_loaded[u], 16)
                for ic in range(HT):
                    sp.dma_start(w2[u][:, ic], src2[bass.ds(e, 1), :, ic]).then_inc(w_loaded[u], 16)

            for u in range(2):
                load(u, u)
            with sp.Fori(1, EXPERTS // 2) as ep:
                for u in range(2):
                    e = ep * 2 + u
                    hold(sp, (y_formed, 2 * QC * (e - 1)))
                    load(e, u)

        @block.tensor
        def _(pe):
            def pair(ep, u, cc, p):
                hold(pe, (w_loaded[u], (ep + 1) * 16 * (KC + HT)))
                taps = w1[u][:].rearrange("p c (j m two) -> p c j m two", j=HT, two=2)
                for c2 in range(2):
                    for j in range(HT):
                        z = p * 2 * HT + c2 * HT + j
                        hold(pe, (g_taken, z - 2 + 1 + G_AHEAD), (l_taken, z - 2 + 1 + G_AHEAD))
                        for two, bank, formed in ((0, gP, g_formed), (1, lP, l_formed)):
                            for ic in range(KC):
                                mm = nc.tensor.matmul(bank[j % 2][:], taps[:, ic, j, :, two],
                                                      M.tT[:, ic, bass.ds(cc * 2 * CH + c2 * CH, CH)],
                                                      start=(ic == 0), stop=(ic == KC - 1))
                            mm.then_inc(formed, 1)
                for c2 in range(2):
                    q = p * 2 + c2
                    hold(pe, (hidden, (q + 1) * HT + H_AHEAD), (y_taken, 2 * q - 4 + 2 + Y_AHEAD))
                    for k in range(4):
                        to = yP[c2][k // 2][:, (k % 2) * D:(k % 2 + 1) * D]
                        for j in range(HT):
                            mm = nc.tensor.matmul(to, hid[:, c2, j, k * P:(k + 1) * P], w2[u][:, j],
                                                  start=(j == 0), stop=(j == HT - 1))
                        if k % 2:
                            mm.then_inc(y_formed, 1)
            pairs(pe, pair)

        @block.scalar
        def _(act):
            def pair(ep, u, cc, p):
                for c2 in range(2):
                    for j in range(HT):
                        z = p * 2 * HT + c2 * HT + j
                        hold(act, (g_taken, z + 1 + G_AHEAD), (gated, z - 2 + 1 + G_AHEAD))
                        nc.scalar.activation(sig[:, j % 2], glu[:, j % 2], ACT.Sigmoid, scale=ALPHA).then_inc(sigged, 1)
            pairs(act, pair)

        @block.gpsimd
        def _(pool):
            pool.sem_inc(gated, G_AHEAD)

            def pair(ep, u, cc, p):
                for c2 in range(2):
                    for j in range(HT):
                        z = p * 2 * HT + c2 * HT + j
                        hold(pool, (sigged, z + 1), (hidden, z - 2 + 1 + H_AHEAD))
                        nc.gpsimd.tensor_tensor(act_glu[:, j % 2], glu[:, j % 2], sig[:, j % 2], ALU.mult).then_inc(gated, 1)
            pairs(pool, pair)

        @block.vector
        def _(dve):
            dve.sem_inc(g_taken, G_AHEAD)
            dve.sem_inc(l_taken, G_AHEAD)
            dve.sem_inc(hidden, H_AHEAD)
            dve.sem_inc(y_taken, Y_AHEAD)

            def pair(ep, u, cc, p):
                def hide(zz):
                    c2, j = divmod(zz, HT)
                    z = p * 2 * HT + zz
                    hold(dve, (gated, z + 1 + G_AHEAD), (l_taken, z + 1 + G_AHEAD))
                    nc.vector.scalar_tensor_tensor(out=hid[:, c2, j], in0=lin[:, j % 2], scalar=1.0 - LIMIT,
                                                   in1=act_glu[:, j % 2], op0=ALU.max, op1=ALU.mult).then_inc(hidden, 1)
                hold(dve, (y_taken, 4 * p + Y_AHEAD))
                for zz in range(2 * HT):
                    c2, j = divmod(zz, HT)
                    z = p * 2 * HT + zz
                    col = bass.ds((ep * 2 + u) * HT + j, 1)
                    hold(dve, (g_formed, z + 1), (gated, z - 2 + 1 + G_AHEAD))
                    nc.vector.tensor_scalar(glu[:, j % 2], gP[j % 2][:], M.b_glu[:, col], LIMIT, ALU.add,
                                            ALU.min).then_inc(g_taken, 1)
                    hold(dve, (l_formed, z + 1), (hidden, z - 2 + 1 + H_AHEAD))
                    nc.vector.tensor_scalar(lin[:, j % 2], lP[j % 2][:], M.b_lin[:, col], LIMIT + 1.0, ALU.add,
                                            ALU.min).then_inc(l_taken, 1)
                    if zz:
                        hide(zz - 1)
                hide(2 * HT - 1)
                for c2 in range(2):
                    for k in range(4):
                        if k % 2 == 0:
                            hold(dve, (y_formed, 2 * (p * 2 + c2) + k // 2 + 1))
                        t = cc * 8 + c2 * 4 + k
                        row = G.x_tok[:, bass.ds(t, 1), :]
                        add = nc.vector.scalar_tensor_tensor(out=row, in0=yP[c2][k // 2][:, (k % 2) * D:(k % 2 + 1) * D],
                                                       scalar=M.w[:, bass.ds(t, 1), bass.ds(ep * 2 + u, 1)],
                                                       in1=row, op0=ALU.mult, op1=ALU.add)
                        if k % 2:
                            add.then_inc(y_taken, 1)
            pairs(dve, pair)


XH = 64
XI = H * XH
XC = XI // P
XSLOTS = 2
X_MASK, X_SHIFT = XH, XH + 1
XROWS = XH + 2


def project_wide(nc, G, A, V):
    kt = tiles_of(NCTX)
    with ExitStack() as stack:
        s = Scope(nc, stack, "l1xp")
        wq, wk = s.sb("wq", [P, KC, XI]), s.sb("wk", [P, KC, XI])
        full = s.sb("full", [P, 2, S])
        rest = s.sb("rest", [P, S])
        parts = s.sb("parts", [P, 2, 2, S], BF16)
        banks = [s.ps(f"bank{b}", [P, CH]) for b in range(4)]
        vbanks = [s.ps(f"vbank{b}", [P, CH]) for b in range(4)]
        loaded, v_loaded, formed, taken, split, rest_done, v_formed, v_taken, v_clear = (s.sem(x) for x in (
            "loaded", "v_loaded", "formed", "taken", "split", "rest_done", "v_formed", "v_taken", "v_clear"))
        stored = [s.sem(f"stored{b}") for b in range(2)]
        units = [(w, oc) for w in range(2) for oc in range(XC)]
        chunks = [tiles_of(S, CH) if w == 0 else tiles_of(NCTX, CH) for w, _ in units]
        ends = [sum(len(x) for x in chunks[:u + 1]) for u in range(len(units))]
        order = [(u, c) for u in range(len(units)) for c in range(len(chunks[u]))]
        v_jobs = [(t, half) for t in range(len(kt)) for half in range(XI // CH)]
        w_kv = A["L1_xattn_w_kv"].rearrange("(c p) n -> p c n", p=P)
        block = stack.enter_context(nc.Block())

        @block.sync
        def _(sp):
            sp.dma_start(wq[:], A["L1_xattn_w_q"].rearrange("(c p) n -> p c n", p=P)).then_inc(loaded, 16)
            sp.dma_start(wk[:], w_kv[:, :, 0:XI]).then_inc(loaded, 16)
            for u, (w, oc) in enumerate(units):
                if u == XC:
                    sp.wait_ge(formed, ends[XC - 1])
                    sp.dma_start(wq[:], w_kv[:, :, XI:2 * XI]).then_inc(v_loaded, 16)
                n = S if w == 0 else NCTX
                sp.wait_ge(split, 2 * (u + 1))
                dst = G.wide_q if w == 0 else G.wide_k
                dst_parts = G.wide_q_parts if w == 0 else G.wide_k_parts
                sp.dma_start(dst[oc * P:(oc + 1) * P, 0:n], full[:, u % 2, 0:n]).then_inc(stored[u % 2], 16)
                for j in range(2):
                    sp.dma_start(dst_parts[j, oc * P:(oc + 1) * P, 0:n], parts[:, u % 2, j, 0:n]).then_inc(stored[u % 2], 16)
            for u in range(2):
                sp.wait_ge(stored[u], 3 * 16 * len(units) // 2)

        @block.gpsimd
        def _(pool):
            nc.gpsimd.memset(V[:, len(kt) - 1], 0.0).then_inc(v_clear, 1)

        @block.tensor
        def _(pe):
            pe.wait_ge(loaded, 32)
            for n, (u, c) in enumerate(order):
                w, oc = units[u]
                a, m = chunks[u][c]
                if n >= 4:
                    pe.wait_ge(taken, n - 3)
                for ic in range(KC):
                    mm = nc.tensor.matmul(banks[n % 4][:, 0:m], (wq, wk)[w][:, ic, oc * P:(oc + 1) * P],
                                          (G.xn, G.ctxT)[w][:, ic, a:a + m], start=(ic == 0), stop=(ic == KC - 1))
                mm.then_inc(formed, 1)
            pe.wait_ge(v_loaded, 16)
            for n, (t, half) in enumerate(v_jobs):
                a, m = kt[t]
                if n >= 4:
                    pe.wait_ge(v_taken, n - 3)
                for ic in range(KC):
                    mm = nc.tensor.matmul(vbanks[n % 4][0:m, :], G.ctxT[:, ic, a:a + m],
                                          wq[:, ic, half * CH:(half + 1) * CH], start=(ic == 0), stop=(ic == KC - 1))
                mm.then_inc(v_formed, 1)

        @block.scalar
        def _(act):
            for u, (w, oc) in enumerate(units):
                n = S if w == 0 else NCTX
                if u >= 2:
                    act.wait_ge(stored[u % 2], 3 * 16 * (u // 2))
                    act.wait_ge(rest_done, u - 1)
                for c, (a, m) in enumerate(chunks[u]):
                    at = (ends[u - 1] if u else 0) + c
                    act.wait_ge(formed, at + 1)
                    nc.scalar.activation(full[:, u % 2, a:a + m], banks[at % 4][:, 0:m], ACT.Copy,
                                         scale=0.125 if w == 0 else 1.0).then_inc(taken, 1)
                act.wait_ge(taken, ends[u])
                nc.scalar.activation(parts[:, u % 2, 0, 0:n], full[:, u % 2, 0:n], ACT.Copy).then_inc(split, 1)
                act.wait_ge(rest_done, u + 1)
                nc.scalar.activation(parts[:, u % 2, 1, 0:n], rest[:, 0:n], ACT.Copy).then_inc(split, 1)

        @block.vector
        def _(dve):
            for u, (w, oc) in enumerate(units):
                n = S if w == 0 else NCTX
                dve.wait_ge(split, 2 * u + 1)
                nc.vector.tensor_tensor(rest[:, 0:n], full[:, u % 2, 0:n], parts[:, u % 2, 0, 0:n],
                                        ALU.subtract).then_inc(rest_done, 1)
            dve.wait_ge(v_clear, 1)
            for n, (t, half) in enumerate(v_jobs):
                dve.wait_ge(v_formed, n + 1)
                m = kt[t][1]
                nc.vector.tensor_copy(V[0:m, t, half * CH:(half + 1) * CH], vbanks[n % 4][0:m, :]).then_inc(v_taken, 1)


def attend_wide(nc, G, V):
    kt = tiles_of(NCTX)
    NKT = len(kt)
    key_chunks = tiles_of(NCTX, CH)
    NCH = len(key_chunks)
    LAG = QT - NKT
    with ExitStack() as stack:
        s = Scope(nc, stack, "l1xc")
        k32, q32 = s.sb("k32", [XROWS, XSLOTS * NKT * P]), s.sb("q32", [XROWS, XSLOTS * S])
        qa = s.sb("q_hm", [P, XSLOTS * S], BF16)
        kh = s.sb("k_hh", [P, XSLOTS * S], BF16)
        km = s.sb("k_m0", [P, XSLOTS * S], BF16)
        part_max = s.sb("part_max", [P, 2, NCH])
        stat, statT = s.sb("stat", [P, 32]), s.sb("statT", [32, P])
        prob = s.sb("prob", [P, 2, QC, CH])
        Kh, Vh = s.sb("k_tile", [XROWS, 2, P]), s.sb("v_tile", [P, 2, XH])
        O_out = s.sb("o_out", [P, 3, CH])
        sA = [s.ps(f"by_query{b}", [P, CH]) for b in range(2)]
        yP = [s.ps(f"less_max{b}", [P, CH]) for b in range(2)]
        O = [s.ps(f"o_sum{b}", [P, CH]) for b in range(2)]
        Den = s.ps("den", [P, CH])
        turned = s.ps("turned", [P, CH])
        (ready, a_loaded, b_loaded, a_formed, a_taken, y_formed, y_taken, k_staged, v_staged, pv_done,
         o_formed, o_taken, o_stored, maxed, stats_set, st_turned, st_out, st_loaded, passed) = (s.sem(x) for x in (
             "ready", "a_loaded", "b_loaded", "a_formed", "a_taken", "y_formed", "y_taken", "k_staged",
             "v_staged", "pv_done", "o_formed", "o_taken", "o_stored", "maxed", "stats_set", "st_turned",
             "st_out", "st_loaded", "passed"))
        AHEAD = 2
        F_AHEAD = 2 * QC
        READY = 11
        A_LOADS, B_LOADS = 5 * 16, 2 * 16
        block = stack.enter_context(nc.Block())

        def hold(eng, *events):
            for sem, n in events:
                eng.wait_ge(sem, n)
            if eng in (nc.vector, nc.gpsimd, nc.sync):
                eng.sem_inc(passed, 1)

        def heads(eng, step, a_end=None, b_start=None, b_end=None):
            def pair(ha, hb, g, last=False):
                for u in range(2):
                    step(ha, hb if not (last and u) else None, g, u)

            def head(ha, hb):
                if b_start and hb is not None:
                    b_start(hb)
                if hb is None:
                    with eng.Fori(0, QT // 2) as g:
                        pair(ha, None, g)
                else:
                    with eng.Fori(0, NKT // 2) as g:
                        pair(ha, hb, g)
                    pair(ha, hb, NKT // 2, last=True)
                    if ha is not None:
                        for g in range(NKT // 2 + 1, QT // 2):
                            pair(ha, None, g)
                if b_end and hb is not None:
                    b_end(hb)
                if a_end and ha is not None:
                    a_end(ha)

            head(0, None)
            with eng.Fori(0, H - 1) as h:
                head(h + 1, h)
            head(None, H - 1)

        @block.sync
        def _(sp):
            def load_a(h):
                at = bass.ds((h & (XSLOTS - 1)) * S, S)
                atk = bass.ds((h & (XSLOTS - 1)) * S, NCTX)
                rows = bass.ds(h * XH, XH)
                sp.dma_start(qa[0:XH, at], G.wide_q_parts[0, rows, :]).then_inc(a_loaded, 16)
                sp.dma_start(qa[XH:P, at], G.wide_q_parts[1, rows, :]).then_inc(a_loaded, 16)
                sp.dma_start(kh[0:XH, atk], G.wide_k_parts[0, rows, 0:NCTX]).then_inc(a_loaded, 16)
                sp.dma_start(kh[XH:P, atk], G.wide_k_parts[0, rows, 0:NCTX]).then_inc(a_loaded, 16)
                sp.dma_start(km[0:XH, atk], G.wide_k_parts[1, rows, 0:NCTX]).then_inc(a_loaded, 16)
                hold(sp, (a_loaded, A_LOADS * (h + 1)))

            def load_b(h):
                slot = h & (XSLOTS - 1)
                rows = bass.ds(h * XH, XH)
                sp.dma_start(k32[0:XH, bass.ds(slot * NKT * P, NCTX)], G.wide_k[rows, 0:NCTX]).then_inc(b_loaded, 16)
                sp.dma_start(q32[0:XH, bass.ds(slot * S, S)], G.wide_q[rows, :]).then_inc(b_loaded, 16)
                hold(sp, (b_loaded, B_LOADS * (h + 1)))

            def stats(h):
                hold(sp, (st_out, h + 1))
                slot = h & (XSLOTS - 1)
                sp.dma_start(q32[X_SHIFT:X_SHIFT + 1, bass.ds(slot * S, S)], statT[0:QT]).then_inc(st_loaded, 16)
                hold(sp, (st_loaded, 16 * (h + 1) + 16))

            sp.sem_inc(st_loaded, 16)
            sp.wait_ge(ready, READY)
            load_a(0)
            load_b(0)
            load_a(1)
            load_b(1)
            stats(0)
            with sp.Fori(1, H - 1) as h:
                hold(sp, (stats_set, h))
                load_a(h + 1)
                stats(h)
                hold(sp, (o_formed, h))
                load_b(h + 1)
            stats(H - 1)

        @block.gpsimd
        def _(pool):
            last = NCTX - (NKT - 1) * P
            steps = [(k32[:], 0.0), (k32[X_MASK:XROWS], 1.0), (q32[X_MASK:XROWS], 1.0), (km[:], 0.0),
                     (stat[:], 0.0), (O_out[:], 0.0), (part_max[:], 0.0)]
            for slot in range(XSLOTS):
                at = slot * NKT * P
                steps += [(k32[X_MASK:X_MASK + 1, at:at + NCTX], 0.0),
                          (k32[X_MASK:X_MASK + 1, at + NCTX:at + NKT * P], NEG)]
            for j, (what, value) in enumerate(steps):
                if j:
                    pool.wait_ge(ready, j)
                nc.gpsimd.memset(what, value).then_inc(ready, 1)
            pool.wait_ge(ready, len(steps))
            assert len(steps) == READY

            def step(ha, hb, g, u):
                if hb is not None:
                    i = 2 * g + u
                    m = hb * NKT + i
                    slot = hb & (XSLOTS - 1)
                    if u == 0:
                        hold(pool, (b_loaded, B_LOADS * (hb + 1)))
                    hold(pool, (y_formed, QC * (m - 2 + 1) + F_AHEAD))
                    nc.gpsimd.tensor_copy(Kh[:, u], k32[:, bass.ds(slot * NKT * P + i * P, P)]).then_inc(k_staged, 1)
                    hold(pool, (k_staged, m + 1), (pv_done, m - 2 + 1 + AHEAD))
                    nc.gpsimd.tensor_copy(Vh[:, u], V[:, bass.ds(i, 1), bass.ds(hb * XH, XH)]).then_inc(v_staged, 1)
                    hold(pool, (v_staged, m + 1))

            def b_start(h):
                hold(pool, (pv_done, h * NKT + AHEAD))

            heads(pool, step, b_start=b_start)

        @block.tensor
        def _(pe):
            pe.sem_inc(pv_done, AHEAD)
            pe.sem_inc(y_formed, F_AHEAD)
            pe.wait_ge(ready, READY)

            def by_query(h, i, c):
                n = h * QT + i
                slot = h & (XSLOTS - 1)
                a, w = key_chunks[c]
                hold(pe, (a_taken, NCH * n + c - 2 + 1 + AHEAD))
                bank = sA[c % 2][:, 0:w]
                lhs = qa[:, bass.ds(slot * S + i * P, P)]
                nc.tensor.matmul(bank, lhs, kh[:, bass.ds(slot * S + a, w)], start=True, stop=False)
                nc.tensor.matmul(bank, lhs, km[:, bass.ds(slot * S + a, w)], start=False, stop=True).then_inc(a_formed, 1)

            def by_key(h, g, u, c):
                m = h * NKT + 2 * g + u
                slot = h & (XSLOTS - 1)
                hold(pe, (y_taken, QC * m + c - 2 + 1 + AHEAD))
                nc.tensor.matmul(yP[c % 2][:], Kh[:, u], q32[:, bass.ds(slot * S + c * CH, CH)],
                                 start=True, stop=True).then_inc(y_formed, 1)

            def sums(m, u, c):
                if c == 0:
                    hold(pe, (v_staged, m + 1), (y_taken, QC * (m + 1) + AHEAD))
                half = (c % 2) * XH
                nc.tensor.matmul(O[c // 2][half:half + XH, :], Vh[:, u], prob[:, u, c],
                                 start=False, stop=False, skip_group_check=True)
                if c == QC - 1:
                    for c in range(QC):
                        mm = nc.tensor.matmul(Den[32 * c:32 * (c + 1), :], G.ones[:, 0:32], prob[:, u, c],
                                              start=False, stop=False, skip_group_check=True)
                    mm.then_inc(pv_done, 1)

            def step(ha, hb, g, u):
                m = hb * NKT + 2 * g + u
                hold(pe, (k_staged, m + 1))
                first = isinstance(g, int) and g == 0 and u == 0
                for c in range(QC):
                    by_key(hb, g, u, c)
                    if ha is not None and c < NCH:
                        by_query(ha, 2 * g + (u + LAG), c)
                    if not first and c % 2:
                        sums(m - 1, 1 - u, c - 1)
                        sums(m - 1, 1 - u, c)

            def head(ha, hb):
                if ha is not None:
                    hold(pe, (a_loaded, A_LOADS * (ha + 1)))
                    for i in range(LAG):
                        for c in range(NCH):
                            by_query(ha, i, c)
                b_start(hb)
                hold(pe, (st_loaded, 16 * (hb + 1) + 16))
                for u in range(2):
                    step(ha, hb, 0, u)
                with pe.Fori(1, NKT // 2) as g:
                    for u in range(2):
                        step(ha, hb, g, u)
                step(ha, hb, NKT // 2, 0)
                b_end(hb)
                if ha is not None:
                    a_end(ha)

            def b_start(h):
                hold(pe, (o_taken, h + 1))
                for bank in (O[0], O[1], Den):
                    nc.tensor.matmul(bank[:], G.zerob[:, 0:P], G.zerob[:], start=True, stop=False, skip_group_check=True)

            def b_end(h):
                for c in range(QC):
                    sums((h + 1) * NKT - 1, (NKT - 1) % 2, c)
                hold(pe, (pv_done, (h + 1) * NKT + AHEAD))
                pe.sem_inc(o_formed, 1)

            def a_end(h):
                hold(pe, (stats_set, h + 1))
                nc.tensor.transpose(turned[0:32, 0:P], stat[:], G.ident[:]).then_inc(st_turned, 1)

            hold(pe, (a_loaded, A_LOADS))
            with pe.Fori(0, QT) as i:
                for c in range(NCH):
                    by_query(0, i, c)
            a_end(0)
            with pe.Fori(0, H - 1) as h:
                head(h + 1, h)
            head(None, H - 1)

        @block.scalar
        def _(act):
            act.sem_inc(y_taken, AHEAD)
            act.sem_inc(o_taken, 1)
            act.sem_inc(o_stored, 16)
            act.wait_ge(ready, READY)

            def step(ha, hb, g, u):
                if hb is not None:
                    m = hb * NKT + 2 * g + u
                    hold(act, (pv_done, m - 2 + 1 + AHEAD))
                    for c in range(QC):
                        hold(act, (y_formed, QC * m + c + 1 + F_AHEAD))
                        nc.scalar.activation(prob[:, u, c], yP[c % 2][:], ACT.Exp).then_inc(y_taken, 1)

            def b_start(h):
                hold(act, (pv_done, h * NKT + AHEAD))

            def b_end(h):
                hold(act, (o_formed, h + 1), (o_stored, 128 * h + 16))
                for b in range(2):
                    nc.scalar.activation(O_out[:, b], O[b][:], ACT.Copy)
                nc.scalar.activation(O_out[:, 2], Den[:], ACT.Copy).then_inc(o_taken, 1)
                hold(act, (o_taken, h + 2))
                for c in range(QC):
                    half = (c % 2) * XH
                    act.dma_start(G.wide_sums[bass.ds(h, 1), 0:XH, c * CH:(c + 1) * CH],
                                  O_out[half:half + XH, c // 2]).then_inc(o_stored, 16)
                    act.dma_start(G.wide_sums[bass.ds(h, 1), XH:XH + 32, c * CH:(c + 1) * CH],
                                  O_out[32 * c:32 * (c + 1), 2]).then_inc(o_stored, 16)

            heads(act, step, b_start=b_start, b_end=b_end)
            act.wait_ge(o_stored, 128 * H + 16)

        @block.vector
        def _(dve):
            dve.sem_inc(a_taken, AHEAD)
            dve.sem_inc(maxed, 1)
            dve.wait_ge(ready, READY)

            def step(ha, hb, g, u):
                if ha is not None:
                    i = 2 * g + u
                    n = ha * QT + i
                    for c, (a, w) in enumerate(key_chunks):
                        hold(dve, (a_formed, NCH * n + c + 1))
                        nc.vector.tensor_reduce(part_max[:, u, c:c + 1], sA[c % 2][:, 0:w], AX.X, ALU.max).then_inc(a_taken, 1)
                    hold(dve, (a_taken, NCH * (n + 1) + AHEAD))
                    nc.vector.tensor_reduce(stat[:, bass.ds(i, 1)], part_max[:, u], AX.X, ALU.max,
                                            negate=True).then_inc(maxed, 1)
                    hold(dve, (maxed, n + 2))

            def a_end(h):
                dve.sem_inc(stats_set, 1)
                hold(dve, (st_turned, h + 1), (st_loaded, 16 * h + 16))
                nc.vector.tensor_copy(statT[:], turned[0:32, 0:P]).then_inc(st_out, 1)
                hold(dve, (st_out, h + 1))

            heads(dve, step, a_end=a_end)


def finish_wide(nc, G, A):
    with ExitStack() as stack:
        s = Scope(nc, stack, "l1xf")
        w = s.sb("w", [P, XC, D])
        bias, gate = s.sb("bias", [1, D]), s.sb("gate", [1, 1])
        tgate = s.sb("tgate", [P, 1])
        num, den = s.sb("num", [P, XC, S]), s.sb("den", [P, 2, S])
        banks = [s.ps(f"bank{b}", [P, CH]) for b in range(4)]
        gate_bank = s.ps("gate_bank", [P, CH])
        w_loaded, inv, normed, gated, gate_ready, formed, added = (s.sem(x) for x in (
            "w_loaded", "inv", "normed", "gated", "gate_ready", "formed", "added"))
        loaded = [s.sem(f"loaded{b}") for b in range(2)]
        block = stack.enter_context(nc.Block())

        @block.sync
        def _(sp):
            sp.dma_start(w[:], A["L1_xattn_w_out"].rearrange("(c p) d -> p c d", p=P)).then_inc(w_loaded, 16)
            sp.dma_start(bias[:], A["L1_xattn_b_out"].rearrange("(o n) -> o n", o=1)).then_inc(w_loaded, 16)
            sp.dma_start(gate[:], A["L1_xattn_gate"].rearrange("(o n) -> o n", o=1)).then_inc(w_loaded, 16)
            for c in range(XC):
                if c >= 2:
                    sp.wait_ge(normed, c - 1)
                for j in range(2):
                    h = 2 * c + j
                    sp.dma_start(num[j * XH:(j + 1) * XH, c], G.wide_sums[h, 0:XH]).then_inc(loaded[c % 2], 16)
                    for r in range(2):
                        sp.dma_start(den[j * XH + 32 * r:j * XH + 32 * (r + 1), c % 2],
                                     G.wide_sums[h, XH:XH + 32]).then_inc(loaded[c % 2], 16)

        @block.tensor
        def _(pe):
            pe.wait_ge(w_loaded, 48)
            nc.tensor.matmul(gate_bank[:, 0:1], G.ones[0:1, 0:P], gate[:], start=True, stop=True).then_inc(gated, 1)
            pe.wait_ge(normed, XC)
            for t in range(QT):
                if t >= 4:
                    pe.wait_ge(added, t - 3)
                bank = banks[t % 4][:, 0:D]
                for c in range(XC):
                    nc.tensor.matmul(bank, num[:, c, t * P:(t + 1) * P], w[:, c], start=(c == 0), stop=False)
                nc.tensor.matmul(bank, G.ones[0:1, 0:P], bias[:], start=False, stop=True).then_inc(formed, 1)

        @block.scalar
        def _(act):
            act.wait_ge(gated, 1)
            nc.scalar.activation(tgate[:], gate_bank[:, 0:1], ACT.Tanh).then_inc(gate_ready, 1)

        @block.vector
        def _(dve):
            for c in range(XC):
                dve.wait_ge(loaded[c % 2], 6 * 16 * (c // 2 + 1))
                nc.vector.reciprocal(den[:, c % 2], den[:, c % 2]).then_inc(inv, 1)
                dve.wait_ge(inv, c + 1)
                nc.vector.tensor_tensor(num[:, c], num[:, c], den[:, c % 2], ALU.mult).then_inc(normed, 1)
            dve.wait_ge(gate_ready, 1)
            for t in range(QT):
                dve.wait_ge(formed, t + 1)
                nc.vector.scalar_tensor_tensor(out=G.x_tok[:, t], in0=banks[t % 4][:, 0:D], scalar=tgate[:],
                                               in1=G.x_tok[:, t], op0=ALU.mult, op1=ALU.add).then_inc(added, 1)


FP8_MAX = 448.0


def fp8_linear(nc, G, A):
    with ExitStack() as stack:
        s = Scope(nc, stack, "fp8")
        code = s.sb("code", [P, KC * D], U8)
        bits, field = s.sb("bits", [P, KC * D], I32), s.sb("field", [P, 3, KC * D], I32)
        fieldf = s.sb("fieldf", [P, 3, KC * D])
        power = s.sb("power", [P, KC * D], I32)
        weight = s.sb("weight", [P, KC, D])
        wT = s.sb("wT", [P, KC, D], BF16)
        row = s.sb("row", [1, D + 1])
        spread = s.sb("spread", [P, D + 1])
        amax, scale, inv_scale, out_scale = (s.sb(x, [P, QT]) for x in ("amax", "scale", "inv_scale", "out_scale"))
        y, magic = s.sb("y", [P, QT * D]), s.sb("magic", [P, QT * D])
        qT = s.sb("qT", [P, KC, S], BF16)
        banks = [s.ps(f"bank{b}", [P, CH]) for b in range(2)]
        out_banks = [s.ps(f"out{b}", [P, CH]) for b in range(4)]
        row_bank = s.ps("row_bank", [P, CH])
        (loaded, step, w_set, turned, taken, spread_formed, spread_set, quant, formed, added, based) = (
            s.sem(x) for x in ("loaded", "step", "w_set", "turned", "taken", "spread_formed", "spread_set",
                               "quant", "formed", "added", "based"))
        jobs = [(c, g) for g in range(0, QT, 4) for c in range(KC)]
        block = stack.enter_context(nc.Block())

        @block.sync
        def _(sp):
            sp.dma_start(code[:].rearrange("p (c n) -> p c n", c=KC),
                         A["L1_ffn_weight"].bitcast(U8).rearrange("(c p) n -> p c n", p=P)).then_inc(loaded, 16)
            sp.dma_start(row[:, 0:D], A["L1_ffn_bias"].rearrange("(o n) -> o n", o=1)).then_inc(loaded, 16)
            sp.dma_start(row[:, D:D + 1], A["L1_ffn_weight_scale"].rearrange("(o n) -> o n", o=1)).then_inc(loaded, 16)

        @block.tensor
        def _(pe):
            pe.wait_ge(loaded, 48)
            nc.tensor.matmul(row_bank[:, 0:D + 1], G.ones[0:1, 0:P], row[:], start=True, stop=True).then_inc(spread_formed, 1)
            pe.wait_ge(w_set, 1)
            for ic in range(KC):
                for oc in range(KC):
                    mm = nc.tensor.transpose(banks[0][:, ic * D + oc * P:ic * D + (oc + 1) * P],
                                             weight[:, oc, ic * P:(ic + 1) * P], G.ident[:])
            mm.then_inc(turned, 1)
            for j, (c, g) in enumerate(jobs):
                pe.wait_ge(quant, 1)
                if j:
                    pe.wait_ge(taken, j)
                for k in range(4):
                    at = (g + k) * D + c * P
                    mm = nc.tensor.transpose(banks[(j + 1) % 2][:, k * P:(k + 1) * P], y[:, at:at + P], G.ident[:])
                mm.then_inc(turned, 1)
            pe.wait_ge(taken, len(jobs) + 1)
            for t in range(QT):
                if t >= 4:
                    pe.wait_ge(added, t - 3)
                for c in range(KC):
                    mm = nc.tensor.matmul(out_banks[t % 4][:, 0:D], qT[:, c, t * P:(t + 1) * P], wT[:, c],
                                          start=(c == 0), stop=(c == KC - 1))
                mm.then_inc(formed, 1)

        @block.scalar
        def _(act):
            act.wait_ge(spread_formed, 1)
            nc.scalar.activation(spread[:], row_bank[:, 0:D + 1], ACT.Copy).then_inc(spread_set, 1)
            act.wait_ge(turned, 1)
            nc.scalar.activation(wT[:], banks[0][:].rearrange("p (c d) -> p c d", c=KC), ACT.Copy).then_inc(taken, 1)
            for j, (c, g) in enumerate(jobs):
                act.wait_ge(turned, j + 2)
                nc.scalar.activation(qT[:, c, g * P:(g + 4) * P], banks[(j + 1) % 2][:], ACT.Copy).then_inc(taken, 1)

        @block.vector
        def _(dve):
            count = [0]

            def then(ins):
                count[0] += 1
                ins.then_inc(step, 1)
                dve.wait_ge(step, count[0])

            dve.wait_ge(loaded, 48)
            then(nc.vector.tensor_copy(bits[:], code[:]))
            then(nc.vector.tensor_scalar(field[:, 0], bits[:], 7, None, ALU.logical_shift_right))
            then(nc.vector.tensor_scalar(field[:, 1], bits[:], 3, 15, ALU.logical_shift_right, ALU.bitwise_and))
            then(nc.vector.tensor_scalar(field[:, 2], bits[:], 7, None, ALU.bitwise_and))
            then(nc.vector.tensor_copy(fieldf[:], field[:]))
            sign, expo, mant = (fieldf[:, j] for j in range(3))
            flat = weight[:].rearrange("p c d -> p (c d)")
            then(nc.vector.tensor_scalar(flat, expo, 0.0, 8.0, ALU.is_gt, ALU.mult))
            then(nc.vector.tensor_tensor(flat, flat, mant, ALU.add))
            then(nc.vector.tensor_scalar(expo, expo, 1.0, 117.0, ALU.max, ALU.add))
            then(nc.vector.tensor_copy(power[:], expo))
            then(nc.vector.tensor_scalar(power[:], power[:], 23, None, ALU.logical_shift_left))
            then(nc.vector.tensor_tensor(flat, flat, power[:].bitcast(F32), ALU.mult))
            then(nc.vector.tensor_scalar(sign, sign, -2.0, 1.0, ALU.mult, ALU.add))
            nc.vector.tensor_tensor(flat, flat, sign, ALU.mult).then_inc(w_set, 1)
            for t in range(QT):
                mx = nc.vector.tensor_reduce(amax[:, t:t + 1], G.x_tok[:, t], AX.X, ALU.max, apply_absolute_value=True)
            then(mx)
            then(nc.vector.tensor_scalar(scale[:], amax[:], 1e-12, 1.0 / FP8_MAX, ALU.max, ALU.mult))
            then(nc.vector.reciprocal(inv_scale[:], scale[:]))
            dve.wait_ge(spread_set, 1)
            for t in range(QT):
                ins = nc.vector.tensor_scalar(y[:, t * D:(t + 1) * D], G.x_tok[:, t], inv_scale[:, t:t + 1], None, ALU.mult)
            then(ins)
            then(nc.vector.tensor_scalar(out_scale[:], scale[:], spread[:, D:D + 1], None, ALU.mult))
            for t in range(QT):
                ins = nc.vector.tensor_tensor(G.x_tok[:, t], G.x_tok[:, t], spread[:, 0:D], ALU.add)
            then(ins)
            then(nc.vector.tensor_scalar(magic[:].bitcast(I32), y[:].bitcast(I32), 0x7F800000, None, ALU.bitwise_and))
            then(nc.vector.tensor_scalar(magic[:], magic[:], 2.0 ** -6, 1.5 * 2.0 ** 20, ALU.max, ALU.mult))
            then(nc.vector.tensor_tensor(y[:], y[:], magic[:], ALU.add))
            nc.vector.tensor_tensor(y[:], y[:], magic[:], ALU.subtract).then_inc(quant, 1)
            for t in range(QT):
                dve.wait_ge(formed, t + 1)
                nc.vector.scalar_tensor_tensor(out=G.x_tok[:, t], in0=out_banks[t % 4][:, 0:D],
                                               scalar=out_scale[:, t:t + 1], in1=G.x_tok[:, t],
                                               op0=ALU.mult, op1=ALU.add).then_inc(added, 1)


class Resident:
    pass


def decoder(nc, A, out):
    G = Resident()
    with ExitStack() as stack:
        s = Scope(nc, stack, "keep")
        G.x_tok = s.sb("x_tok", [P, QT, D])
        G.xT = s.sb("xT", [P, KC, S])
        G.ctxT = s.sb("ctxT", [P, KC, NCTX])
        G.ident = s.sb("ident", [P, P])
        G.identb = s.sb("identb", [P, P], BF16)
        G.band = s.sb("band", [P, 2, 3 * P + CH], BF16)
        G.ones = s.sb("ones", [P, CH])
        G.zerob = s.sb("zerob", [P, CH], BF16)
        G.mask_row = s.sb("mask_row", [1, S], BF16)
        G.q_parts = nc.dram_tensor("q_parts", (3, D, S), BF16, kind="Internal").ap()
        G.k_parts = nc.dram_tensor("k_parts", (3, D, S), BF16, kind="Internal").ap()
        G.wide_q = nc.dram_tensor("wide_q", (XI, S), F32, kind="Internal").ap()
        G.wide_k = nc.dram_tensor("wide_k", (XI, S), F32, kind="Internal").ap()
        G.wide_q_parts = nc.dram_tensor("wide_q_parts", (2, XI, S), BF16, kind="Internal").ap()
        G.wide_k_parts = nc.dram_tensor("wide_k_parts", (2, XI, S), BF16, kind="Internal").ap()
        G.wide_sums = nc.dram_tensor("wide_sums", (H, XH + 32, S), F32, kind="Internal").ap()
        G.sums = nc.dram_tensor("sums", (H, 2 * DH, S), F32, kind="Internal").ap()

        load_inputs(nc, G, A)
        with ExitStack() as layer:
            V = Scope(nc, layer, "l0a").sb("v", [P, QT, H, 2 * DH])
            w, b = A["L0_attn_w_qkv"], A["L0_attn_b_qkv"].rearrange("(o n) -> o n", o=1)
            project(nc, G, A, "l0ap", G.xT, S, w[0:D], w[D:2 * D], w[2 * D:3 * D],
                    b[:, 0:D], b[:, D:2 * D], b[:, 2 * D:3 * D], True, None, V)
            attend_causal(nc, G, "l0ac", V)
        row = lambda name: A[name].rearrange("(o n) -> o n", o=1)
        finish(nc, G, A, "l0af", A["L0_attn_w_out"], row("L0_attn_b_out"), 1e-8)
        with ExitStack() as layer:
            V = Scope(nc, layer, "l0x").sb("v", [P, len(tiles_of(NCTX)), H, 2 * DH])
            project(nc, G, A, "l0xp", G.ctxT, NCTX, A["L0_xattn_wq_w"], A["L0_xattn_wk_w"],
                    A["L0_xattn_wv_w"], row("L0_xattn_wq_b"), row("L0_xattn_wk_b"),
                    row("L0_xattn_wv_b"), False, A["mask_BxS2_bf1"], V)
            attend_top(nc, G, "l0xc", NCTX, V)
        finish(nc, G, A, "l0xf", A["L0_xattn_wo_w"], row("L0_xattn_wo_b"), None)
        with ExitStack() as layer:
            M = Resident()
            keep = Scope(nc, layer, "moek")
            M.tT = keep.sb("tT", [P, KC, S])
            M.w = keep.sb("w", [P, QT, EXPERTS])
            M.b_glu = keep.sb("b_glu", [P, 4 * EXPERTS])
            M.b_lin = keep.sb("b_lin", [P, 4 * EXPERTS])
            moe_gate(nc, G, A, M)
            moe_experts(nc, G, A, M)
        layer_norm(nc, G, A, "l0n")
        with ExitStack() as layer:
            V = Scope(nc, layer, "l1a").sb("v", [P, QT, H, 2 * DH])
            project(nc, G, A, "l1ap", G.xT, S, A["L1_attn_Wq"], A["L1_attn_Wk"], A["L1_attn_Wv"],
                    row("L1_attn_bq"), row("L1_attn_bk"), row("L1_attn_bv"), False, None, V)
            attend_top(nc, G, "l1ac", S, V)
        finish(nc, G, A, "l1af", A["L1_attn_Wo"], row("L1_attn_bo"), None)
        with ExitStack() as layer:
            V = Scope(nc, layer, "l1x").sb("v", [P, len(tiles_of(NCTX)), XI])
            with ExitStack() as inner:
                G.xn = Scope(nc, inner, "l1xn").sb("xn", [P, KC, S])
                layer_norm(nc, G, A, "l1xl", affine=(A["L1_xattn_ln_gamma"], A["L1_xattn_ln_beta"]))
                project_wide(nc, G, A, V)
            attend_wide(nc, G, V)
        finish_wide(nc, G, A)
        layer_norm(nc, G, A, "l1xm")
        fp8_linear(nc, G, A)
        layer_norm(nc, G, A, "last", out)


_INS = ['x', 'ctx_1024', 'mask_BxS2_bf1', 'L0_attn_w_qkv', 'L0_attn_b_qkv', 'L0_attn_w_out', 'L0_attn_b_out',
        'L0_xattn_wq_w', 'L0_xattn_wq_b', 'L0_xattn_wk_w', 'L0_xattn_wk_b', 'L0_xattn_wv_w', 'L0_xattn_wv_b',
        'L0_xattn_wo_w', 'L0_xattn_wo_b', 'L0_ffn_norm_scale', 'L0_ffn_gate_w', 'L0_ffn_gate_b',
        'L0_ffn_mlp1_w', 'L0_ffn_mlp1_b', 'L0_ffn_mlp2_w', 'L0_ffn_mlp2_b', 'L1_attn_Wq', 'L1_attn_bq',
        'L1_attn_Wk', 'L1_attn_bk', 'L1_attn_Wv', 'L1_attn_bv', 'L1_attn_Wo', 'L1_attn_bo',
        'L1_xattn_ln_gamma', 'L1_xattn_ln_beta', 'L1_xattn_w_q', 'L1_xattn_w_kv', 'L1_xattn_w_out',
        'L1_xattn_b_out', 'L1_xattn_gate', 'L1_ffn_weight', 'L1_ffn_weight_scale', 'L1_ffn_bias']
_OUTS = [((1, S, D), 'float32')]


def shape_constants():
    import numpy as np
    p = np.arange(P)[:, None]
    z = np.arange(3 * P + CH)[None, :] - 3 * P
    band = np.stack([np.where(z > p, NEG, 0.0), np.where(z < p, NEG, 0.0)], 1).astype(np.float32)
    freq = (np.float32(10000.0) ** (-np.arange(0, DH, 2, dtype=np.float32) / np.float32(DH))).astype(np.float32)
    angle = np.arange(S, dtype=np.float32)[None, :] * np.repeat(freq, 2)[:, None]
    rope = np.stack([np.cos(angle), np.sin(angle)]).astype(np.float32)
    experts = np.broadcast_to(np.arange(8, dtype=np.float32), (P, 8))
    return {"const_ident": np.eye(P, dtype=np.float32), "const_band": band, "const_rope": rope,
            "const_experts": np.ascontiguousarray(experts)}


def kernel(**inputs):
    import numpy as _np
    import concourse.bacc as _bacc
    from concourse import mybir as _mybir
    from concourse.bass_utils import run_bass_kernel_spmd as _run

    nc = _bacc.Bacc("TRN2", target_bir_lowering=False, num_devices=1)
    arrays, args = {}, {}
    for name, a in [(n, inputs[n]) for n in _INS] + list(shape_constants().items()):
        a = _np.ascontiguousarray(a)
        a = a.reshape(a.shape or (1,))
        arrays[f"in_{name}_dram"] = a
        args[name] = nc.dram_tensor(f"in_{name}_dram", a.shape, _mybir.dt.from_np(a.dtype), kind="ExternalInput").ap()
    (shape, dtype), = _OUTS
    out = nc.dram_tensor("out_0_dram", shape, _mybir.dt.from_np(_np.dtype(dtype)), kind="ExternalOutput").ap()
    decoder(nc, args, out)
    r = _run(nc, [arrays], core_ids=[0])
    return r.results[0]["out_0_dram"]
```
